# Optimizing a Trainium2 kernel written in Bass

```python
import numpy as np
import jax
import jax.numpy as jnp

def _softmax(x, axis=-1):
    return jax.nn.softmax(x, axis=axis)

def _gelu(x):
    return jax.nn.gelu(x, approximate=True)

def _silu(x):
    return jax.nn.silu(x)

def _sigmoid(x):
    return jax.nn.sigmoid(x)

def _layernorm(x, axis=-1, eps=1e-05):
    m = jnp.mean(x, axis=axis, keepdims=True)
    v = jnp.var(x, axis=axis, keepdims=True)
    return (x - m) / jnp.sqrt(v + eps)

def _scatter_add(tgt, idx, src, axis=0):
    return tgt.at[idx].add(src)

def _segment_sum(src, seg, n):
    return jax.ops.segment_sum(src, seg, n)
kernel_name = 'mk_recurrent_d1_jaxref_r4_e6720c'

def setup_inputs(seed: int=0):
    np.random.seed(seed)
    _w = jnp.asarray

    def _L0_attn_setup():
        import jax, jax.numpy as jnp
        import numpy as np
        H = 16
        D_H = 128
        D_HR = 64
        THETA = 10000.0

        def rope(x, pos, theta=THETA):
            d = x.shape[-1]
            inv_freq = theta ** (-jnp.arange(0, d, 2, dtype=jnp.float32) / d)
            ang = pos.astype(jnp.float32)[:, None] * inv_freq[None, :]
            cos, sin = (jnp.cos(ang), jnp.sin(ang))
            x1, x2 = (x[..., 0::2], x[..., 1::2])
            out = jnp.stack([x1 * cos - x2 * sin, x1 * sin + x2 * cos], axis=-1)
            return out.reshape(x.shape)
        key = jax.random.key(seed)
        ks = jax.random.split(key, 9)
        d_model, d_latent = (512, 128)

        def w(k, shape):
            fan_in = shape[-1]
            return jax.random.normal(k, shape, dtype=jnp.float32) / jnp.sqrt(fan_in)
        return {'x': jax.random.normal(ks[0], (1, 512, d_model), dtype=jnp.float32), 'W_DQ': w(ks[1], (d_latent, d_model)), 'W_UQ': w(ks[2], (H * D_H, d_latent)), 'W_QR': w(ks[3], (H * D_HR, d_latent)), 'W_DKV': w(ks[4], (d_latent, d_model)), 'W_UK': w(ks[5], (H * D_H, d_latent)), 'W_UV': w(ks[6], (H * D_H, d_latent)), 'W_KR': w(ks[7], (D_HR, d_model)), 'W_O': w(ks[8], (d_model, H * D_H))}
    _L0_attn_in = _L0_attn_setup()

    def _L0_ffn_setup():
        import jax, jax.numpy as jnp
        import numpy as np
        NUM_EXPERTS = 8
        RANK = 16
        TOP_K = 2
        SCALING = 32.0 / RANK
        IN_F = 512
        OUT_F = 512
        key = jax.random.key(seed)
        k1, k2, k3, k4, k5 = jax.random.split(key, 5)
        B, T = (4, 512)
        x = jax.random.normal(k1, (B, T, IN_F), dtype=jnp.float32)
        bound_w = 1.0 / np.sqrt(IN_F)
        weight = jax.random.uniform(k2, (OUT_F, IN_F), jnp.float32, -bound_w, bound_w)
        lora_A = jax.random.uniform(k3, (NUM_EXPERTS, RANK, IN_F), jnp.float32, -bound_w, bound_w)
        lora_B = 0.02 * jax.random.normal(k4, (NUM_EXPERTS, OUT_F, RANK), dtype=jnp.float32)
        router_w = jax.random.uniform(k5, (NUM_EXPERTS, IN_F), jnp.float32, -bound_w, bound_w)
        return {'x': x, 'weight': weight, 'lora_A': lora_A, 'lora_B': lora_B, 'router_w': router_w}
    _L0_ffn_in = _L0_ffn_setup()
    _d = {'L0_attn_x': _L0_attn_in['x'], 'L0_attn_W_DQ': _L0_attn_in['W_DQ'], 'L0_attn_W_UQ': _L0_attn_in['W_UQ'], 'L0_attn_W_QR': _L0_attn_in['W_QR'], 'L0_attn_W_DKV': _L0_attn_in['W_DKV'], 'L0_attn_W_UK': _L0_attn_in['W_UK'], 'L0_attn_W_UV': _L0_attn_in['W_UV'], 'L0_attn_W_KR': _L0_attn_in['W_KR'], 'L0_attn_W_O': _L0_attn_in['W_O'], 'L0_ffn_weight': _L0_ffn_in['weight'], 'L0_ffn_lora_A': _L0_ffn_in['lora_A'], 'L0_ffn_lora_B': _L0_ffn_in['lora_B'], 'L0_ffn_router_w': _L0_ffn_in['router_w']}
    _x0 = _d['L0_attn_x']
    _d['L0_attn_x'] = jax.random.normal(jax.random.fold_in(jax.random.key(seed), 1), (1, 2048, 512), dtype=_x0.dtype)
    del _x0
    return _d

def reference(L0_attn_x, L0_attn_W_DQ, L0_attn_W_UQ, L0_attn_W_QR, L0_attn_W_DKV, L0_attn_W_UK, L0_attn_W_UV, L0_attn_W_KR, L0_attn_W_O, L0_ffn_weight, L0_ffn_lora_A, L0_ffn_lora_B, L0_ffn_router_w):

    def _L0_attn_ref(x, W_DQ, W_UQ, W_QR, W_DKV, W_UK, W_UV, W_KR, W_O):
        import jax, jax.numpy as jnp
        import numpy as np
        H = 16
        D_H = 128
        D_HR = 64
        THETA = 10000.0

        def rope(x, pos, theta=THETA):
            d = x.shape[-1]
            inv_freq = theta ** (-jnp.arange(0, d, 2, dtype=jnp.float32) / d)
            ang = pos.astype(jnp.float32)[:, None] * inv_freq[None, :]
            cos, sin = (jnp.cos(ang), jnp.sin(ang))
            x1, x2 = (x[..., 0::2], x[..., 1::2])
            out = jnp.stack([x1 * cos - x2 * sin, x1 * sin + x2 * cos], axis=-1)
            return out.reshape(x.shape)
        B, S, _ = x.shape
        pos = jnp.arange(S)
        c_Q = x @ W_DQ.T
        q_C = (c_Q @ W_UQ.T).reshape(B, S, H, D_H).transpose(0, 2, 1, 3)
        q_R = (c_Q @ W_QR.T).reshape(B, S, H, D_HR).transpose(0, 2, 1, 3)
        q_R = rope(q_R, pos)
        q = jnp.concatenate([q_C, q_R], axis=-1)
        c_KV = x @ W_DKV.T
        k_C = (c_KV @ W_UK.T).reshape(B, S, H, D_H).transpose(0, 2, 1, 3)
        k_R = rope(x @ W_KR.T, pos)[:, None]
        k_R = jnp.broadcast_to(k_R, (B, H, S, D_HR))
        k = jnp.concatenate([k_C, k_R], axis=-1)
        v = (c_KV @ W_UV.T).reshape(B, S, H, D_H).transpose(0, 2, 1, 3)
        d_qk = D_H + D_HR
        scores = jnp.einsum('bhqd,bhkd->bhqk', q, k)
        scores = jnp.clip(scores, -80.0, 80.0)
        causal = pos[:, None] >= pos[None, :]
        scores = jnp.where(causal[None, None], scores, -jnp.inf)
        weights = jax.nn.softmax(scores / jnp.sqrt(jnp.float32(d_qk)), axis=-1)
        attn = jnp.einsum('bhqk,bhkd->bhqd', weights, v)
        out = attn.transpose(0, 2, 1, 3).reshape(B, S, H * D_H) @ W_O.T
        return out

    def _L0_ffn_ref(x, weight, lora_A, lora_B, router_w):
        import jax, jax.numpy as jnp
        import numpy as np
        NUM_EXPERTS = 8
        RANK = 16
        TOP_K = 2
        SCALING = 32.0 / RANK
        IN_F = 512
        OUT_F = 512
        B, T, D = x.shape
        N = B * T
        base = jnp.einsum('btd,od->bto', x, weight)
        logits = jnp.einsum('btd,ed->bte', x, router_w)
        probs = jax.nn.softmax(logits, axis=-1)
        topk_vals, topk_idx = jax.lax.top_k(probs, TOP_K)
        topk_vals = topk_vals / topk_vals.sum(axis=-1, keepdims=True)
        w_dense = jnp.zeros((N, NUM_EXPERTS), dtype=x.dtype).at[jnp.arange(N)[:, None], topk_idx.reshape(N, TOP_K)].set(topk_vals.reshape(N, TOP_K))
        x_flat = x.reshape(N, D)
        Ax = jnp.einsum('nd,erd->ner', x_flat, lora_A)
        expert_out = jnp.einsum('ner,ne,eor->no', Ax, w_dense, lora_B) * SCALING
        return base + expert_out.reshape(B, T, OUT_F)
    x = L0_attn_x
    xn = _layernorm(x, axis=-1)
    s = _L0_attn_ref(xn, L0_attn_W_DQ, L0_attn_W_UQ, L0_attn_W_QR, L0_attn_W_DKV, L0_attn_W_UK, L0_attn_W_UV, L0_attn_W_KR, L0_attn_W_O)
    g = _silu(_L0_ffn_ref(xn, L0_ffn_weight, L0_ffn_lora_A, L0_ffn_lora_B, L0_ffn_router_w))
    x = x + s * g
    return x

_drawn_inputs = setup_inputs


def setup_inputs(seed=0):
    import zlib

    import numpy as np

    out = dict(_drawn_inputs(seed))
    spreads = {}
    factors = {'L0_ffn_lora_A': 8.0, 'L0_ffn_lora_B': 8.0, 'L0_ffn_router_w': 8.0}
    for name, (base, spread) in spreads.items():
        noise = np.random.default_rng([zlib.crc32(name.encode()), seed]).standard_normal(out[name].shape)
        drawn = base * np.exp(spread * noise) if base else spread * noise
        out[name] = jnp.asarray(drawn.astype(out[name].dtype))
    for name, factor in factors.items():
        out[name] = (out[name] * factor).astype(out[name].dtype)
    return out
```

```python
from contextlib import ExitStack

import concourse.bass as bass
from concourse import mybir
from concourse.alu_op_type import AluOpType as ALU

ACT = mybir.ActivationFunctionType
AX = mybir.AxisListType
F32 = mybir.dt.float32
F32R = mybir.dt.float32r

P = 128
SEQ = 2048
DIM = 512
KC = DIM // P
TILES = SEQ // P
HEADS = 16
LAT = 128
ROT = 64
HALF = ROT // 2
EXPERTS, RANK = 8, 16
ER = EXPERTS * RANK
LORA_SCALE = 32.0 / RANK
EPS = 1e-5
QK_SCALE = (P + ROT) ** -0.5
CLIP = 80.0
P_MAX = 2.718281828459045 ** (CLIP * QK_SCALE)
P_MIN = 2.718281828459045 ** (-CLIP * QK_SCALE)

GROUP = 4
GROUPS = TILES // GROUP
GT = GROUP * P

C_BASE = 0
C_A = DIM
C_ROUTER = C_A + ER
C_KV = C_ROUTER + EXPERTS
C_Q = C_KV + LAT
C_KR = C_Q + LAT
C_ALL = C_KR + 2 * ROT
SMALL = C_Q - C_A

COUPLES = TILES // 2
CT = 2 * P
UNITS = 2 * COUPLES
UHEADS = HEADS // 2
HQ = UHEADS * CT
HW = HQ // 2
HH = UHEADS // 2
SK = 3 * P
SV = 2 * P


def since(eng, sem, count):
    if not isinstance(count, int) or count > 0:
        eng.wait_ge(sem, count)


def raw(ap):
    return ap.bitcast(F32)


class Persistent:

    def __init__(self, nc, ctx):
        def sb(name, shape, dt):
            return ctx.enter_context(nc.sbuf_tensor(name, shape, dt))

        self.cos = sb("cos", [P, SEQ + CT], F32)
        self.sin = sb("sin", [P, SEQ + CT], F32)
        self.absorb_h = sb("absorb_h", [P, HQ], F32R)
        self.absorb_l = sb("absorb_l", [P, HQ], F32R)
        self.qr_h = sb("qr_h", [P, 2 * GT], F32R)
        self.qr_l = sb("qr_l", [P, 2 * GT], F32R)
        self.cq_h = sb("cq_h", [P, SEQ + CT], F32R)
        self.cq_l = sb("cq_l", [P, SEQ + CT], F32R)
        self.causal = sb("causal", [P, CT], F32)
        self.strip = sb("strip", [P, 2 * UHEADS - 1], F32)


def prepare(nc, keep, x, w_all, w_uq, w_uk, w_qr, lora_b, cos, sin, keys, values, linear):
    ctx = ExitStack()
    with ctx:
        def sb(name, shape, dt=F32):
            return ctx.enter_context(nc.sbuf_tensor(name, shape, dt))

        def ps(name, shape):
            return ctx.enter_context(nc.psum_tensor(name, shape, F32))

        def sem(name):
            return ctx.enter_context(nc.semaphore(name))

        x_all = sb("x_all", [P, TILES, DIM])
        w_stage = sb("w_stage", [P, KC, C_ALL])
        w_h = sb("w_h", [P, KC, C_ALL], F32R)
        w_l = sb("w_l", [P, KC, C_ALL], F32R)
        xn = sb("xn", [P, GROUP, DIM])
        y = sb("y", [P, GROUP, DIM])
        qr_stage = sb("qr_stage", [P, 2 * GT])
        b_stage = sb("b_stage", [P, DIM])
        b_h = sb("b_h", [P, DIM], F32R)
        b_l = sb("b_l", [P, DIM], F32R)
        xt_h = sb("xt_h", [P, KC, GT], F32R)
        xt_l = sb("xt_l", [P, KC, GT], F32R)
        key_out = sb("key_out", [P, GROUP, SK], F32R)
        value_out = sb("value_out", [P, GROUP, SV], F32R)
        small = sb("small", [P, GROUP, ER + EXPERTS])
        turn_h = sb("turn_h", [P, GROUP, P], F32R)
        turn_l = sb("turn_l", [P, GROUP, P], F32R)
        weighted = sb("weighted", [P, GROUP, ER])
        rot_a = sb("rot_a", [P, GT])
        rot_b = sb("rot_b", [P, GT])
        ident = sb("ident", [P, P])
        stats = sb("stats", [P, TILES, 6])
        moments = sb("moments", [P, TILES, 2])
        deviation = sb("deviation", [P, TILES])
        rstd = sb("rstd", [P, TILES])
        eps = sb("eps", [P, 1])
        order = sb("order", [P, EXPERTS])
        r1 = sb("r1", [P, GROUP])
        rt = [sb(f"rt{n}", [P, GROUP, EXPERTS]) for n in range(5)]
        rw = sb("rw", [P, GROUP, EXPERTS])

        base_ps = ps("base_ps", [P, GROUP, DIM])
        turn_ps = ps("turn_ps", [P, 2, 512])
        work_ps = ps("work_ps", [P, 2, 512])

        x_in = [sem(f"x_in{g}") for g in range(GROUPS)]
        uqk_in, w_in, rest_in = sem("uqk_in"), sem("w_in"), sem("rest_in")
        constants = sem("constants")
        cleared = sem("cleared")
        absorbed = sem("absorbed")
        absorb_high = sem("absorb_high")
        absorb_split = sem("absorb_split")
        high_done = sem("high_done")
        low_done = sem("low_done")
        chain = sem("chain")
        var_done, dev_done = sem("var_done"), sem("dev_done")
        norm_done = sem("norm_done")
        turned = sem("turned")
        turn_high = sem("turn_high")
        turn_used = sem("turn_used")
        worked = sem("worked")
        work_high = sem("work_high")
        work_used = sem("work_used")
        based = sem("based")
        router_x = sem("router_x")
        router_e = sem("router_e")
        router_s = sem("router_s")
        weighted_done = sem("weighted_done")
        linear_done = sem("linear_done")
        y_done = sem("y_done")
        rope_s = sem("rope_s")
        keys_out, values_out, y_out = sem("keys_out"), sem("values_out"), sem("y_out")

        uq = xn[:, :, :].rearrange("p a n -> p (a n)")
        uk = y[:, :, :].rearrange("p a n -> p (a n)")
        WORK = GROUP + 3
        TURN = 2 * GROUP
        ROUTER = 15
        ROPE = 5
        KEY_STORES = 5

        block = ctx.enter_context(nc.Block())

        @block.sync
        def _(sp):
            sp.dma_start(uq, w_uq).then_inc(uqk_in, 16)
            sp.dma_start(uk, w_uk).then_inc(uqk_in, 16)
            for g in range(GROUPS):
                sp.dma_start(x_all[:, g * GROUP:(g + 1) * GROUP, :],
                             x[g * GT:(g + 1) * GT, :].rearrange("(a p) n -> p a n", p=P)).then_inc(x_in[g], 16)
                if g == 0:
                    sp.dma_start(w_stage[:, :, :], w_all.rearrange("(c p) n -> p c n", p=P)).then_inc(w_in, 16)
            sp.dma_start(qr_stage[:, :], w_qr).then_inc(rest_in, 16)
            sp.dma_start(b_stage[:, :], lora_b).then_inc(rest_in, 16)
            sp.dma_start(keep.cos[:, 0:SEQ], cos).then_inc(rest_in, 16)
            sp.dma_start(keep.sin[:, 0:SEQ], sin).then_inc(rest_in, 16)
            with sp.Fori(0, GROUPS) as g:
                sp.wait_ge(work_used, WORK * g + GROUP)
                sp.dma_start(values[bass.ds(g * GROUP, GROUP), :, :].rearrange("a p n -> p a n"),
                             raw(value_out[:, :, :])).then_inc(values_out, 16)
                sp.wait_ge(rope_s, ROPE * (g + 1))
                out = keys[bass.ds(g * GROUP, GROUP), :, :]
                sp.dma_start(out[:, :, 0:2 * P].rearrange("a p n -> p a n"),
                             raw(key_out[:, :, 0:2 * P])).then_inc(keys_out, 16)
                for n in range(4):
                    rows = out[:, (n // 2) * ROT:(n // 2 + 1) * ROT, 2 * P:SK].rearrange("a (f e) n -> e f a n", e=2)
                    sp.dma_start(rows[n % 2], raw(key_out[n * HALF:(n + 1) * HALF, :, 2 * P:SK])).then_inc(keys_out, 16)
                sp.wait_ge(y_done, GROUP * (g + 1))
                sp.dma_start(linear[bass.ds(g * GROUP, GROUP), :, :].rearrange("a p n -> p a n"),
                             y[:, :, :]).then_inc(y_out, 16)
            sp.wait_ge(keys_out, 16 * KEY_STORES * GROUPS)
            for s in (values_out, y_out):
                sp.wait_ge(s, 16 * GROUPS)

        @block.gpsimd
        def _(pool):
            nc.gpsimd.memset(ident[:, :], 0.0).then_inc(cleared, 1)
            nc.gpsimd.memset(keep.causal[:, :], 1.0).then_inc(cleared, 1)
            nc.gpsimd.memset(keep.strip[:, :], 0.0).then_inc(cleared, 1)
            nc.gpsimd.memset(eps[:, :], EPS).then_inc(constants, 1)
            for e in range(EXPERTS):
                nc.gpsimd.memset(order[:, e:e + 1], float(EXPERTS - e)).then_inc(constants, 1)
            for t in (keep.cos, keep.sin, raw(keep.cq_h[:, :]), raw(keep.cq_l[:, :])):
                nc.gpsimd.memset(t[:, SEQ:SEQ + CT], 0.0).then_inc(constants, 1)
            pool.wait_ge(cleared, 3)
            nc.gpsimd.affine_select(out=ident[:, :], in_=ident[:, :], compare_op=ALU.not_equal, fill=1.0,
                                    base=0, pattern=[[-1, P]], channel_multiplier=1).then_inc(constants, 1)
            nc.gpsimd.affine_select(out=keep.causal[:, :], in_=keep.causal[:, :], compare_op=ALU.is_ge, fill=0.0,
                                    base=0, pattern=[[1, CT]], channel_multiplier=-1).then_inc(constants, 1)
            nc.gpsimd.memset(keep.strip[:, UHEADS - 1:UHEADS], 1.0).then_inc(constants, 1)

        CONSTANTS = 1 + EXPERTS + 4 + 3

        @block.tensor
        def _(pe):
            pe.wait_ge(uqk_in, 32)
            for h in range(HEADS):
                mm = pe.matmul(base_ps[:, h // 4, (h % 4) * P:(h % 4 + 1) * P], uq[:, h * P:(h + 1) * P],
                               uk[:, h * P:(h + 1) * P], start=True, stop=True)
                if h % 8 == 7:
                    mm.then_inc(absorbed, 1)
            pe.wait_ge(constants, CONSTANTS)

            def turn_x(a, ready, n):
                pe.wait_ge(norm_done, ready + a + 1)
                since(pe, turn_used, n + a - 1)
                for c in range(KC):
                    mm = pe.transpose(turn_ps[:, a % 2, c * P:(c + 1) * P], xn[:, a, c * P:(c + 1) * P], ident[:, :])
                mm.then_inc(turned, 1)

            for a in range(GROUP):
                turn_x(a, 0, 0)

            def group(g, last):
                pe.wait_ge(turn_used, TURN * g + GROUP)
                for a in range(GROUP):
                    since(pe, work_used, WORK * g + (a - 1 if a else 0))
                    n = 0
                    for c in range(KC):
                        for xs, ws in ((xt_h, w_h), (xt_l, w_h), (xt_h, w_l)):
                            mm = pe.matmul(work_ps[:, a % 2, 0:SMALL], xs[:, c, a * P:(a + 1) * P],
                                           ws[:, c, C_A:C_Q], start=(n == 0), stop=(n == 3 * KC - 1))
                            n += 1
                    mm.then_inc(worked, 1)
                for k, col in enumerate((C_KV, C_Q, C_KR)):
                    pe.wait_ge(work_used, WORK * g + GROUP + k - 1)
                    n = 0
                    for c in range(KC):
                        for ws, xs in ((w_h, xt_h), (w_l, xt_h), (w_h, xt_l)):
                            mm = pe.matmul(work_ps[:, (GROUP + k) % 2, :], ws[:, c, col:col + P], xs[:, c, :],
                                           start=(n == 0), stop=(n == 3 * KC - 1))
                            n += 1
                    mm.then_inc(worked, 1)
                since(pe, y_done, GROUP * g)
                for a in range(GROUP):
                    n = 0
                    for c in range(KC):
                        for xs, ws in ((xt_h, w_h), (xt_l, w_h), (xt_h, w_l)):
                            mm = pe.matmul(base_ps[:, a, :], xs[:, c, a * P:(a + 1) * P], ws[:, c, 0:DIM],
                                           start=(n == 0), stop=False)
                            n += 1
                mm.then_inc(based, 1)
                if not last:
                    for a in range(GROUP):
                        turn_x(a, GROUP * (g + 1), TURN * g + GROUP)
                pe.wait_ge(weighted_done, g + 1)
                n0 = TURN * g + (GROUP if last else 2 * GROUP)
                for a in range(GROUP):
                    pe.wait_ge(turn_used, n0 + a - 1)
                    pe.transpose(turn_ps[:, a % 2, 0:P], weighted[:, a, :], ident[:, :]).then_inc(turned, 1)
                for a in range(GROUP):
                    pe.wait_ge(turn_used, n0 + a + 1)
                    pe.matmul(base_ps[:, a, :], turn_h[:, a, :], b_h[:, :], start=False, stop=False)
                    pe.matmul(base_ps[:, a, :], turn_l[:, a, :], b_h[:, :], start=False, stop=False)
                    pe.matmul(base_ps[:, a, :], turn_h[:, a, :], b_l[:, :], start=False,
                              stop=True).then_inc(linear_done, 1)

            pe.wait_ge(absorb_split, 2)
            pe.wait_ge(low_done, 3)
            group(0, False)
            with pe.Fori(1, GROUPS - 1) as g:
                group(g, False)
            group(GROUPS - 1, True)

        @block.scalar
        def _(act):
            for half in range(2):
                act.wait_ge(absorbed, half + 1)
                nc.scalar.copy(keep.absorb_h[:, half * HW:(half + 1) * HW],
                               base_ps[:, 2 * half:2 * half + 2, :]).then_inc(absorb_high, 1)
            act.wait_ge(w_in, 16)
            nc.scalar.copy(w_h[:, :, :], w_stage[:, :, :]).then_inc(high_done, 1)
            act.wait_ge(rest_in, 64)
            nc.scalar.copy(keep.qr_h[:, :], qr_stage[:, :]).then_inc(high_done, 1)
            nc.scalar.copy(b_h[:, :], b_stage[:, :]).then_inc(high_done, 1)
            act.wait_ge(var_done, 1)
            act.wait_ge(constants, 1)
            nc.scalar.activation(deviation[:, :], moments[:, :, 1], ACT.Sqrt, bias=eps[:, 0:1]).then_inc(dev_done, 1)

            def turn_x(a, n):
                act.wait_ge(turned, n + a + 1)
                nc.scalar.copy(xt_h[:, :, a * P:(a + 1) * P],
                               turn_ps[:, a % 2, :].rearrange("p (c t) -> p c t", c=KC)).then_inc(turn_high, 1)

            for a in range(GROUP):
                turn_x(a, 0)

            def group(g, last):
                since(act, values_out, 16 * g)
                for a in range(GROUP):
                    act.wait_ge(worked, WORK * g + a + 1)
                    nc.scalar.copy(value_out[:, a, 0:P], work_ps[:, a % 2, C_KV - C_A:SMALL]).then_inc(work_high, 1)
                act.wait_ge(router_x, g + 1)
                nc.scalar.activation(rt[1][:, :, :], rt[0][:, :, :], ACT.Exp).then_inc(router_e, 1)
                since(act, keys_out, 16 * KEY_STORES * g)
                act.wait_ge(worked, WORK * g + GROUP + 1)
                nc.scalar.copy(key_out[:, :, 0:P],
                               work_ps[:, 0, :].rearrange("p (a t) -> p a t", a=GROUP)).then_inc(work_high, 1)
                act.wait_ge(worked, WORK * g + GROUP + 2)
                nc.scalar.copy(keep.cq_h[:, bass.ds(g * GT, GT)], work_ps[:, 1, :]).then_inc(work_high, 1)
                if not last:
                    act.wait_ge(based, g + 1)
                    for a in range(GROUP):
                        turn_x(a, TURN * g + GROUP)
                n0 = TURN * g + (GROUP if last else 2 * GROUP)
                for a in range(GROUP):
                    act.wait_ge(turned, n0 + a + 1)
                    nc.scalar.copy(turn_h[:, a, :], turn_ps[:, a % 2, 0:P]).then_inc(turn_high, 1)
                since(act, y_out, 16 * g)
                for a in range(GROUP):
                    act.wait_ge(linear_done, GROUP * g + a + 1)
                    nc.scalar.copy(y[:, a, :], base_ps[:, a, :]).then_inc(y_done, 1)

            group(0, False)
            with act.Fori(1, GROUPS - 1) as g:
                group(g, False)
            group(GROUPS - 1, True)

        @block.vector
        def _(dve):
            for half in range(2):
                dve.wait_ge(absorb_high, half + 1)
                cols = slice(half * HW, (half + 1) * HW)
                nc.vector.tensor_tensor(keep.absorb_l[:, cols], base_ps[:, 2 * half:2 * half + 2, :].rearrange("p b n -> p (b n)"),
                                        keep.absorb_h[:, cols], ALU.subtract).then_inc(absorb_split, 1)
            for t in range(TILES):
                if t % GROUP == 0:
                    dve.wait_ge(x_in[t // GROUP], 16)
                nc.vector.bn_stats(stats[:, t, :], x_all[:, t, :]).then_inc(chain, 1)
            for t in range(TILES):
                dve.wait_ge(chain, t + 1)
                ins = nc.vector.bn_aggr(moments[:, t, :], stats[:, t, :])
            ins.then_inc(var_done, 1)
            dve.wait_ge(high_done, 1)
            nc.vector.tensor_tensor(w_l[:, :, :], w_stage[:, :, :], w_h[:, :, :], ALU.subtract).then_inc(low_done, 1)
            dve.wait_ge(high_done, 3)
            nc.vector.tensor_tensor(keep.qr_l[:, :], qr_stage[:, :], keep.qr_h[:, :], ALU.subtract).then_inc(low_done, 1)
            nc.vector.tensor_tensor(b_l[:, :], b_stage[:, :], b_h[:, :], ALU.subtract).then_inc(low_done, 1)
            dve.wait_ge(dev_done, 1)
            nc.vector.reciprocal(rstd[:, :], deviation[:, :]).then_inc(chain, 1)
            dve.wait_ge(chain, TILES + 1)

            def normalise(g, a):
                t = g * GROUP + a
                nc.vector.tensor_scalar(xn[:, a, :], x_all[:, bass.ds(t, 1), :].rearrange("p a n -> p (a n)"),
                                        moments[:, bass.ds(t, 1), 0], rstd[:, bass.ds(t, 1)],
                                        ALU.subtract, ALU.mult).then_inc(norm_done, 1)

            def turn_x(a, n):
                dve.wait_ge(turn_high, n + a + 1)
                cols = slice(a * P, (a + 1) * P)
                nc.vector.tensor_tensor(xt_l[:, :, cols], turn_ps[:, a % 2, :].rearrange("p (c t) -> p c t", c=KC),
                                        xt_h[:, :, cols], ALU.subtract).then_inc(turn_used, 1)

            for a in range(GROUP):
                normalise(0, a)
            for a in range(GROUP):
                turn_x(a, 0)
            dve.wait_ge(constants, CONSTANTS)

            def group(g, last):
                for a in range(GROUP):
                    dve.wait_ge(work_high, (WORK - 1) * g + a + 1)
                    nc.vector.tensor_copy(small[:, a, :], work_ps[:, a % 2, 0:ER + EXPERTS])
                    nc.vector.tensor_tensor(value_out[:, a, P:SV], work_ps[:, a % 2, C_KV - C_A:SMALL],
                                            value_out[:, a, 0:P], ALU.subtract).then_inc(work_used, 1)
                shape = [P, GROUP, EXPERTS]
                logits = small[:, :, ER:ER + EXPERTS]
                ranks = order[:, :].unsqueeze(1).to_broadcast(shape)
                most = r1[:, :].unsqueeze(2).to_broadcast(shape)
                key, expo, first, second, rest = rt[0], rt[1], rt[2], rt[3], rt[4]
                step = [0]

                def then(ins):
                    step[0] += 1
                    ins.then_inc(router_s, 1)
                    dve.wait_ge(router_s, ROUTER * g + step[0])

                dve.wait_ge(work_used, WORK * g + GROUP)
                then(nc.vector.tensor_reduce(r1[:, :], logits, AX.X, ALU.max))
                nc.vector.tensor_tensor(rt[0][:, :, :], logits, most, ALU.subtract).then_inc(router_x, 1)
                then(nc.vector.tensor_tensor(first[:, :, :], logits, most, ALU.is_equal))
                then(nc.vector.tensor_tensor(second[:, :, :], first[:, :, :], ranks, ALU.mult))
                then(nc.vector.tensor_reduce(r1[:, :], second[:, :, :], AX.X, ALU.max))
                then(nc.vector.tensor_tensor(first[:, :, :], second[:, :, :], most, ALU.is_equal))
                then(nc.vector.scalar_tensor_tensor(out=rest[:, :, :], in0=first[:, :, :], scalar=-3.0e38, in1=logits,
                                                    op0=ALU.mult, op1=ALU.add))
                then(nc.vector.tensor_reduce(r1[:, :], rest[:, :, :], AX.X, ALU.max))
                then(nc.vector.tensor_tensor(second[:, :, :], rest[:, :, :], most, ALU.is_equal))
                then(nc.vector.tensor_tensor(rest[:, :, :], second[:, :, :], ranks, ALU.mult))
                then(nc.vector.tensor_reduce(r1[:, :], rest[:, :, :], AX.X, ALU.max))
                then(nc.vector.tensor_tensor(second[:, :, :], rest[:, :, :], most, ALU.is_equal))
                then(nc.vector.tensor_tensor(rest[:, :, :], first[:, :, :], second[:, :, :], ALU.add))
                dve.wait_ge(router_e, g + 1)
                then(nc.vector.tensor_tensor(rest[:, :, :], rest[:, :, :], expo[:, :, :], ALU.mult))
                then(nc.vector.tensor_reduce(r1[:, :], rest[:, :, :], AX.X, ALU.add))
                then(nc.vector.reciprocal(r1[:, :], r1[:, :]))
                nc.vector.scalar_tensor_tensor(out=rw[:, :, :], in0=rest[:, :, :], scalar=LORA_SCALE, in1=most,
                                               op0=ALU.mult, op1=ALU.mult).then_inc(chain, 1)
                dve.wait_ge(chain, g + TILES + 2)
                nc.vector.tensor_tensor(
                    weighted[:, :, :].rearrange("p a (e r) -> p (a e) r", r=RANK),
                    small[:, :, 0:ER].rearrange("p a (e r) -> p a e r", r=RANK),
                    rw[:, :, :].rearrange("p a e -> p (a e)").unsqueeze(2).to_broadcast([P, GROUP * EXPERTS, RANK]),
                    ALU.mult).then_inc(weighted_done, 1)
                assert step[0] == ROUTER

                dve.wait_ge(work_high, (WORK - 1) * g + GROUP + 1)
                nc.vector.tensor_tensor(key_out[:, :, P:2 * P], work_ps[:, 0, :].rearrange("p (a t) -> p a t", a=GROUP),
                                        key_out[:, :, 0:P], ALU.subtract).then_inc(work_used, 1)
                dve.wait_ge(work_high, (WORK - 1) * g + GROUP + 2)
                nc.vector.tensor_tensor(keep.cq_l[:, bass.ds(g * GT, GT)], work_ps[:, 1, :],
                                        keep.cq_h[:, bass.ds(g * GT, GT)], ALU.subtract).then_inc(work_used, 1)
                dve.wait_ge(worked, WORK * g + WORK)
                nc.vector.tensor_tensor(rot_a[0:ROT, :], work_ps[0:ROT, 0, :], keep.cos[0:ROT, bass.ds(g * GT, GT)],
                                        ALU.mult).then_inc(rope_s, 1)
                nc.vector.tensor_tensor(rot_b[0:ROT, :], work_ps[ROT:P, 0, :], keep.sin[ROT:P, bass.ds(g * GT, GT)],
                                        ALU.mult).then_inc(work_used, 1)
                dve.wait_ge(work_used, WORK * (g + 1))
                nc.vector.tensor_tensor(rot_a[0:HALF, :], rot_a[0:HALF, :], rot_b[0:HALF, :],
                                        ALU.subtract).then_inc(rope_s, 1)
                nc.vector.tensor_tensor(rot_a[HALF:ROT, :], rot_a[HALF:ROT, :], rot_b[HALF:ROT, :],
                                        ALU.add).then_inc(rope_s, 1)
                dve.wait_ge(rope_s, ROPE * g + 3)
                turned_keys = rot_a[0:ROT, :].rearrange("p (a t) -> p a t", a=GROUP)
                nc.vector.tensor_copy(key_out[0:ROT, :, 2 * P:SK], turned_keys).then_inc(rope_s, 1)
                dve.wait_ge(rope_s, ROPE * g + 4)
                nc.vector.tensor_tensor(key_out[ROT:P, :, 2 * P:SK], turned_keys, key_out[0:ROT, :, 2 * P:SK],
                                        ALU.subtract).then_inc(rope_s, 1)

                if not last:
                    for a in range(GROUP):
                        normalise(g + 1, a)
                    for a in range(GROUP):
                        turn_x(a, TURN * g + GROUP)
                n0 = TURN * g + (GROUP if last else 2 * GROUP)
                for a in range(GROUP):
                    dve.wait_ge(turn_high, n0 + a + 1)
                    nc.vector.tensor_tensor(turn_l[:, a, :], turn_ps[:, a % 2, 0:P], turn_h[:, a, :],
                                            ALU.subtract).then_inc(turn_used, 1)

            group(0, False)
            with dve.Fori(1, GROUPS - 1) as g:
                group(g, False)
            group(GROUPS - 1, True)


FULL, CORNER, LATE = range(3)


def sweep(eng, pair):

    def two(t, unit, couple, par, k, prev):
        pair(t, unit, couple, k, par, 0, FULL, prev)
        pair(t + 1, unit, couple, k + 1, par, 1, FULL, FULL)

    def start(t, unit, couple, par, prev):
        pair(t, unit, couple, 2 * couple, par, 0, CORNER, prev)
        pair(t + 1, unit, couple, 2 * couple + 1, par, 1, LATE, CORNER)

    start(0, 0, 0, 0, None)
    start(2, 1, 0, 1, LATE)
    for par in range(2):
        start(4 + 4 * par, 2 + par, 1, par, FULL if par else LATE)
        two(6 + 4 * par, 2 + par, 1, par, 0, LATE)
    done = eng.alloc_register("pairs_done")
    eng.reg_mov(done, 12)
    with eng.Fori(2, COUPLES) as m:
        before = eng.snap(done, min_val=12, max_val=PAIRS)
        for par in range(2):
            t = before + par * (2 * m + 2)
            start(t, 2 * m + par, m, par, FULL)
            two(t + 2, 2 * m + par, m, par, 0, LATE)
            with eng.Fori(1, m) as n:
                two(t + 2 + 2 * n, 2 * m + par, m, par, 2 * n, FULL)
        eng.reg_add(done, done, 4 * m + 4)


PAIRS = 2 * COUPLES * (COUPLES + 1)
SPREADS = 3


def attend(nc, keep, keys, values, turned, heads_out, sums_out):
    ctx = ExitStack()
    with ctx:
        def sb(name, shape, dt=F32):
            return ctx.enter_context(nc.sbuf_tensor(name, shape, dt))

        def sem(name):
            return ctx.enter_context(nc.semaphore(name))

        key_slot = [sb(f"key_slot{n}", [P, SK], F32R) for n in range(2)]
        value_slot = [sb(f"value_slot{n}", [P, SV], F32R) for n in range(2)]
        q_h = [sb(f"q_h{n}", [P, HQ], F32R) for n in range(2)]
        q_l = [sb(f"q_l{n}", [P, HQ], F32R) for n in range(2)]
        rot_hh = [sb(f"rot_hh{n}", [P, HQ], F32R) for n in range(2)]
        rot_l0 = [sb(f"rot_l0{n}", [P, HQ], F32R) for n in range(2)]
        prob = [sb(f"prob{n}", [P, HW]) for n in range(2)]
        prob_h = [sb(f"prob_h{n}", [P, HW], F32R) for n in range(2)]
        prob_l = [sb(f"prob_l{n}", [P, HW], F32R) for n in range(2)]
        total = [sb(f"total{n}", [P, HQ]) for n in range(2)]
        head_rows = sb("head_rows", [P, HQ])
        prod = [sb(f"prod{n}", [P, 512]) for n in range(4)]
        rot_f = sb("rot_f", [P, 2, 512])
        rot_hl = sb("rot_hl", [P, 2, 2, 512], F32R)
        inverse = sb("inverse", [UHEADS, CT])

        score_ps = ctx.enter_context(nc.psum_tensor("score_ps", [P, 2, HW], F32))
        out_ps = ctx.enter_context(nc.psum_tensor("out_ps", [P, 4, 512], F32))

        zeroed = sem("zeroed")
        keys_in, values_in = sem("keys_in"), sem("values_in")
        scored = sem("scored")
        exp_done = sem("exp_done")
        min_done = sem("min_done")
        clipped = sem("clipped")
        high_done = sem("high_done")
        summed = sem("summed")
        split = sem("split")
        weighed = sem("weighed")
        out_read = sem("out_read")
        q_scored = sem("q_scored")
        q_high = sem("q_high")
        q_split = sem("q_split")
        r_scored = sem("r_scored")
        r_read = sem("r_read")
        r_step = sem("r_step")
        passed = sem("passed")
        scattered = sem("scattered")
        summed_up = sem("summed_up")
        inverted = sem("inverted")
        heads_stored, sums_stored = sem("heads_stored"), sem("sums_stored")

        block = ctx.enter_context(nc.Block())

        def one_of(ap, n):
            return ap[bass.ds(n, 1), :, :].rearrange("a p n -> (a p) n")

        @block.sync
        def _(sp):
            loads_before = sp.alloc_register("loads_before")

            def pair(t, unit, couple, k, par, slot, kind, prev):
                loaded = 16 * t
                if not isinstance(t, int):
                    sp.reg_mov(loads_before, loaded)
                    loaded = sp.snap(loads_before, min_val=0, max_val=16 * PAIRS)
                since(sp, scored, 2 * (t - 1))
                since(sp, keys_in, loaded)
                sp.dma_start(raw(key_slot[slot][:, :]), one_of(keys, k)).then_inc(keys_in, 16)
                since(sp, weighed, 2 * (t - 1))
                since(sp, values_in, loaded)
                sp.dma_start(raw(value_slot[slot][:, :]), one_of(values, k)).then_inc(values_in, 16)

            sweep(sp, pair)
            sp.wait_ge(heads_stored, 16 * UNITS)
            sp.wait_ge(sums_stored, 16 * UNITS)
            sp.wait_ge(scattered, 16 * SPREADS * (UNITS + 1))

        @block.gpsimd
        def _(pool):
            passes = pool.alloc_register("passes")
            pool.reg_mov(passes, 16)
            for n in range(2):
                nc.gpsimd.memset(raw(rot_l0[n][ROT:P, :]), 0.0).then_inc(zeroed, 1)

            def spread(unit, par):
                mine = turned[bass.ds(unit, 1), :, :, :]
                pool.wait_ge(r_step, 4 * unit + 4)
                pool.dma_start(mine.rearrange("a w p n -> p (a w) n"),
                               raw(rot_hl[:, :, :, :]).rearrange("p w e n -> p w (e n)")).then_inc(passed, 16)
                pool.wait_ge(passed, passes)
                pool.reg_add(passes, passes, 16)
                for to, rows, part in ((rot_hh, 0, 0), (rot_hh, ROT, 0), (rot_l0, 0, 1)):
                    pool.dma_start(raw(to[par][rows:rows + ROT, :]).rearrange("r (q n) -> r q n", q=4),
                                   mine[:, part, :, :].rearrange("a (q f) (e n) -> (f e) (a q) n", q=4, e=2)).then_inc(scattered, 16)

            def store(unit):
                pool.wait_ge(out_read, 2 * unit + 2)
                pool.dma_start(one_of(heads_out, unit), head_rows[:, :]).then_inc(heads_stored, 16)
                pool.wait_ge(inverted, unit + 1)
                pool.dma_start(one_of(sums_out, unit), inverse[:, :]).then_inc(sums_stored, 16)

            spread(0, 0)
            spread(1, 1)
            spread(2, 0)
            store(0)
            with pool.Fori(1, COUPLES) as m:
                spread(2 * m + 1, 1)
                store(2 * m - 1)
                spread(2 * m + 2, 0)
                store(2 * m)
            store(UNITS - 1)

        @block.tensor
        def _(pe):
            def latent(couple, heads, half):
                tokens = bass.ds(couple * CT, CT)
                for h in range(HH):
                    head = heads * UHEADS + half * HH + h
                    w, out = slice(head * P, (head + 1) * P), score_ps[:, half, h * CT:(h + 1) * CT]
                    pe.matmul(out, keep.absorb_h[:, w], keep.cq_h[:, tokens], start=True, stop=False)
                    pe.matmul(out, keep.absorb_h[:, w], keep.cq_l[:, tokens], start=False, stop=False)
                    mm = pe.matmul(out, keep.absorb_l[:, w], keep.cq_h[:, tokens], start=False, stop=True)
                mm.then_inc(q_scored, 1)

            def rotary(couple, heads):
                tokens = bass.ds(couple * CT, CT)
                for n in range(4):
                    w, out = slice((4 * heads + n) * P, (4 * heads + n + 1) * P), score_ps[:, 0, n * CT:(n + 1) * CT]
                    pe.matmul(out, keep.qr_h[:, w], keep.cq_h[:, tokens], start=True, stop=False)
                    pe.matmul(out, keep.qr_h[:, w], keep.cq_l[:, tokens], start=False, stop=False)
                    mm = pe.matmul(out, keep.qr_l[:, w], keep.cq_h[:, tokens], start=False, stop=True)
                mm.then_inc(r_scored, 1)

            def sum_up(par):
                for h in range(UHEADS):
                    mm = pe.matmul(score_ps[0:UHEADS, 1, 0:CT], keep.strip[:, UHEADS - 1 - h:2 * UHEADS - 1 - h],
                                   total[par][:, h * CT:(h + 1) * CT], start=(h == 0), stop=(h == UHEADS - 1))
                mm.then_inc(summed_up, 1)

            def scores(half, par, slot, kind):
                key_high, key_low, key_rot = (key_slot[slot][:, n * P:(n + 1) * P] for n in range(3))

                def columns(buffer, c):
                    if kind == LATE:
                        heads = buffer[:, :].rearrange("p (h t) -> p h t", t=CT)
                        return heads[:, half * HH:(half + 1) * HH, P:CT]
                    return buffer[:, half * HW + c * 512:half * HW + (c + 1) * 512]

                for c in range(1 if kind == LATE else 2):
                    out = score_ps[:, half, c * 512:(c + 1) * 512]
                    pe.matmul(out, key_high, columns(q_h[par], c), start=True, stop=False)
                    pe.matmul(out, key_high, columns(q_l[par], c), start=False, stop=False)
                    pe.matmul(out, key_low, columns(q_h[par], c), start=False, stop=False)
                    pe.matmul(out, key_rot, columns(rot_hh[par], c), start=False, stop=False)
                    mm = pe.matmul(out, key_rot, columns(rot_l0[par], c), start=False, stop=True)
                mm.then_inc(scored, 1)

            def weigh(t, half, slot, kind, last):
                pe.wait_ge(split, 2 * t + half + 1)
                high, low = value_slot[slot][:, 0:P], value_slot[slot][:, P:SV]
                first = kind == CORNER
                for c in range(2):
                    out = out_ps[:, 2 * half + c, :]
                    cols = slice(c * 512, (c + 1) * 512)
                    p_h, p_l = prob_h[half][:, cols], prob_l[half][:, cols]
                    if kind == LATE:
                        out = out.rearrange("p (h t) -> p h t", t=CT)[:, :, P:CT]
                        cols = slice(c * 256, (c + 1) * 256)
                        p_h, p_l = (p[half][:, cols].rearrange("p (h t) -> p h t", t=P) for p in (prob_h, prob_l))
                    pe.matmul(out, high, p_h, start=first, stop=False)
                    pe.matmul(out, high, p_l, start=False, stop=False)
                    mm = pe.matmul(out, low, p_h, start=False, stop=last)
                mm.then_inc(weighed, 1)

            def pair(t, unit, couple, k, par, slot, kind, prev):
                pe.wait_ge(keys_in, 16 * (t + 1))
                if kind == CORNER:
                    pe.wait_ge(q_split, 2 * unit + 2)
                    pe.wait_ge(scattered, 16 * SPREADS * (unit + 1))
                if kind == LATE:
                    pe.wait_ge(r_read, 4 * (unit + 2))
                since(pe, exp_done, 2 * t - 1)
                scores(0, par, slot, kind)
                if prev is not None:
                    pe.wait_ge(values_in, 16 * t)
                    if prev == CORNER:
                        since(pe, out_read, 2 * unit - 1)
                    weigh(t - 1, 0, 1 - slot, prev, kind == CORNER)
                if kind == LATE:
                    since(pe, inverted, unit)
                since(pe, exp_done, 2 * t)
                scores(1, par, slot, kind)
                if kind == CORNER:
                    pe.wait_ge(exp_done, 2 * t + 1)
                    latent(couple + par, 1 - par, 0)
                if prev is not None:
                    if prev == CORNER:
                        since(pe, out_read, 2 * unit)
                    weigh(t - 1, 1, 1 - slot, prev, kind == CORNER)
                if kind == CORNER:
                    pe.wait_ge(exp_done, 2 * t + 2)
                    latent(couple + par, 1 - par, 1)
                    pe.wait_ge(q_split, 2 * unit + 3)
                    rotary(couple + par, 1 - par)
                    if prev is not None:
                        pe.wait_ge(q_split, 2 * unit + 4)
                        pe.wait_ge(summed, 2 * t)
                        sum_up(1 - par)

            latent(0, 0, 0)
            latent(0, 0, 1)
            pe.wait_ge(q_split, 1)
            rotary(0, 0)
            pe.wait_ge(r_read, 4)
            pe.wait_ge(zeroed, 2)
            sweep(pe, pair)
            pe.wait_ge(values_in, 16 * PAIRS)
            for half in range(2):
                weigh(PAIRS - 1, half, 1, FULL, True)
            pe.wait_ge(exp_done, 2 * PAIRS)
            pe.wait_ge(summed, 2 * PAIRS)
            sum_up(1)

        @block.scalar
        def _(act):
            def latent_high(unit, par, half):
                act.wait_ge(q_scored, 2 * unit + half + 1)
                nc.scalar.copy(q_h[par][:, half * HW:(half + 1) * HW], score_ps[:, half, :]).then_inc(q_high, 1)

            def read_out(unit, half):
                if half == 0:
                    since(act, heads_stored, 16 * unit)
                nc.scalar.copy(head_rows[:, half * HW:(half + 1) * HW],
                               out_ps[:, 2 * half:2 * half + 2, :]).then_inc(out_read, 1)

            def pair(t, unit, couple, k, par, slot, kind, prev):
                width = HW // 2 if kind == LATE else HW
                for half in range(2):
                    s = 2 * t + half
                    act.wait_ge(scored, s + 1)
                    since(act, split, s - 1)
                    nc.scalar.activation(prob[half][:, 0:width], score_ps[:, half, 0:width], ACT.Exp,
                                         scale=QK_SCALE).then_inc(exp_done, 1)
                    act.wait_ge(clipped, s + 1)
                    since(act, weighed, s - 1)
                    nc.scalar.copy(prob_h[half][:, 0:width], prob[half][:, 0:width]).then_inc(high_done, 1)
                if kind == CORNER:
                    latent_high(unit + 1, 1 - par, 0)
                    if prev is not None:
                        act.wait_ge(weighed, 2 * t - 1)
                        read_out(unit - 1, 0)
                        act.wait_ge(weighed, 2 * t)
                        read_out(unit - 1, 1)
                    latent_high(unit + 1, 1 - par, 1)

            for half in range(2):
                latent_high(0, 0, half)
            sweep(act, pair)
            for half in range(2):
                act.wait_ge(weighed, 2 * PAIRS - 1 + half)
                read_out(UNITS - 1, half)

        @block.vector
        def _(dve):
            def latent_low(unit, par, half):
                dve.wait_ge(q_high, 2 * unit + half + 1)
                cols = slice(half * HW, (half + 1) * HW)
                nc.vector.tensor_tensor(q_l[par][:, cols], score_ps[:, half, :], q_h[par][:, cols],
                                        ALU.subtract).then_inc(q_split, 1)

            def turn(unit, couple):
                dve.wait_ge(r_scored, unit + 1)
                tokens = bass.ds(couple * CT, CT)
                cos, sin = (w[:, tokens].unsqueeze(1).to_broadcast([P, 2, CT]) for w in (keep.cos, keep.sin))
                even, odd = (score_ps[:, 0, n * 512:(n + 1) * 512].rearrange("p (g t) -> p g t", g=2) for n in range(2))
                for out, rows, angle in zip(prod, (even, odd, even, odd), (cos, sin, sin, cos)):
                    nc.vector.tensor_tensor(out[:, :].rearrange("p (g t) -> p g t", g=2), rows, angle,
                                            ALU.mult).then_inc(r_read, 1)
                dve.wait_ge(r_read, 4 * unit + 4)
                nc.vector.tensor_tensor(rot_f[:, 0, :], prod[0][:, :], prod[1][:, :], ALU.subtract).then_inc(r_step, 1)
                nc.vector.tensor_tensor(rot_f[:, 1, :], prod[2][:, :], prod[3][:, :], ALU.add).then_inc(r_step, 1)
                since(dve, scattered, 16 * SPREADS * unit)
                dve.wait_ge(r_step, 4 * unit + 2)
                nc.vector.tensor_copy(rot_hl[:, 0, :, :], rot_f[:, :, :]).then_inc(r_step, 1)
                dve.wait_ge(r_step, 4 * unit + 3)
                nc.vector.tensor_tensor(rot_hl[:, 1, :, :], rot_f[:, :, :], rot_hl[:, 0, :, :],
                                        ALU.subtract).then_inc(r_step, 1)

            def invert(unit):
                dve.wait_ge(summed_up, unit + 1)
                since(dve, sums_stored, 16 * unit)
                nc.vector.reciprocal(inverse[:, :], score_ps[0:UHEADS, 1, 0:CT]).then_inc(inverted, 1)

            def pair(t, unit, couple, k, par, slot, kind, prev):
                tokens = P if kind == LATE else CT
                for half in range(2):
                    s = 2 * t + half
                    p, p_h, p_l = (b[half][:, 0:HH * tokens] for b in (prob, prob_h, prob_l))
                    p_by_head = p.rearrange("p (h t) -> p h t", t=tokens)
                    sums = total[par][:, half * HW:(half + 1) * HW].rearrange("p (h t) -> p h t", t=CT)[:, :, CT - tokens:CT]
                    dve.wait_ge(exp_done, s + 1)
                    if kind == FULL:
                        nc.vector.tensor_scalar(p, p, P_MIN, P_MAX, ALU.max, ALU.min).then_inc(clipped, 1)
                    else:
                        nc.vector.tensor_scalar(p, p, P_MAX, None, ALU.min).then_inc(min_done, 1)
                        dve.wait_ge(min_done, 4 * unit + (2 if kind == LATE else 0) + half + 1)
                        nc.vector.scalar_tensor_tensor(
                            out=p_by_head, in0=p_by_head, scalar=P_MIN,
                            in1=keep.causal[:, 0:tokens].unsqueeze(1).to_broadcast([P, HH, tokens]),
                            op0=ALU.max, op1=ALU.mult).then_inc(clipped, 1)
                    dve.wait_ge(clipped, s + 1)
                    if kind == CORNER:
                        since(dve, summed_up, unit - 1)
                        nc.vector.tensor_copy(sums, p_by_head).then_inc(summed, 1)
                    else:
                        dve.wait_ge(summed, s - 1)
                        nc.vector.tensor_tensor(sums, sums, p_by_head, ALU.add).then_inc(summed, 1)
                    dve.wait_ge(high_done, s + 1)
                    nc.vector.tensor_tensor(p_l, p, p_h, ALU.subtract).then_inc(split, 1)
                if kind == CORNER:
                    latent_low(unit + 1, 1 - par, 0)
                    latent_low(unit + 1, 1 - par, 1)
                    turn(unit + 1, couple + par)
                    if prev is not None:
                        invert(unit - 1)

            latent_low(0, 0, 0)
            latent_low(0, 0, 1)
            turn(0, 0)
            sweep(dve, pair)
            invert(UNITS - 1)


def combine(nc, x, w_uv, w_o, heads_in, inverses, linear, out):
    ctx = ExitStack()
    with ctx:
        def sb(name, shape, dt=F32):
            return ctx.enter_context(nc.sbuf_tensor(name, shape, dt))

        def sem(name):
            return ctx.enter_context(nc.semaphore(name))

        LOADS = 4
        PART = HEADS // LOADS
        uv = sb("uv", [P, HEADS, LAT])
        wo = sb("wo", [P, HEADS, DIM])
        merged_h = sb("merged_h", [P, HEADS, DIM], F32R)
        merged_l = sb("merged_l", [P, HEADS, DIM], F32R)
        rows = [sb(f"rows{n}", [P, HEADS, P]) for n in range(2)]
        scale = [sb(f"scale{n}", [P, HEADS, P]) for n in range(2)]
        rows_h = [sb(f"rows_h{n}", [P, HEADS, P], F32R) for n in range(2)]
        rows_l = [sb(f"rows_l{n}", [P, HEADS, P], F32R) for n in range(2)]
        x_in = [sb(f"x_in{n}", [P, DIM]) for n in range(2)]
        lin_in = [sb(f"lin_in{n}", [P, DIM]) for n in range(2)]
        gate = [sb(f"gate{n}", [P, DIM]) for n in range(2)]
        result = [sb(f"result{n}", [P, DIM]) for n in range(2)]
        merge_ps = ctx.enter_context(nc.psum_tensor("merge_ps", [P, 4, DIM], F32))
        sum_ps = ctx.enter_context(nc.psum_tensor("sum_ps", [P, 2, DIM], F32))

        weights_in = [sem(f"weights_in{n}") for n in range(LOADS)]
        merged = sem("merged")
        merge_high = sem("merge_high")
        merge_split = sem("merge_split")
        rows_in = [sem(f"rows_in{n}") for n in range(2)]
        gate_in = [sem(f"gate_in{n}") for n in range(2)]
        scaled = sem("scaled")
        rows_high = sem("rows_high")
        rows_split = sem("rows_split")
        sigmoid = sem("sigmoid")
        gated = sem("gated")
        projected = [sem(f"projected{n}") for n in range(2)]
        times = [sem(f"times{n}") for n in range(2)]
        finished = sem("finished")
        stored = [sem(f"stored{n}") for n in range(2)]

        block = ctx.enter_context(nc.Block())

        def tile_of(ap, t):
            return ap[bass.ds(t, 1), :, :].rearrange("a p n -> (a p) n")

        x_tiles = x.rearrange("(t p) n -> t p n", p=P)
        out_tiles = out.rearrange("(t p) n -> t p n", p=P)
        uv_in = w_uv.rearrange("p (h l) -> p h l", h=HEADS)

        @block.sync
        def _(sp):
            for n in range(LOADS):
                hs = slice(n * PART, (n + 1) * PART)
                sp.dma_start(uv[:, hs, :], uv_in[:, hs, :]).then_inc(weights_in[n], 16)
                sp.dma_start(wo[:, hs, :], w_o[:, hs, :]).then_inc(weights_in[n], 16)

            def load(t, par):
                since(sp, rows_split, 2 * (t - 1))
                tokens = slice(par * P, (par + 1) * P)
                for half in range(2):
                    unit, heads = bass.ds(t - par + half, 1), slice(half * UHEADS, (half + 1) * UHEADS)
                    sp.dma_start(rows[par][:, heads, :], heads_in[unit, :, :].rearrange(
                        "a p (h t) -> (a p) h t", t=CT)[:, :, tokens]).then_inc(rows_in[par], 16)
                    sp.dma_start(scale[par][:, heads, :], inverses[unit, :, tokens].to_broadcast(
                        [P, UHEADS, P])).then_inc(rows_in[par], 16)
                since(sp, finished, t - 1)
                sp.dma_start(x_in[par][:, :], tile_of(x_tiles, t)).then_inc(gate_in[par], 16)
                sp.dma_start(lin_in[par][:, :], tile_of(linear, t)).then_inc(gate_in[par], 16)

            def store(t, par):
                sp.wait_ge(finished, t + 1)
                sp.dma_start(tile_of(out_tiles, t), result[par][:, :]).then_inc(stored[par], 16)

            load(0, 0)
            load(1, 1)
            with sp.Fori(0, COUPLES - 1) as n:
                for par in range(2):
                    load(2 * n + par + 2, par)
                    store(2 * n + par, par)
            for par in range(2):
                store(TILES - 2 + par, par)
            for par in range(2):
                sp.wait_ge(stored[par], 16 * COUPLES)

        @block.tensor
        def _(pe):
            for h in range(HEADS):
                if h % PART == 0:
                    pe.wait_ge(weights_in[h // PART], 32)
                since(pe, merge_split, h - 3)
                pe.matmul(merge_ps[:, h % 4, :], uv[:, h, :], wo[:, h, :], start=True, stop=True).then_inc(merged, 1)
            pe.wait_ge(merge_split, HEADS)

            def couple(n):
                for par in range(2):
                    t = 2 * n + par
                    since(pe, times[par], n)
                    for half in range(2):
                        pe.wait_ge(rows_split, 2 * t + half + 1)
                        for h in range(half * UHEADS, (half + 1) * UHEADS):
                            pe.matmul(sum_ps[:, par, :], rows_h[par][:, h, :], merged_h[:, h, :], start=(h == 0), stop=False)
                            pe.matmul(sum_ps[:, par, :], rows_h[par][:, h, :], merged_l[:, h, :], start=False, stop=False)
                            mm = pe.matmul(sum_ps[:, par, :], rows_l[par][:, h, :], merged_h[:, h, :],
                                           start=False, stop=(h == HEADS - 1))
                    mm.then_inc(projected[par], 1)

            couple(0)
            with pe.Fori(1, COUPLES) as n:
                couple(n)

        @block.scalar
        def _(act):
            for h in range(HEADS):
                act.wait_ge(merged, h + 1)
                nc.scalar.copy(merged_h[:, h, :], merge_ps[:, h % 4, :]).then_inc(merge_high, 1)

            def couple(n):
                for par in range(2):
                    t = 2 * n + par
                    since(act, projected[par], n)
                    for half in range(2):
                        heads = slice(half * UHEADS, (half + 1) * UHEADS)
                        act.wait_ge(scaled, 2 * t + half + 1)
                        nc.scalar.copy(rows_h[par][:, heads, :], rows[par][:, heads, :]).then_inc(rows_high, 1)
                    act.wait_ge(gate_in[par], 32 * (n + 1))
                    since(act, times[par], n)
                    nc.scalar.activation(gate[par][:, :], lin_in[par][:, :], ACT.Sigmoid).then_inc(sigmoid, 1)

            couple(0)
            with act.Fori(1, COUPLES) as n:
                couple(n)

        @block.vector
        def _(dve):
            for h in range(HEADS):
                dve.wait_ge(merge_high, h + 1)
                nc.vector.tensor_tensor(merged_l[:, h, :], merge_ps[:, h % 4, :], merged_h[:, h, :],
                                        ALU.subtract).then_inc(merge_split, 1)

            def scale_rows(t, par, n):
                dve.wait_ge(rows_in[par], 64 * (n + 1))
                for half in range(2):
                    heads = slice(half * UHEADS, (half + 1) * UHEADS)
                    nc.vector.tensor_tensor(rows[par][:, heads, :], rows[par][:, heads, :], scale[par][:, heads, :],
                                            ALU.mult).then_inc(scaled, 1)
                for half in range(2):
                    heads = slice(half * UHEADS, (half + 1) * UHEADS)
                    dve.wait_ge(rows_high, 2 * t + half + 1)
                    nc.vector.tensor_tensor(rows_l[par][:, heads, :], rows[par][:, heads, :], rows_h[par][:, heads, :],
                                            ALU.subtract).then_inc(rows_split, 1)
                dve.wait_ge(sigmoid, t + 1)
                nc.vector.tensor_tensor(gate[par][:, :], gate[par][:, :], lin_in[par][:, :], ALU.mult).then_inc(gated, 1)

            def finish(t, par, n):
                dve.wait_ge(projected[par], n + 1)
                dve.wait_ge(gated, t + 1)
                since(dve, stored[par], 16 * n)
                nc.vector.tensor_tensor(result[par][:, :], sum_ps[:, par, :], gate[par][:, :], ALU.mult).then_inc(times[par], 1)
                dve.wait_ge(times[par], n + 1)
                nc.vector.tensor_tensor(result[par][:, :], result[par][:, :], x_in[par][:, :], ALU.add).then_inc(finished, 1)

            def couple(n):
                scale_rows(2 * n + 1, 1, n)
                finish(2 * n, 0, n)
                scale_rows(2 * n + 2, 0, n + 1)
                finish(2 * n + 1, 1, n)

            scale_rows(0, 0, 0)
            couple(0)
            with dve.Fori(1, COUPLES - 1) as n:
                couple(n)
            scale_rows(TILES - 1, 1, COUPLES - 1)
            finish(TILES - 2, 0, COUPLES - 1)
            finish(TILES - 1, 1, COUPLES - 1)


def program(nc, x, w_all, w_uq, w_uk, w_qr, lora_b, w_uv, w_o, cos, sin, out):
    keys = nc.dram_tensor("keys", [TILES, P, SK], F32, kind="Internal").ap()
    values = nc.dram_tensor("values", [TILES, P, SV], F32, kind="Internal").ap()
    linear = nc.dram_tensor("linear", [TILES, P, DIM], F32, kind="Internal").ap()
    heads_rows = nc.dram_tensor("heads_rows", [UNITS, P, HQ], F32, kind="Internal").ap()
    inverses = nc.dram_tensor("inverses", [UNITS, UHEADS, CT], F32, kind="Internal").ap()
    turned = nc.dram_tensor("turned", [UNITS + 1, 2, P, 1024], F32, kind="Internal").ap()
    with ExitStack() as ctx:
        keep = Persistent(nc, ctx)
        prepare(nc, keep, x, w_all, w_uq, w_uk, w_qr, lora_b, cos, sin, keys, values, linear)
        attend(nc, keep, keys, values, turned, heads_rows, inverses)
    combine(nc, x, w_uv, w_o, heads_rows, inverses, linear, out)


def layout(L0_attn_x, L0_attn_W_DQ, L0_attn_W_UQ, L0_attn_W_QR, L0_attn_W_DKV, L0_attn_W_UK, L0_attn_W_UV,
           L0_attn_W_KR, L0_attn_W_O, L0_ffn_weight, L0_ffn_lora_A, L0_ffn_lora_B, L0_ffn_router_w):
    import numpy as np
    x = L0_attn_x.reshape(SEQ, DIM)
    kr_even, kr_odd = L0_attn_W_KR[0::2], L0_attn_W_KR[1::2]
    w_all = np.concatenate([L0_ffn_weight, L0_ffn_lora_A.reshape(ER, DIM), L0_ffn_router_w, L0_attn_W_DKV,
                            L0_attn_W_DQ, kr_even, kr_odd, kr_odd, kr_even], axis=0).T

    def by_head(w):
        return w.reshape(HEADS, P, LAT).transpose(1, 0, 2).reshape(P, HEADS * LAT)

    w_qr = L0_attn_W_QR.reshape(2, 4, 2, HALF, 2, LAT).transpose(5, 0, 4, 2, 1, 3).reshape(LAT, 2 * GT)
    inv_freq = np.float32(10000.0) ** (-np.arange(0, ROT, 2, dtype=np.float32) / np.float32(ROT))
    angle = np.tile(inv_freq[:, None] * np.arange(SEQ, dtype=np.float32)[None, :], (P // HALF, 1))
    arrays = {
        "x": x, "w_all": w_all, "w_uq": by_head(L0_attn_W_UQ), "w_uk": by_head(L0_attn_W_UK), "w_qr": w_qr,
        "lora_b": L0_ffn_lora_B.transpose(0, 2, 1).reshape(ER, DIM),
        "w_uv": by_head(L0_attn_W_UV), "w_o": L0_attn_W_O.T.reshape(HEADS, P, DIM).transpose(1, 0, 2),
        "cos": np.cos(angle), "sin": np.sin(angle),
    }
    return {name: np.ascontiguousarray(a) for name, a in arrays.items()}


def kernel(**inputs):
    import numpy as np
    import concourse.bacc as bacc
    from concourse.bass_utils import run_bass_kernel_spmd

    nc = bacc.Bacc("TRN2", target_bir_lowering=False, num_devices=1)
    arrays = {f"in_{n}": a for n, a in layout(**{n: np.asarray(a) for n, a in inputs.items()}).items()}
    args = [nc.dram_tensor(n, a.shape, mybir.dt.from_np(a.dtype), kind="ExternalInput").ap() for n, a in arrays.items()]
    args.append(nc.dram_tensor("out", (SEQ, DIM), F32, kind="ExternalOutput").ap())
    program(nc, *args)
    result = run_bass_kernel_spmd(nc, [arrays], core_ids=[0])
    return result.results[0]["out"].reshape(1, SEQ, DIM)
```

```python
from contextlib import ExitStack

import concourse.bass as bass
from concourse import mybir
from concourse.alu_op_type import AluOpType as ALU

ACT = mybir.ActivationFunctionType
AX = mybir.AxisListType
F32 = mybir.dt.float32
F32R = mybir.dt.float32r

P = 128
SEQ = 2048
DIM = 512
KC = DIM // P
TILES = SEQ // P
HEADS = 16
LAT = 128
ROT = 64
HALF = ROT // 2
EXPERTS, RANK = 8, 16
ER = EXPERTS * RANK
LORA_SCALE = 32.0 / RANK
EPS = 1e-5
QK_SCALE = (P + ROT) ** -0.5
CLIP = 80.0
P_MAX = 2.718281828459045 ** (CLIP * QK_SCALE)
P_MIN = 2.718281828459045 ** (-CLIP * QK_SCALE)

GROUP = 4
GROUPS = TILES // GROUP
GT = GROUP * P

C_BASE = 0
C_A = DIM
C_ROUTER = C_A + ER
C_KV = C_ROUTER + EXPERTS
C_Q = C_KV + LAT
C_KR = C_Q + LAT
C_ALL = C_KR + 2 * ROT
SMALL = C_Q - C_A

COUPLES = TILES // 2
CT = 2 * P
UNITS = 2 * COUPLES
UHEADS = HEADS // 2
HQ = UHEADS * CT
HW = HQ // 2
HH = UHEADS // 2
SK = 3 * P
SV = 2 * P


def since(eng, sem, count):
    if not isinstance(count, int) or count > 0:
        eng.wait_ge(sem, count)


def raw(ap):
    return ap.bitcast(F32)


class Persistent:

    def __init__(self, nc, ctx):
        def sb(name, shape, dt):
            return ctx.enter_context(nc.sbuf_tensor(name, shape, dt))

        self.cos = sb("cos", [P, SEQ + CT], F32)
        self.sin = sb("sin", [P, SEQ + CT], F32)
        self.absorb_h = sb("absorb_h", [P, HQ], F32R)
        self.absorb_l = sb("absorb_l", [P, HQ], F32R)
        self.qr_h = sb("qr_h", [P, 2 * GT], F32R)
        self.qr_l = sb("qr_l", [P, 2 * GT], F32R)
        self.cq_h = sb("cq_h", [P, SEQ + CT], F32R)
        self.cq_l = sb("cq_l", [P, SEQ + CT], F32R)
        self.causal = sb("causal", [P, CT], F32)
        self.strip = sb("strip", [P, 2 * UHEADS - 1], F32)


class Top:

    def __init__(self, nc, ctx):
        with ExitStack() as lent:
            self.q_h, self.q_l, self.rot_hh, self.rot_l0 = (
                lent.enter_context(nc.sbuf_tensor(name, [P, HQ], F32R, side="right"))
                for name in ("q_h0", "q_l0", "rot_hh0", "rot_l0"))
            self.total = lent.enter_context(nc.sbuf_tensor("total0", [P, HQ], F32, side="right"))
        self.wo = ctx.enter_context(nc.sbuf_tensor("wo", [P, HEADS, DIM], F32, side="right"))
        self.uv = ctx.enter_context(nc.sbuf_tensor("uv", [P, HEADS, LAT], F32, side="right"))


def prepare(nc, keep, x, w_all, w_uq, w_uk, w_qr, lora_b, cos, sin, keys, values, linear, turned_out):
    ctx = ExitStack()
    with ctx:
        def sb(name, shape, dt=F32):
            return ctx.enter_context(nc.sbuf_tensor(name, shape, dt))

        def ps(name, shape):
            return ctx.enter_context(nc.psum_tensor(name, shape, F32))

        def sem(name):
            return ctx.enter_context(nc.semaphore(name))

        x_all = sb("x_all", [P, TILES, DIM])
        w_stage = sb("w_stage", [P, KC, C_ALL])
        w_h = sb("w_h", [P, KC, C_ALL], F32R)
        w_l = sb("w_l", [P, KC, C_ALL], F32R)
        xn = sb("xn", [P, GROUP, DIM])
        y = sb("y", [P, GROUP, DIM])
        qr_stage = sb("qr_stage", [P, 2 * GT])
        b_stage = sb("b_stage", [P, DIM])
        b_h = sb("b_h", [P, DIM], F32R)
        b_l = sb("b_l", [P, DIM], F32R)
        xt_h = sb("xt_h", [P, KC, GT], F32R)
        xt_l = sb("xt_l", [P, KC, GT], F32R)
        key_out = sb("key_out", [P, GROUP, SK], F32R)
        value_out = sb("value_out", [P, GROUP, SV], F32R)
        small = sb("small", [P, GROUP, ER + EXPERTS])
        turn_h = sb("turn_h", [P, GROUP, P], F32R)
        turn_l = sb("turn_l", [P, GROUP, P], F32R)
        weighted = sb("weighted", [P, GROUP, ER])
        rot_a = sb("rot_a", [P, GT])
        rot_b = sb("rot_b", [P, GT])
        ident = sb("ident", [P, P])
        prod = [w_stage[:, 0, n * 512:(n + 1) * 512] for n in range(2)] + [w_stage[:, 1, n * 512:(n + 1) * 512] for n in range(2)]
        rot_f = w_stage[:, 2, 0:1024].rearrange("p (e n) -> p e n", e=2)
        rot_hl = [x_all[:, 4 * n:4 * n + 4, :].bitcast(F32R).rearrange("p (w e) n -> p w e n", w=2) for n in range(2)]
        stats = sb("stats", [P, TILES, 6])
        moments = sb("moments", [P, TILES, 2])
        deviation = sb("deviation", [P, TILES])
        rstd = sb("rstd", [P, TILES])
        eps = sb("eps", [P, 1])
        order = sb("order", [P, EXPERTS])
        r1 = sb("r1", [P, GROUP])
        rt = [sb(f"rt{n}", [P, GROUP, EXPERTS]) for n in range(5)]
        rw = sb("rw", [P, GROUP, EXPERTS])

        base_ps = ps("base_ps", [P, GROUP, DIM])
        turn_ps = ps("turn_ps", [P, 2, 512])
        work_ps = ps("work_ps", [P, 2, 512])

        x_in = [sem(f"x_in{g}") for g in range(GROUPS)]
        uqk_in, w_in, rest_in = sem("uqk_in"), sem("w_in"), sem("rest_in")
        constants = sem("constants")
        cleared = sem("cleared")
        absorbed = sem("absorbed")
        absorb_high = sem("absorb_high")
        absorb_split = sem("absorb_split")
        high_done = sem("high_done")
        low_done = sem("low_done")
        chain = sem("chain")
        var_done, dev_done = sem("var_done"), sem("dev_done")
        norm_done = sem("norm_done")
        turned = sem("turned")
        turn_high = sem("turn_high")
        turn_used = sem("turn_used")
        worked = sem("worked")
        work_high = sem("work_high")
        work_used = sem("work_used")
        based = sem("based")
        router_x = sem("router_x")
        router_e = sem("router_e")
        router_s = sem("router_s")
        weighted_done = sem("weighted_done")
        linear_done = sem("linear_done")
        y_done = sem("y_done")
        rope_s = sem("rope_s")
        r_scored = sem("r_scored")
        r_read = sem("r_read")
        r_step = sem("r_step")
        turned_stored = sem("turned_stored")
        keys_out, values_out, y_out = sem("keys_out"), sem("values_out"), sem("y_out")

        uq = xn[:, :, :].rearrange("p a n -> p (a n)")
        uk = y[:, :, :].rearrange("p a n -> p (a n)")
        WORK = GROUP + 3
        TURN = 2 * GROUP
        ROUTER = 15
        ROPE = 5
        KEY_STORES = 5

        block = ctx.enter_context(nc.Block())

        @block.sync
        def _(sp):
            sp.dma_start(uq, w_uq).then_inc(uqk_in, 16)
            sp.dma_start(uk, w_uk).then_inc(uqk_in, 16)
            for g in range(GROUPS):
                sp.dma_start(x_all[:, g * GROUP:(g + 1) * GROUP, :],
                             x[g * GT:(g + 1) * GT, :].rearrange("(a p) n -> p a n", p=P)).then_inc(x_in[g], 16)
                if g == 0:
                    sp.dma_start(w_stage[:, :, :], w_all.rearrange("(c p) n -> p c n", p=P)).then_inc(w_in, 16)
            sp.dma_start(qr_stage[:, :], w_qr).then_inc(rest_in, 16)
            sp.dma_start(b_stage[:, :], lora_b).then_inc(rest_in, 16)
            sp.dma_start(keep.cos[:, 0:SEQ], cos).then_inc(rest_in, 16)
            sp.dma_start(keep.sin[:, 0:SEQ], sin).then_inc(rest_in, 16)
            with sp.Fori(0, GROUPS) as g:
                sp.wait_ge(work_used, WORK * g + GROUP)
                sp.dma_start(values[bass.ds(g * GROUP, GROUP), :, :].rearrange("a p n -> p a n"),
                             raw(value_out[:, :, :])).then_inc(values_out, 16)
                sp.wait_ge(rope_s, ROPE * (g + 1))
                out = keys[bass.ds(g * GROUP, GROUP), :, :]
                sp.dma_start(out[:, :, 0:2 * P].rearrange("a p n -> p a n"),
                             raw(key_out[:, :, 0:2 * P])).then_inc(keys_out, 16)
                for n in range(4):
                    rows = out[:, (n // 2) * ROT:(n // 2 + 1) * ROT, 2 * P:SK].rearrange("a (f e) n -> e f a n", e=2)
                    sp.dma_start(rows[n % 2], raw(key_out[n * HALF:(n + 1) * HALF, :, 2 * P:SK])).then_inc(keys_out, 16)
                sp.wait_ge(y_done, GROUP * (g + 1))
                sp.dma_start(linear[bass.ds(g * GROUP, GROUP), :, :].rearrange("a p n -> p a n"),
                             y[:, :, :]).then_inc(y_out, 16)
            for n in range(2):
                sp.wait_ge(r_step, 4 * n + 4)
                sp.dma_start(turned_out[n].rearrange("w p n -> p w n"),
                             raw(rot_hl[n]).rearrange("p w e n -> p w (e n)")).then_inc(turned_stored, 16)
            sp.wait_ge(turned_stored, 32)
            sp.wait_ge(keys_out, 16 * KEY_STORES * GROUPS)
            for s in (values_out, y_out):
                sp.wait_ge(s, 16 * GROUPS)

        @block.gpsimd
        def _(pool):
            nc.gpsimd.memset(ident[:, :], 0.0).then_inc(cleared, 1)
            nc.gpsimd.memset(keep.causal[:, :], 1.0).then_inc(cleared, 1)
            nc.gpsimd.memset(keep.strip[:, :], 0.0).then_inc(cleared, 1)
            nc.gpsimd.memset(eps[:, :], EPS).then_inc(constants, 1)
            for e in range(EXPERTS):
                nc.gpsimd.memset(order[:, e:e + 1], float(EXPERTS - e)).then_inc(constants, 1)
            for t in (keep.cos, keep.sin, raw(keep.cq_h[:, :]), raw(keep.cq_l[:, :])):
                nc.gpsimd.memset(t[:, SEQ:SEQ + CT], 0.0).then_inc(constants, 1)
            pool.wait_ge(cleared, 3)
            nc.gpsimd.affine_select(out=ident[:, :], in_=ident[:, :], compare_op=ALU.not_equal, fill=1.0,
                                    base=0, pattern=[[-1, P]], channel_multiplier=1).then_inc(constants, 1)
            nc.gpsimd.affine_select(out=keep.causal[:, :], in_=keep.causal[:, :], compare_op=ALU.is_ge, fill=0.0,
                                    base=0, pattern=[[1, CT]], channel_multiplier=-1).then_inc(constants, 1)
            nc.gpsimd.memset(keep.strip[:, UHEADS - 1:UHEADS], 1.0).then_inc(constants, 1)

        CONSTANTS = 1 + EXPERTS + 4 + 3

        @block.tensor
        def _(pe):
            pe.wait_ge(uqk_in, 32)
            for h in range(HEADS):
                mm = pe.matmul(base_ps[:, h // 4, (h % 4) * P:(h % 4 + 1) * P], uq[:, h * P:(h + 1) * P],
                               uk[:, h * P:(h + 1) * P], start=True, stop=True)
                if h % 8 == 7:
                    mm.then_inc(absorbed, 1)
            pe.wait_ge(constants, CONSTANTS)

            def turn_x(a, ready, n):
                pe.wait_ge(norm_done, ready + a + 1)
                since(pe, turn_used, n + a - 1)
                for c in range(KC):
                    mm = pe.transpose(turn_ps[:, a % 2, c * P:(c + 1) * P], xn[:, a, c * P:(c + 1) * P], ident[:, :])
                mm.then_inc(turned, 1)

            for a in range(GROUP):
                turn_x(a, 0, 0)

            def rotary(n, banks):
                for m in range(4):
                    w, out = slice((4 * n + m) * P, (4 * n + m + 1) * P), banks[:, m // 2, (m % 2) * CT:(m % 2 + 1) * CT]
                    pe.matmul(out, keep.qr_h[:, w], keep.cq_h[:, 0:CT], start=True, stop=False)
                    pe.matmul(out, keep.qr_h[:, w], keep.cq_l[:, 0:CT], start=False, stop=False)
                    mm = pe.matmul(out, keep.qr_l[:, w], keep.cq_h[:, 0:CT], start=False, stop=True)
                mm.then_inc(r_scored, 1)

            def group(g, last):
                pe.wait_ge(turn_used, TURN * g + GROUP)
                for a in range(GROUP):
                    since(pe, work_used, WORK * g + (a - 1 if a else 0))
                    n = 0
                    for c in range(KC):
                        for xs, ws in ((xt_h, w_h), (xt_l, w_h), (xt_h, w_l)):
                            mm = pe.matmul(work_ps[:, a % 2, 0:SMALL], xs[:, c, a * P:(a + 1) * P],
                                           ws[:, c, C_A:C_Q], start=(n == 0), stop=(n == 3 * KC - 1))
                            n += 1
                    mm.then_inc(worked, 1)
                for k, col in enumerate((C_KV, C_Q, C_KR)):
                    pe.wait_ge(work_used, WORK * g + GROUP + k - 1)
                    n = 0
                    for c in range(KC):
                        for ws, xs in ((w_h, xt_h), (w_l, xt_h), (w_h, xt_l)):
                            mm = pe.matmul(work_ps[:, (GROUP + k) % 2, :], ws[:, c, col:col + P], xs[:, c, :],
                                           start=(n == 0), stop=(n == 3 * KC - 1))
                            n += 1
                    mm.then_inc(worked, 1)
                if last:
                    rotary(0, turn_ps)
                since(pe, y_done, GROUP * g)
                for a in range(GROUP):
                    if last and a == 2:
                        pe.wait_ge(work_used, WORK * GROUPS)
                        rotary(1, work_ps)
                    n = 0
                    for c in range(KC):
                        for xs, ws in ((xt_h, w_h), (xt_l, w_h), (xt_h, w_l)):
                            mm = pe.matmul(base_ps[:, a, :], xs[:, c, a * P:(a + 1) * P], ws[:, c, 0:DIM],
                                           start=(n == 0), stop=False)
                            n += 1
                mm.then_inc(based, 1)
                if not last:
                    for a in range(GROUP):
                        turn_x(a, GROUP * (g + 1), TURN * g + GROUP)
                pe.wait_ge(weighted_done, g + 1)
                if last:
                    pe.wait_ge(r_read, 4)
                n0 = TURN * g + (GROUP if last else 2 * GROUP)
                for a in range(GROUP):
                    pe.wait_ge(turn_used, n0 + a - 1)
                    pe.transpose(turn_ps[:, a % 2, 0:P], weighted[:, a, :], ident[:, :]).then_inc(turned, 1)
                for a in range(GROUP):
                    pe.wait_ge(turn_used, n0 + a + 1)
                    pe.matmul(base_ps[:, a, :], turn_h[:, a, :], b_h[:, :], start=False, stop=False)
                    pe.matmul(base_ps[:, a, :], turn_l[:, a, :], b_h[:, :], start=False, stop=False)
                    pe.matmul(base_ps[:, a, :], turn_h[:, a, :], b_l[:, :], start=False,
                              stop=True).then_inc(linear_done, 1)

            pe.wait_ge(absorb_split, 2)
            pe.wait_ge(low_done, 3)
            group(0, False)
            with pe.Fori(1, GROUPS - 1) as g:
                group(g, False)
            group(GROUPS - 1, True)

        @block.scalar
        def _(act):
            for half in range(2):
                act.wait_ge(absorbed, half + 1)
                nc.scalar.copy(keep.absorb_h[:, half * HW:(half + 1) * HW],
                               base_ps[:, 2 * half:2 * half + 2, :]).then_inc(absorb_high, 1)
            act.wait_ge(w_in, 16)
            nc.scalar.copy(w_h[:, :, :], w_stage[:, :, :]).then_inc(high_done, 1)
            act.wait_ge(rest_in, 64)
            nc.scalar.copy(keep.qr_h[:, :], qr_stage[:, :]).then_inc(high_done, 1)
            nc.scalar.copy(b_h[:, :], b_stage[:, :]).then_inc(high_done, 1)
            act.wait_ge(var_done, 1)
            act.wait_ge(constants, 1)
            nc.scalar.activation(deviation[:, :], moments[:, :, 1], ACT.Sqrt, bias=eps[:, 0:1]).then_inc(dev_done, 1)

            def turn_x(a, n):
                act.wait_ge(turned, n + a + 1)
                nc.scalar.copy(xt_h[:, :, a * P:(a + 1) * P],
                               turn_ps[:, a % 2, :].rearrange("p (c t) -> p c t", c=KC)).then_inc(turn_high, 1)

            for a in range(GROUP):
                turn_x(a, 0)

            def group(g, last):
                since(act, values_out, 16 * g)
                for a in range(GROUP):
                    act.wait_ge(worked, WORK * g + a + 1)
                    nc.scalar.copy(value_out[:, a, 0:P], work_ps[:, a % 2, C_KV - C_A:SMALL]).then_inc(work_high, 1)
                act.wait_ge(router_x, g + 1)
                nc.scalar.activation(rt[1][:, :, :], rt[0][:, :, :], ACT.Exp).then_inc(router_e, 1)
                since(act, keys_out, 16 * KEY_STORES * g)
                act.wait_ge(worked, WORK * g + GROUP + 1)
                nc.scalar.copy(key_out[:, :, 0:P],
                               work_ps[:, 0, :].rearrange("p (a t) -> p a t", a=GROUP)).then_inc(work_high, 1)
                act.wait_ge(worked, WORK * g + GROUP + 2)
                nc.scalar.copy(keep.cq_h[:, bass.ds(g * GT, GT)], work_ps[:, 1, :]).then_inc(work_high, 1)
                if not last:
                    act.wait_ge(based, g + 1)
                    for a in range(GROUP):
                        turn_x(a, TURN * g + GROUP)
                n0 = TURN * g + (GROUP if last else 2 * GROUP)
                for a in range(GROUP):
                    act.wait_ge(turned, n0 + a + 1)
                    nc.scalar.copy(turn_h[:, a, :], turn_ps[:, a % 2, 0:P]).then_inc(turn_high, 1)
                since(act, y_out, 16 * g)
                for a in range(GROUP):
                    act.wait_ge(linear_done, GROUP * g + a + 1)
                    nc.scalar.copy(y[:, a, :], base_ps[:, a, :]).then_inc(y_done, 1)

            group(0, False)
            with act.Fori(1, GROUPS - 1) as g:
                group(g, False)
            group(GROUPS - 1, True)

        @block.vector
        def _(dve):
            for half in range(2):
                dve.wait_ge(absorb_high, half + 1)
                cols = slice(half * HW, (half + 1) * HW)
                nc.vector.tensor_tensor(keep.absorb_l[:, cols], base_ps[:, 2 * half:2 * half + 2, :].rearrange("p b n -> p (b n)"),
                                        keep.absorb_h[:, cols], ALU.subtract).then_inc(absorb_split, 1)
            for t in range(TILES):
                if t % GROUP == 0:
                    dve.wait_ge(x_in[t // GROUP], 16)
                nc.vector.bn_stats(stats[:, t, :], x_all[:, t, :]).then_inc(chain, 1)
            for t in range(TILES):
                dve.wait_ge(chain, t + 1)
                ins = nc.vector.bn_aggr(moments[:, t, :], stats[:, t, :])
            ins.then_inc(var_done, 1)
            dve.wait_ge(high_done, 1)
            nc.vector.tensor_tensor(w_l[:, :, :], w_stage[:, :, :], w_h[:, :, :], ALU.subtract).then_inc(low_done, 1)
            dve.wait_ge(high_done, 3)
            nc.vector.tensor_tensor(keep.qr_l[:, :], qr_stage[:, :], keep.qr_h[:, :], ALU.subtract).then_inc(low_done, 1)
            nc.vector.tensor_tensor(b_l[:, :], b_stage[:, :], b_h[:, :], ALU.subtract).then_inc(low_done, 1)
            dve.wait_ge(dev_done, 1)
            nc.vector.reciprocal(rstd[:, :], deviation[:, :]).then_inc(chain, 1)
            dve.wait_ge(chain, TILES + 1)

            def normalise(g, a):
                t = g * GROUP + a
                nc.vector.tensor_scalar(xn[:, a, :], x_all[:, bass.ds(t, 1), :].rearrange("p a n -> p (a n)"),
                                        moments[:, bass.ds(t, 1), 0], rstd[:, bass.ds(t, 1)],
                                        ALU.subtract, ALU.mult).then_inc(norm_done, 1)

            def turn_x(a, n):
                dve.wait_ge(turn_high, n + a + 1)
                cols = slice(a * P, (a + 1) * P)
                nc.vector.tensor_tensor(xt_l[:, :, cols], turn_ps[:, a % 2, :].rearrange("p (c t) -> p c t", c=KC),
                                        xt_h[:, :, cols], ALU.subtract).then_inc(turn_used, 1)

            for a in range(GROUP):
                normalise(0, a)
            for a in range(GROUP):
                turn_x(a, 0)
            dve.wait_ge(constants, CONSTANTS)

            def group(g, last):
                for a in range(GROUP):
                    dve.wait_ge(work_high, (WORK - 1) * g + a + 1)
                    nc.vector.tensor_copy(small[:, a, :], work_ps[:, a % 2, 0:ER + EXPERTS])
                    nc.vector.tensor_tensor(value_out[:, a, P:SV], work_ps[:, a % 2, C_KV - C_A:SMALL],
                                            value_out[:, a, 0:P], ALU.subtract).then_inc(work_used, 1)
                shape = [P, GROUP, EXPERTS]
                logits = small[:, :, ER:ER + EXPERTS]
                ranks = order[:, :].unsqueeze(1).to_broadcast(shape)
                most = r1[:, :].unsqueeze(2).to_broadcast(shape)
                key, expo, first, second, rest = rt[0], rt[1], rt[2], rt[3], rt[4]
                step = [0]

                def then(ins):
                    step[0] += 1
                    ins.then_inc(router_s, 1)
                    dve.wait_ge(router_s, ROUTER * g + step[0])

                dve.wait_ge(work_used, WORK * g + GROUP)
                then(nc.vector.tensor_reduce(r1[:, :], logits, AX.X, ALU.max))
                nc.vector.tensor_tensor(rt[0][:, :, :], logits, most, ALU.subtract).then_inc(router_x, 1)
                then(nc.vector.tensor_tensor(first[:, :, :], logits, most, ALU.is_equal))
                then(nc.vector.tensor_tensor(second[:, :, :], first[:, :, :], ranks, ALU.mult))
                then(nc.vector.tensor_reduce(r1[:, :], second[:, :, :], AX.X, ALU.max))
                then(nc.vector.tensor_tensor(first[:, :, :], second[:, :, :], most, ALU.is_equal))
                then(nc.vector.scalar_tensor_tensor(out=rest[:, :, :], in0=first[:, :, :], scalar=-3.0e38, in1=logits,
                                                    op0=ALU.mult, op1=ALU.add))
                then(nc.vector.tensor_reduce(r1[:, :], rest[:, :, :], AX.X, ALU.max))
                then(nc.vector.tensor_tensor(second[:, :, :], rest[:, :, :], most, ALU.is_equal))
                then(nc.vector.tensor_tensor(rest[:, :, :], second[:, :, :], ranks, ALU.mult))
                then(nc.vector.tensor_reduce(r1[:, :], rest[:, :, :], AX.X, ALU.max))
                then(nc.vector.tensor_tensor(second[:, :, :], rest[:, :, :], most, ALU.is_equal))
                then(nc.vector.tensor_tensor(rest[:, :, :], first[:, :, :], second[:, :, :], ALU.add))
                dve.wait_ge(router_e, g + 1)
                then(nc.vector.tensor_tensor(rest[:, :, :], rest[:, :, :], expo[:, :, :], ALU.mult))
                then(nc.vector.tensor_reduce(r1[:, :], rest[:, :, :], AX.X, ALU.add))
                then(nc.vector.reciprocal(r1[:, :], r1[:, :]))
                nc.vector.scalar_tensor_tensor(out=rw[:, :, :], in0=rest[:, :, :], scalar=LORA_SCALE, in1=most,
                                               op0=ALU.mult, op1=ALU.mult).then_inc(chain, 1)
                dve.wait_ge(chain, g + TILES + 2)
                nc.vector.tensor_tensor(
                    weighted[:, :, :].rearrange("p a (e r) -> p (a e) r", r=RANK),
                    small[:, :, 0:ER].rearrange("p a (e r) -> p a e r", r=RANK),
                    rw[:, :, :].rearrange("p a e -> p (a e)").unsqueeze(2).to_broadcast([P, GROUP * EXPERTS, RANK]),
                    ALU.mult).then_inc(weighted_done, 1)
                assert step[0] == ROUTER

                dve.wait_ge(work_high, (WORK - 1) * g + GROUP + 1)
                nc.vector.tensor_tensor(key_out[:, :, P:2 * P], work_ps[:, 0, :].rearrange("p (a t) -> p a t", a=GROUP),
                                        key_out[:, :, 0:P], ALU.subtract).then_inc(work_used, 1)
                dve.wait_ge(work_high, (WORK - 1) * g + GROUP + 2)
                nc.vector.tensor_tensor(keep.cq_l[:, bass.ds(g * GT, GT)], work_ps[:, 1, :],
                                        keep.cq_h[:, bass.ds(g * GT, GT)], ALU.subtract).then_inc(work_used, 1)
                dve.wait_ge(worked, WORK * g + WORK)
                nc.vector.tensor_tensor(rot_a[0:ROT, :], work_ps[0:ROT, 0, :], keep.cos[0:ROT, bass.ds(g * GT, GT)],
                                        ALU.mult).then_inc(rope_s, 1)
                nc.vector.tensor_tensor(rot_b[0:ROT, :], work_ps[ROT:P, 0, :], keep.sin[ROT:P, bass.ds(g * GT, GT)],
                                        ALU.mult).then_inc(work_used, 1)
                dve.wait_ge(work_used, WORK * (g + 1))
                nc.vector.tensor_tensor(rot_a[0:HALF, :], rot_a[0:HALF, :], rot_b[0:HALF, :],
                                        ALU.subtract).then_inc(rope_s, 1)
                nc.vector.tensor_tensor(rot_a[HALF:ROT, :], rot_a[HALF:ROT, :], rot_b[HALF:ROT, :],
                                        ALU.add).then_inc(rope_s, 1)
                dve.wait_ge(rope_s, ROPE * g + 3)
                turned_keys = rot_a[0:ROT, :].rearrange("p (a t) -> p a t", a=GROUP)
                nc.vector.tensor_copy(key_out[0:ROT, :, 2 * P:SK], turned_keys).then_inc(rope_s, 1)
                dve.wait_ge(rope_s, ROPE * g + 4)
                nc.vector.tensor_tensor(key_out[ROT:P, :, 2 * P:SK], turned_keys, key_out[0:ROT, :, 2 * P:SK],
                                        ALU.subtract).then_inc(rope_s, 1)

                if not last:
                    for a in range(GROUP):
                        normalise(g + 1, a)
                    for a in range(GROUP):
                        turn_x(a, TURN * g + GROUP)
                if last:
                    turn_queries(0, turn_ps)
                n0 = TURN * g + (GROUP if last else 2 * GROUP)
                for a in range(GROUP):
                    dve.wait_ge(turn_high, n0 + a + 1)
                    nc.vector.tensor_tensor(turn_l[:, a, :], turn_ps[:, a % 2, 0:P], turn_h[:, a, :],
                                            ALU.subtract).then_inc(turn_used, 1)

            def turn_queries(n, banks):
                dve.wait_ge(r_scored, n + 1)
                cos, sin = (w[:, 0:CT].unsqueeze(1).to_broadcast([P, 2, CT]) for w in (keep.cos, keep.sin))
                even, odd = (banks[:, eo, :].rearrange("p (g t) -> p g t", g=2) for eo in range(2))
                for out, rows, angle in zip(prod, (even, odd, even, odd), (cos, sin, sin, cos)):
                    nc.vector.tensor_tensor(out.rearrange("p (g t) -> p g t", g=2), rows, angle, ALU.mult).then_inc(r_read, 1)
                dve.wait_ge(r_read, 4 * n + 4)
                nc.vector.tensor_tensor(rot_f[:, 0, :], prod[0], prod[1], ALU.subtract).then_inc(r_step, 1)
                nc.vector.tensor_tensor(rot_f[:, 1, :], prod[2], prod[3], ALU.add).then_inc(r_step, 1)
                dve.wait_ge(r_step, 4 * n + 2)
                nc.vector.tensor_copy(rot_hl[n][:, 0, :, :], rot_f[:, :, :]).then_inc(r_step, 1)
                dve.wait_ge(r_step, 4 * n + 3)
                nc.vector.tensor_tensor(rot_hl[n][:, 1, :, :], rot_f[:, :, :], rot_hl[n][:, 0, :, :],
                                        ALU.subtract).then_inc(r_step, 1)

            group(0, False)
            with dve.Fori(1, GROUPS - 1) as g:
                group(g, False)
            group(GROUPS - 1, True)
            turn_queries(1, work_ps)


FULL, CORNER, LATE = range(3)


class Unit:

    def __init__(self, couple, par, added):
        self.couple, self.par = couple, par
        self.added = added
        self.n = 2 * couple + par
        last = isinstance(couple, int) and couple == COUPLES - 1
        self.has_next = not (last and par == 1)
        self.has_second = not last
        self.next_couple = couple + par


def sweep(eng, pair):

    def two(t, unit, k, prev):
        pair(t, unit, k, 0, FULL, prev)
        pair(t + 1, unit, k + 1, 1, FULL, FULL)

    def units(m, before, added, prev):
        for par in range(2):
            unit = Unit(m, par, added + par * (4 * m + 2))
            t = before + par * (2 * m + 2)
            pair(t, unit, 2 * m, 0, CORNER, prev)
            pair(t + 1, unit, 2 * m + 1, 1, LATE, CORNER)
            prev = LATE
            if not (isinstance(m, int) and m == 0):
                two(t + 2, unit, 0, LATE)
                prev = FULL
                if not (isinstance(m, int) and m == 1):
                    with eng.Fori(1, m) as n:
                        two(t + 2 + 2 * n, unit, 2 * n, FULL)

    units(0, 0, 0, None)
    units(1, 4, 4, LATE)
    done, adds = eng.alloc_register("pairs_done"), eng.alloc_register("adds_done")
    eng.reg_mov(done, 12)
    eng.reg_mov(adds, 16)
    with eng.Fori(2, COUPLES - 1) as m:
        units(m, eng.snap(done, min_val=12, max_val=PAIRS), eng.snap(adds, min_val=16, max_val=2 * PAIRS), FULL)
        eng.reg_add(done, done, 4 * m + 4)
        eng.reg_add(adds, adds, 8 * m + 4)
    before = PAIRS - 4 * COUPLES
    units(COUPLES - 1, before, 2 * before - 2 * (UNITS - 2), FULL)


PAIRS = 2 * COUPLES * (COUPLES + 1)
SPREADS = 3


def attend(nc, keep, top, keys, values, turned, w_uv, w_o, heads_out, sums_out):
    ctx = ExitStack()
    with ctx:
        def sb(name, shape, dt=F32):
            return ctx.enter_context(nc.sbuf_tensor(name, shape, dt))

        def sem(name):
            return ctx.enter_context(nc.semaphore(name))

        key_slot = [sb(f"key_slot{n}", [P, SK], F32R) for n in range(2)]
        value_slot = [sb(f"value_slot{n}", [P, SV], F32R) for n in range(2)]
        q_h = [top.q_h, sb("q_h1", [P, HQ], F32R)]
        q_l = [top.q_l, sb("q_l1", [P, HQ], F32R)]
        rot_hh = [top.rot_hh, sb("rot_hh1", [P, HQ], F32R)]
        rot_l0 = [top.rot_l0, sb("rot_l01", [P, HQ], F32R)]
        prob = [sb(f"prob{n}", [P, HW]) for n in range(2)]
        prob_h = [sb(f"prob_h{n}", [P, HW], F32R) for n in range(2)]
        prob_l = [sb(f"prob_l{n}", [P, HW], F32R) for n in range(2)]
        total = [top.total, sb("total1", [P, HQ])]
        head_rows = sb("head_rows", [P, HQ])
        prod = [sb(f"prod{n}", [P, 512]) for n in range(4)]
        rot_f = sb("rot_f", [P, 2, 512])
        rot_hl = sb("rot_hl", [P, 2, 2, 512], F32R)
        sums = sb("sums", [UHEADS, CT])

        score_ps = ctx.enter_context(nc.psum_tensor("score_ps", [P, 2, HW], F32))
        out_ps = ctx.enter_context(nc.psum_tensor("out_ps", [P, 4, 512], F32))

        zeroed = sem("zeroed")
        keys_in, values_in = sem("keys_in"), sem("values_in")
        scored = sem("scored")
        exp_done = sem("exp_done")
        bounded = sem("bounded")
        clipped = sem("clipped")
        high_done = sem("high_done")
        begun = sem("begun")
        summed = sem("summed")
        split = sem("split")
        weighed = sem("weighed")
        out_read = sem("out_read")
        q_scored = sem("q_scored")
        q_high = sem("q_high")
        q_split = sem("q_split")
        r_scored = sem("r_scored")
        r_read = sem("r_read")
        r_step = sem("r_step")
        passed = sem("passed")
        scattered = sem("scattered")
        first_scattered = sem("first_scattered")
        summed_up = sem("summed_up")
        sums_read = sem("sums_read")
        weights_in = sem("weights_in")
        heads_stored, sums_stored = sem("heads_stored"), sem("sums_stored")

        block = ctx.enter_context(nc.Block())

        def one_of(ap, n):
            return ap[bass.ds(n, 1), :, :].rearrange("a p n -> (a p) n")

        def gather(eng, n, par, signal):
            mine = turned[bass.ds(n, 1), :, :, :]
            for to, rows, part in ((rot_hh, 0, 0), (rot_hh, ROT, 0), (rot_l0, 0, 1)):
                eng.dma_start(raw(to[par][rows:rows + ROT, :]).rearrange("r (q n) -> r q n", q=4),
                               mine[:, part, :, :].rearrange("a (q f) (e n) -> (f e) (a q) n", q=4, e=2)).then_inc(signal, 16)

        @block.sync
        def _(sp):
            loads_before = sp.alloc_register("loads_before")

            def pair(t, unit, k, slot, kind, prev):
                loaded = 16 * t
                if not isinstance(t, int):
                    sp.reg_mov(loads_before, loaded)
                    loaded = sp.snap(loads_before, min_val=0, max_val=16 * PAIRS)
                since(sp, scored, 2 * (t - 1))
                since(sp, keys_in, loaded)
                sp.dma_start(raw(key_slot[slot][:, :]), one_of(keys, k)).then_inc(keys_in, 16)
                since(sp, weighed, 2 * (t - 1))
                since(sp, values_in, loaded)
                sp.dma_start(raw(value_slot[slot][:, :]), one_of(values, k)).then_inc(values_in, 16)

            sweep(sp, pair)
            sp.wait_ge(heads_stored, 16 * UNITS)
            sp.wait_ge(sums_stored, 16 * UNITS)
            sp.wait_ge(weights_in, 32)

        @block.gpsimd
        def _(pool):
            def store(n):
                pool.wait_ge(out_read, 2 * n + 2)
                pool.dma_start(one_of(heads_out, n), head_rows[:, :]).then_inc(heads_stored, 16)
                pool.wait_ge(sums_read, n + 1)
                pool.dma_start(one_of(sums_out, n), sums[:, :]).then_inc(sums_stored, 16)

            queries = pool.alloc_register("queries")
            pool.reg_mov(queries, 3)

            def during(n, par, first=False, has_next=True, has_second=True):
                if has_next:
                    since(pool, passed, 16 * n)
                    pool.wait_ge(q_scored, queries)
                    pool.reg_add(queries, queries, 2)
                    gather(pool, n + 1, 1 - par, scattered)
                if not first:
                    store(n - 1)
                if has_second:
                    pool.wait_ge(r_step, 4 * n + 4)
                    pool.dma_start(turned[bass.ds(n + 2, 1), :, :, :].rearrange("a w p n -> p (a w) n"),
                                   raw(rot_hl[:, :, :, :]).rearrange("p w e n -> p w (e n)")).then_inc(passed, 16)

            during(0, 0, first=True)
            during(1, 1)
            with pool.Fori(1, COUPLES - 1) as m:
                for par in range(2):
                    during(2 * m + par, par)
            during(UNITS - 2, 0, has_second=False)
            pool.wait_ge(scored, 2 * (PAIRS - 2 * COUPLES) + 1)
            pool.dma_start(top.wo[:, :, :], w_o).then_inc(weights_in, 16)
            during(UNITS - 1, 1, has_next=False, has_second=False)
            pool.wait_ge(summed_up, UNITS - 1)
            pool.dma_start(top.uv[:, :, :], w_uv.rearrange("p (h l) -> p h l", h=HEADS)).then_inc(weights_in, 16)
            store(UNITS - 1)

        @block.tensor
        def _(pe):
            def latent(couple, heads, half):
                tokens = bass.ds(couple * CT, CT)
                for h in range(HH):
                    head = heads * UHEADS + half * HH + h
                    w, out = slice(head * P, (head + 1) * P), score_ps[:, half, h * CT:(h + 1) * CT]
                    pe.matmul(out, keep.absorb_h[:, w], keep.cq_h[:, tokens], start=True, stop=False)
                    pe.matmul(out, keep.absorb_h[:, w], keep.cq_l[:, tokens], start=False, stop=False)
                    mm = pe.matmul(out, keep.absorb_l[:, w], keep.cq_h[:, tokens], start=False, stop=True)
                mm.then_inc(q_scored, 1)

            def rotary(couple, heads):
                tokens = bass.ds(couple * CT, CT)
                for n in range(4):
                    w = slice((4 * heads + n) * P, (4 * heads + n + 1) * P)
                    out = score_ps[:, n // 2, 512 + (n % 2) * CT:512 + (n % 2 + 1) * CT]
                    pe.matmul(out, keep.qr_h[:, w], keep.cq_h[:, tokens], start=True, stop=False)
                    pe.matmul(out, keep.qr_h[:, w], keep.cq_l[:, tokens], start=False, stop=False)
                    mm = pe.matmul(out, keep.qr_l[:, w], keep.cq_h[:, tokens], start=False, stop=True)
                mm.then_inc(r_scored, 1)

            def sum_up(par, out):
                for h in range(UHEADS):
                    mm = pe.matmul(out, keep.strip[:, UHEADS - 1 - h:2 * UHEADS - 1 - h],
                                   total[par][:, h * CT:(h + 1) * CT], start=(h == 0), stop=(h == UHEADS - 1))
                mm.then_inc(summed_up, 1)

            def scores(half, par, slot, kind):
                key_high, key_low, key_rot = (key_slot[slot][:, n * P:(n + 1) * P] for n in range(3))

                def columns(buffer, c):
                    if kind == LATE:
                        heads = buffer[:, :].rearrange("p (h t) -> p h t", t=CT)
                        return heads[:, half * HH:(half + 1) * HH, P:CT]
                    return buffer[:, half * HW + c * 512:half * HW + (c + 1) * 512]

                for c in range(1 if kind == LATE else 2):
                    out = score_ps[:, half, c * 512:(c + 1) * 512]
                    pe.matmul(out, key_high, columns(q_h[par], c), start=True, stop=False)
                    pe.matmul(out, key_high, columns(q_l[par], c), start=False, stop=False)
                    pe.matmul(out, key_low, columns(q_h[par], c), start=False, stop=False)
                    pe.matmul(out, key_rot, columns(rot_hh[par], c), start=False, stop=False)
                    mm = pe.matmul(out, key_rot, columns(rot_l0[par], c), start=False, stop=True)
                mm.then_inc(scored, 1)

            def weigh(t, half, slot, kind, last):
                pe.wait_ge(split, 2 * t + half + 1)
                high, low = value_slot[slot][:, 0:P], value_slot[slot][:, P:SV]
                first = kind == CORNER
                for c in range(2):
                    out = out_ps[:, 2 * half + c, :]
                    cols = slice(c * 512, (c + 1) * 512)
                    p_h, p_l = prob_h[half][:, cols], prob_l[half][:, cols]
                    if kind == LATE:
                        out = out.rearrange("p (h t) -> p h t", t=CT)[:, :, P:CT]
                        cols = slice(c * 256, (c + 1) * 256)
                        p_h, p_l = (p[half][:, cols].rearrange("p (h t) -> p h t", t=P) for p in (prob_h, prob_l))
                    pe.matmul(out, high, p_h, start=first, stop=False)
                    pe.matmul(out, high, p_l, start=False, stop=False)
                    mm = pe.matmul(out, low, p_h, start=False, stop=last)
                mm.then_inc(weighed, 1)

            def pair(t, unit, k, slot, kind, prev):
                n, par = unit.n, unit.par
                pe.wait_ge(keys_in, 16 * (t + 1))
                if kind == CORNER:
                    pe.wait_ge(q_split, 2 * n + 2)
                    pe.wait_ge(first_scattered, 16 * SPREADS)
                    since(pe, scattered, 16 * SPREADS * n)
                    if prev == LATE:
                        since(pe, r_read, 4 * n)
                if kind == LATE and unit.has_next:
                    pe.wait_ge(q_split, 2 * n + 3)
                if kind == FULL and prev == LATE and unit.has_second:
                    pe.wait_ge(r_read, 4 * n + 4)
                since(pe, exp_done, 2 * t - 1)
                scores(0, par, slot, kind)
                if prev is not None:
                    pe.wait_ge(values_in, 16 * t)
                    if prev == CORNER:
                        since(pe, sums_read, n)
                    weigh(t - 1, 0, 1 - slot, prev, kind == CORNER)
                if kind == LATE and unit.has_next:
                    pe.wait_ge(q_split, 2 * n + 4)
                since(pe, exp_done, 2 * t)
                scores(1, par, slot, kind)
                if prev is not None:
                    if prev == CORNER:
                        since(pe, out_read, 2 * n)
                    weigh(t - 1, 1, 1 - slot, prev, kind == CORNER)
                if kind == CORNER:
                    if unit.has_next:
                        for half in range(2):
                            pe.wait_ge(exp_done, 2 * t + 1 + half)
                            latent(unit.next_couple, 1 - par, half)
                    if prev is not None:
                        pe.wait_ge(summed, unit.added)
                        pe.wait_ge(out_read, 2 * n - 1)
                        sum_up(1 - par, out_ps[0:UHEADS, 0, 0:CT])
                    if unit.has_second:
                        pe.wait_ge(q_split, 2 * n + 4)
                        rotary(unit.couple + 1, par)

            latent(0, 0, 0)
            latent(0, 0, 1)
            pe.wait_ge(zeroed, 2)
            sweep(pe, pair)
            pe.wait_ge(values_in, 16 * PAIRS)
            for half in range(2):
                weigh(PAIRS - 1, half, 1, FULL, True)
            pe.wait_ge(exp_done, 2 * PAIRS)
            pe.wait_ge(summed, 2 * (PAIRS - UNITS))
            sum_up(1, score_ps[0:UHEADS, 0, 0:CT])

        @block.scalar
        def _(act):
            def latent_high(unit, par, half):
                act.wait_ge(q_scored, 2 * unit + half + 1)
                nc.scalar.copy(q_h[par][:, half * HW:(half + 1) * HW], score_ps[:, half, :]).then_inc(q_high, 1)

            def read_out(unit, half):
                if half == 0:
                    since(act, heads_stored, 16 * unit)
                nc.scalar.copy(head_rows[:, half * HW:(half + 1) * HW],
                               out_ps[:, 2 * half:2 * half + 2, :]).then_inc(out_read, 1)

            def read_sums(n, bank):
                act.wait_ge(summed_up, n + 1)
                since(act, sums_stored, 16 * n)
                nc.scalar.copy(sums[:, :], bank[0:UHEADS, 0:CT]).then_inc(sums_read, 1)

            def pair(t, unit, k, slot, kind, prev):
                n, par = unit.n, unit.par
                width = HW // 2 if kind == LATE else HW

                def exponential(half):
                    act.wait_ge(scored, 2 * t + half + 1)
                    since(act, split, 2 * t + half - 1)
                    if kind == LATE:
                        act.wait_ge(begun, 2 * n + half + 1)
                    nc.scalar.activation(prob[half][:, 0:width], score_ps[:, half, 0:width], ACT.Exp,
                                         scale=QK_SCALE).then_inc(exp_done, 1)

                def high(half):
                    act.wait_ge(clipped, 2 * t + half + 1)
                    since(act, weighed, 2 * t + half - 1)
                    nc.scalar.copy(prob_h[half][:, 0:width], prob[half][:, 0:width]).then_inc(high_done, 1)

                def begin(half):
                    since(act, summed_up, n - 1)
                    act.wait_ge(clipped, 2 * t + half + 1)
                    nc.scalar.copy(total[par][:, half * HW:(half + 1) * HW], prob[half][:, :]).then_inc(begun, 1)

                if kind != CORNER:
                    for half in range(2):
                        exponential(half)
                        high(half)
                    return
                exponential(0)
                if prev is not None:
                    act.wait_ge(weighed, 2 * t - 1)
                    read_out(n - 1, 0)
                high(0)
                exponential(1)
                begin(0)
                high(1)
                if unit.has_next:
                    latent_high(n + 1, 1 - par, 0)
                    latent_high(n + 1, 1 - par, 1)
                if prev is not None:
                    act.wait_ge(weighed, 2 * t)
                    read_out(n - 1, 1)
                begin(1)
                if prev is not None:
                    read_sums(n - 1, out_ps[:, 0, :])

            gather(act, 0, 0, first_scattered)
            for half in range(2):
                latent_high(0, 0, half)
            sweep(act, pair)
            for half in range(2):
                act.wait_ge(weighed, 2 * PAIRS - 1 + half)
                read_out(UNITS - 1, half)
            read_sums(UNITS - 1, score_ps[:, 0, :])

        @block.vector
        def _(dve):
            def latent_low(unit, par, half):
                dve.wait_ge(q_high, 2 * unit + half + 1)
                cols = slice(half * HW, (half + 1) * HW)
                nc.vector.tensor_tensor(q_l[par][:, cols], score_ps[:, half, :], q_h[par][:, cols],
                                        ALU.subtract).then_inc(q_split, 1)

            def turn(n, couple):
                dve.wait_ge(r_scored, n + 1)
                tokens = bass.ds(couple * CT, CT)
                cos, sin = (w[:, tokens].unsqueeze(1).to_broadcast([P, 2, CT]) for w in (keep.cos, keep.sin))
                even, odd = (score_ps[:, eo, 512:1024].rearrange("p (g t) -> p g t", g=2) for eo in range(2))
                for out, rows, angle in zip(prod, (even, odd, even, odd), (cos, sin, sin, cos)):
                    nc.vector.tensor_tensor(out[:, :].rearrange("p (g t) -> p g t", g=2), rows, angle,
                                            ALU.mult).then_inc(r_read, 1)

            def turned_split(n):
                dve.wait_ge(r_read, 4 * n + 4)
                nc.vector.tensor_tensor(rot_f[:, 0, :], prod[0][:, :], prod[1][:, :], ALU.subtract).then_inc(r_step, 1)
                nc.vector.tensor_tensor(rot_f[:, 1, :], prod[2][:, :], prod[3][:, :], ALU.add).then_inc(r_step, 1)
                since(dve, passed, 16 * n)
                dve.wait_ge(r_step, 4 * n + 2)
                nc.vector.tensor_copy(rot_hl[:, 0, :, :], rot_f[:, :, :]).then_inc(r_step, 1)
                dve.wait_ge(r_step, 4 * n + 3)
                nc.vector.tensor_tensor(rot_hl[:, 1, :, :], rot_f[:, :, :], rot_hl[:, 0, :, :],
                                        ALU.subtract).then_inc(r_step, 1)

            def pair(t, unit, k, slot, kind, prev):
                n, par = unit.n, unit.par
                tokens = P if kind == LATE else CT
                for half in range(2):
                    s = 2 * t + half
                    p, p_h, p_l = (b[half][:, 0:HH * tokens] for b in (prob, prob_h, prob_l))
                    dve.wait_ge(exp_done, s + 1)
                    if kind == FULL:
                        nc.vector.tensor_scalar(p, p, P_MIN, P_MAX, ALU.max, ALU.min).then_inc(clipped, 1)
                    else:
                        nc.vector.tensor_scalar(p, p, P_MIN, P_MAX, ALU.max, ALU.min).then_inc(bounded, 1)
                        dve.wait_ge(bounded, 4 * n + (2 if kind == LATE else 0) + half + 1)
                        masked = p.rearrange("p (h t) -> p h t", t=tokens)[:, :, 0:P]
                        nc.vector.tensor_tensor(masked, masked, keep.causal[:, 0:P].unsqueeze(1).to_broadcast([P, HH, P]),
                                                ALU.mult).then_inc(clipped, 1)
                    if kind != CORNER:
                        sums = total[par][:, half * HW:(half + 1) * HW].rearrange("p (h t) -> p h t", t=CT)[:, :, CT - tokens:CT]
                        dve.wait_ge(clipped, s + 1)
                        dve.wait_ge(begun, 2 * n + half + 1)
                        if kind == FULL:
                            dve.wait_ge(summed, unit.added + 2 * k + 1 + half)
                        nc.vector.tensor_tensor(sums, sums, p.rearrange("p (h t) -> p h t", t=tokens),
                                                ALU.add).then_inc(summed, 1)
                    dve.wait_ge(high_done, s + 1)
                    nc.vector.tensor_tensor(p_l, p, p_h, ALU.subtract).then_inc(split, 1)
                if kind == CORNER:
                    if unit.has_next:
                        latent_low(n + 1, 1 - par, 0)
                        latent_low(n + 1, 1 - par, 1)
                    if unit.has_second:
                        turn(n, unit.couple + 1)
                if kind == LATE and unit.has_second:
                    turned_split(n)

            for n in range(2):
                nc.vector.memset(raw(rot_l0[n][ROT:P, :]), 0.0).then_inc(zeroed, 1)
            latent_low(0, 0, 0)
            latent_low(0, 0, 1)
            sweep(dve, pair)


def combine(nc, top, x, heads_in, sums_in, inverses, linear, out):
    ctx = ExitStack()
    with ctx:
        def sb(name, shape, dt=F32):
            return ctx.enter_context(nc.sbuf_tensor(name, shape, dt))

        def sem(name):
            return ctx.enter_context(nc.semaphore(name))

        FIRST = HEADS * 3 // 4
        all_sums = sb("all_sums", [UNITS * UHEADS, CT])
        merged_h = sb("merged_h", [P, HEADS, DIM], F32R)
        merged_l = sb("merged_l", [P, HEADS, DIM], F32R)
        rows = [sb(f"rows{n}", [P, HEADS, P]) for n in range(2)]
        scale = [sb(f"scale{n}", [P, HEADS, P]) for n in range(2)]
        rows_h = [sb(f"rows_h{n}", [P, HEADS, P], F32R) for n in range(2)]
        rows_l = [sb(f"rows_l{n}", [P, HEADS, P], F32R) for n in range(2)]
        x_in = [sb(f"x_in{n}", [P, DIM]) for n in range(2)]
        lin_in = [sb(f"lin_in{n}", [P, DIM]) for n in range(2)]
        gate = [sb(f"gate{n}", [P, DIM]) for n in range(2)]
        result = [sb(f"result{n}", [P, DIM]) for n in range(2)]
        merge_ps = ctx.enter_context(nc.psum_tensor("merge_ps", [P, 4, DIM], F32))
        sum_ps = ctx.enter_context(nc.psum_tensor("sum_ps", [P, 2, DIM], F32))

        sums_loaded = sem("sums_loaded")
        inverted = sem("inverted")
        inverses_stored = sem("inverses_stored")
        merged = sem("merged")
        merge_high = sem("merge_high")
        merge_split = sem("merge_split")
        rows_in = [sem(f"rows_in{n}") for n in range(2)]
        scale_in = [sem(f"scale_in{n}") for n in range(2)]
        gate_in = [sem(f"gate_in{n}") for n in range(2)]
        scaled = sem("scaled")
        rows_high = sem("rows_high")
        rows_split = sem("rows_split")
        sigmoid = sem("sigmoid")
        gated = sem("gated")
        projected = [sem(f"projected{n}") for n in range(2)]
        times = [sem(f"times{n}") for n in range(2)]
        finished = sem("finished")
        stored = [sem(f"stored{n}") for n in range(2)]

        block = ctx.enter_context(nc.Block())

        def tile_of(ap, t):
            return ap[bass.ds(t, 1), :, :].rearrange("a p n -> (a p) n")

        x_tiles = x.rearrange("(t p) n -> t p n", p=P)
        out_tiles = out.rearrange("(t p) n -> t p n", p=P)

        @block.sync
        def _(sp):
            sp.dma_start(all_sums[:, :], sums_in.rearrange("u h t -> (u h) t")).then_inc(sums_loaded, 16)

            def load_rows(t, par):
                since(sp, rows_split, 2 * (t - 1))
                tokens = slice(par * P, (par + 1) * P)
                for half in range(2):
                    unit, heads = bass.ds(t - par + half, 1), slice(half * UHEADS, (half + 1) * UHEADS)
                    sp.dma_start(rows[par][:, heads, :], heads_in[unit, :, :].rearrange(
                        "a p (h t) -> (a p) h t", t=CT)[:, :, tokens]).then_inc(rows_in[par], 16)

            def load_scale(t, par):
                tokens = slice(par * P, (par + 1) * P)
                for half in range(2):
                    unit, heads = bass.ds(t - par + half, 1), slice(half * UHEADS, (half + 1) * UHEADS)
                    sp.dma_start(scale[par][:, heads, :], inverses[unit, :, tokens].to_broadcast(
                        [P, UHEADS, P])).then_inc(scale_in[par], 16)

            def load_rest(t, par):
                since(sp, finished, t - 1)
                sp.dma_start(x_in[par][:, :], tile_of(x_tiles, t)).then_inc(gate_in[par], 16)
                sp.dma_start(lin_in[par][:, :], tile_of(linear, t)).then_inc(gate_in[par], 16)

            def store(t, par):
                sp.wait_ge(finished, t + 1)
                sp.dma_start(tile_of(out_tiles, t), result[par][:, :]).then_inc(stored[par], 16)

            for par in range(2):
                load_rows(par, par)
                load_rest(par, par)
            sp.wait_ge(inverted, 1)
            sp.dma_start(inverses.rearrange("u h t -> (u h) t"), all_sums[:, :]).then_inc(inverses_stored, 16)
            sp.wait_ge(inverses_stored, 16)
            for par in range(2):
                load_scale(par, par)
            with sp.Fori(0, COUPLES - 1) as n:
                for par in range(2):
                    load_rows(2 * n + par + 2, par)
                    load_scale(2 * n + par + 2, par)
                    load_rest(2 * n + par + 2, par)
                    store(2 * n + par, par)
            for par in range(2):
                store(TILES - 2 + par, par)
            for par in range(2):
                sp.wait_ge(stored[par], 16 * COUPLES)

        @block.tensor
        def _(pe):
            for h in range(HEADS):
                since(pe, merge_split, h - 3)
                pe.matmul(merge_ps[:, h % 4, :], top.uv[:, h, :], top.wo[:, h, :], start=True, stop=True).then_inc(merged, 1)
            pe.wait_ge(merge_split, HEADS)

            def couple(n):
                for par in range(2):
                    t = 2 * n + par
                    since(pe, times[par], n)
                    for half in range(2):
                        pe.wait_ge(rows_split, 2 * t + half + 1)
                        for h in range(half * UHEADS, (half + 1) * UHEADS):
                            pe.matmul(sum_ps[:, par, :], rows_h[par][:, h, :], merged_h[:, h, :], start=(h == 0), stop=False)
                            pe.matmul(sum_ps[:, par, :], rows_h[par][:, h, :], merged_l[:, h, :], start=False, stop=False)
                            mm = pe.matmul(sum_ps[:, par, :], rows_l[par][:, h, :], merged_h[:, h, :],
                                           start=False, stop=(h == HEADS - 1))
                    mm.then_inc(projected[par], 1)

            couple(0)
            with pe.Fori(1, COUPLES) as n:
                couple(n)

        @block.scalar
        def _(act):
            def high_rows(t, par, n):
                since(act, projected[par], n)
                for half in range(2):
                    heads = slice(half * UHEADS, (half + 1) * UHEADS)
                    act.wait_ge(scaled, 2 * t + half + 1)
                    nc.scalar.copy(rows_h[par][:, heads, :], rows[par][:, heads, :]).then_inc(rows_high, 1)

            def gates(par, n):
                act.wait_ge(gate_in[par], 32 * (n + 1))
                since(act, times[par], n)
                nc.scalar.activation(gate[par][:, :], lin_in[par][:, :], ACT.Sigmoid).then_inc(sigmoid, 1)

            for h in range(HEADS):
                if h == FIRST:
                    high_rows(0, 0, 0)
                act.wait_ge(merged, h + 1)
                nc.scalar.copy(merged_h[:, h, :], merge_ps[:, h % 4, :]).then_inc(merge_high, 1)
            gates(0, 0)
            high_rows(1, 1, 0)
            gates(1, 0)
            with act.Fori(1, COUPLES) as n:
                for par in range(2):
                    high_rows(2 * n + par, par, n)
                    gates(par, n)

        @block.vector
        def _(dve):
            dve.wait_ge(sums_loaded, 16)
            nc.vector.reciprocal(all_sums[:, :], all_sums[:, :]).then_inc(inverted, 1)

            def scale_rows(t, par, n):
                dve.wait_ge(rows_in[par], 32 * (n + 1))
                dve.wait_ge(scale_in[par], 32 * (n + 1))
                for half in range(2):
                    heads = slice(half * UHEADS, (half + 1) * UHEADS)
                    nc.vector.tensor_tensor(rows[par][:, heads, :], rows[par][:, heads, :], scale[par][:, heads, :],
                                            ALU.mult).then_inc(scaled, 1)
                for half in range(2):
                    heads = slice(half * UHEADS, (half + 1) * UHEADS)
                    dve.wait_ge(rows_high, 2 * t + half + 1)
                    nc.vector.tensor_tensor(rows_l[par][:, heads, :], rows[par][:, heads, :], rows_h[par][:, heads, :],
                                            ALU.subtract).then_inc(rows_split, 1)

            def gates(t, par):
                dve.wait_ge(sigmoid, t + 1)
                nc.vector.tensor_tensor(gate[par][:, :], gate[par][:, :], lin_in[par][:, :], ALU.mult).then_inc(gated, 1)

            def finish(t, par, n):
                dve.wait_ge(projected[par], n + 1)
                dve.wait_ge(gated, t + 1)
                since(dve, stored[par], 16 * n)
                nc.vector.tensor_tensor(result[par][:, :], sum_ps[:, par, :], gate[par][:, :], ALU.mult).then_inc(times[par], 1)
                dve.wait_ge(times[par], n + 1)
                nc.vector.tensor_tensor(result[par][:, :], result[par][:, :], x_in[par][:, :], ALU.add).then_inc(finished, 1)

            def couple(n):
                scale_rows(2 * n + 1, 1, n)
                gates(2 * n + 1, 1)
                finish(2 * n, 0, n)
                scale_rows(2 * n + 2, 0, n + 1)
                gates(2 * n + 2, 0)
                finish(2 * n + 1, 1, n)

            for h in range(HEADS):
                if h == FIRST:
                    scale_rows(0, 0, 0)
                dve.wait_ge(merge_high, h + 1)
                nc.vector.tensor_tensor(merged_l[:, h, :], merge_ps[:, h % 4, :], merged_h[:, h, :],
                                        ALU.subtract).then_inc(merge_split, 1)
            gates(0, 0)
            couple(0)
            with dve.Fori(1, COUPLES - 1) as n:
                couple(n)
            scale_rows(TILES - 1, 1, COUPLES - 1)
            gates(TILES - 1, 1)
            finish(TILES - 2, 0, COUPLES - 1)
            finish(TILES - 1, 1, COUPLES - 1)


def program(nc, x, w_all, w_uq, w_uk, w_qr, lora_b, w_uv, w_o, cos, sin, out):
    keys = nc.dram_tensor("keys", [TILES, P, SK], F32, kind="Internal").ap()
    values = nc.dram_tensor("values", [TILES, P, SV], F32, kind="Internal").ap()
    linear = nc.dram_tensor("linear", [TILES, P, DIM], F32, kind="Internal").ap()
    heads_rows = nc.dram_tensor("heads_rows", [UNITS, P, HQ], F32, kind="Internal").ap()
    sums = nc.dram_tensor("sums_rows", [UNITS, UHEADS, CT], F32, kind="Internal").ap()
    inverses = nc.dram_tensor("inverses", [UNITS, UHEADS, CT], F32, kind="Internal").ap()
    turned = nc.dram_tensor("turned", [UNITS, 2, P, 1024], F32, kind="Internal").ap()
    with ExitStack() as ctx:
        with ExitStack() as first_phases:
            keep = Persistent(nc, first_phases)
            prepare(nc, keep, x, w_all, w_uq, w_uk, w_qr, lora_b, cos, sin, keys, values, linear, turned)
            top = Top(nc, ctx)
            attend(nc, keep, top, keys, values, turned, w_uv, w_o, heads_rows, sums)
        combine(nc, top, x, heads_rows, sums, inverses, linear, out)


def layout(L0_attn_x, L0_attn_W_DQ, L0_attn_W_UQ, L0_attn_W_QR, L0_attn_W_DKV, L0_attn_W_UK, L0_attn_W_UV,
           L0_attn_W_KR, L0_attn_W_O, L0_ffn_weight, L0_ffn_lora_A, L0_ffn_lora_B, L0_ffn_router_w):
    import numpy as np
    x = L0_attn_x.reshape(SEQ, DIM)
    kr_even, kr_odd = L0_attn_W_KR[0::2], L0_attn_W_KR[1::2]
    w_all = np.concatenate([L0_ffn_weight, L0_ffn_lora_A.reshape(ER, DIM), L0_ffn_router_w, L0_attn_W_DKV,
                            L0_attn_W_DQ, kr_even, kr_odd, kr_odd, kr_even], axis=0).T

    def by_head(w):
        return w.reshape(HEADS, P, LAT).transpose(1, 0, 2).reshape(P, HEADS * LAT)

    w_qr = L0_attn_W_QR.reshape(2, 4, 2, HALF, 2, LAT).transpose(5, 0, 4, 2, 1, 3).reshape(LAT, 2 * GT)
    inv_freq = np.float32(10000.0) ** (-np.arange(0, ROT, 2, dtype=np.float32) / np.float32(ROT))
    angle = np.tile(inv_freq[:, None] * np.arange(SEQ, dtype=np.float32)[None, :], (P // HALF, 1))
    arrays = {
        "x": x, "w_all": w_all, "w_uq": by_head(L0_attn_W_UQ), "w_uk": by_head(L0_attn_W_UK), "w_qr": w_qr,
        "lora_b": L0_ffn_lora_B.transpose(0, 2, 1).reshape(ER, DIM),
        "w_uv": by_head(L0_attn_W_UV), "w_o": L0_attn_W_O.T.reshape(HEADS, P, DIM).transpose(1, 0, 2),
        "cos": np.cos(angle), "sin": np.sin(angle),
    }
    return {name: np.ascontiguousarray(a) for name, a in arrays.items()}


def kernel(**inputs):
    import numpy as np
    import concourse.bacc as bacc
    from concourse.bass_utils import run_bass_kernel_spmd

    nc = bacc.Bacc("TRN2", target_bir_lowering=False, num_devices=1)
    arrays = {f"in_{n}": a for n, a in layout(**{n: np.asarray(a) for n, a in inputs.items()}).items()}
    args = [nc.dram_tensor(n, a.shape, mybir.dt.from_np(a.dtype), kind="ExternalInput").ap() for n, a in arrays.items()]
    args.append(nc.dram_tensor("out", (SEQ, DIM), F32, kind="ExternalOutput").ap())
    program(nc, *args)
    result = run_bass_kernel_spmd(nc, [arrays], core_ids=[0])
    return result.results[0]["out"].reshape(1, SEQ, DIM)
```

```python
from contextlib import ExitStack

import concourse.bass as bass
from concourse import mybir
from concourse.alu_op_type import AluOpType as ALU

ACT = mybir.ActivationFunctionType
AX = mybir.AxisListType
F32 = mybir.dt.float32
F32R = mybir.dt.float32r

P = 128
SEQ = 2048
DIM = 512
KC = DIM // P
TILES = SEQ // P
HEADS = 16
LAT = 128
ROT = 64
HALF = ROT // 2
EXPERTS, RANK = 8, 16
ER = EXPERTS * RANK
LORA_SCALE = 32.0 / RANK
EPS = 1e-5
QK_SCALE = (P + ROT) ** -0.5
CLIP = 80.0
P_MAX = 2.718281828459045 ** (CLIP * QK_SCALE)
P_MIN = 2.718281828459045 ** (-CLIP * QK_SCALE)

GROUP = 4
GROUPS = TILES // GROUP
GT = GROUP * P

C_BASE = 0
C_A = DIM
C_ROUTER = C_A + ER
C_KV = C_ROUTER + EXPERTS
C_Q = C_KV + LAT
C_KR = C_Q + LAT
C_ALL = C_KR + 2 * ROT
SMALL = C_Q - C_A

COUPLES = TILES // 2
CT = 2 * P
UNITS = 2 * COUPLES
UHEADS = HEADS // 2
HQ = UHEADS * CT
HW = HQ // 2
HH = UHEADS // 2
SK = 3 * P
SV = 2 * P


def since(eng, sem, count):
    if not isinstance(count, int) or count > 0:
        eng.wait_ge(sem, count)


def raw(ap):
    return ap.bitcast(F32)


class Persistent:

    def __init__(self, nc, ctx):
        def sb(name, shape, dt):
            return ctx.enter_context(nc.sbuf_tensor(name, shape, dt))

        self.cos = sb("cos", [P, SEQ], F32)
        self.sin = sb("sin", [P, SEQ], F32)
        self.absorb_h = sb("absorb_h", [P, HQ], F32R)
        self.absorb_l = sb("absorb_l", [P, HQ], F32R)
        self.qr_h = sb("qr_h", [P, 2 * GT], F32R)
        self.qr_l = sb("qr_l", [P, 2 * GT], F32R)
        self.cq_h = sb("cq_h", [P, SEQ], F32R)
        self.cq_l = sb("cq_l", [P, SEQ], F32R)
        self.causal = sb("causal", [P, P], F32)
        self.ones = sb("ones", [P, 32], F32)


class Top:

    def __init__(self, nc, ctx):
        self.head_rows = ctx.enter_context(nc.sbuf_tensor("head_rows", [P, HQ], F32, side="right"))
        self.sums = ctx.enter_context(nc.sbuf_tensor("sums", [P, 512], F32, side="right"))
        with ExitStack() as lent:
            self.q_h, self.q_l, self.rot_hh, self.rot_l0 = (
                lent.enter_context(nc.sbuf_tensor(name, [P, HQ], F32R, side="right"))
                for name in ("q_h0", "q_l0", "rot_hh0", "rot_l0"))
            self.total = lent.enter_context(nc.sbuf_tensor("total0", [P, HQ], F32, side="right"))
        self.wo = ctx.enter_context(nc.sbuf_tensor("wo", [P, HEADS, DIM], F32, side="right"))
        self.uv = ctx.enter_context(nc.sbuf_tensor("uv", [P, HEADS, LAT], F32, side="right"))


def prepare(nc, keep, x, w_all, w_uq, w_uk, w_qr, lora_b, cos, sin, keys, values, linear, turned_out):
    ctx = ExitStack()
    with ctx:
        def sb(name, shape, dt=F32):
            return ctx.enter_context(nc.sbuf_tensor(name, shape, dt))

        def ps(name, shape):
            return ctx.enter_context(nc.psum_tensor(name, shape, F32))

        def sem(name):
            return ctx.enter_context(nc.semaphore(name))

        x_all = sb("x_all", [P, TILES, DIM])
        w_stage = sb("w_stage", [P, KC, C_ALL])
        w_h = sb("w_h", [P, KC, C_ALL], F32R)
        w_l = sb("w_l", [P, KC, C_ALL], F32R)
        xn = sb("xn", [P, GROUP, DIM])
        y = sb("y", [P, GROUP, DIM])
        qr_stage = sb("qr_stage", [P, 2 * GT])
        b_stage = sb("b_stage", [P, DIM])
        b_h = sb("b_h", [P, DIM], F32R)
        b_l = sb("b_l", [P, DIM], F32R)
        xt_h = sb("xt_h", [P, KC, GT], F32R)
        xt_l = sb("xt_l", [P, KC, GT], F32R)
        key_out = sb("key_out", [P, GROUP, SK], F32R)
        value_out = sb("value_out", [P, GROUP, SV], F32R)
        small = sb("small", [P, GROUP, ER + EXPERTS])
        turn_h = sb("turn_h", [P, GROUP, P], F32R)
        turn_l = sb("turn_l", [P, GROUP, P], F32R)
        weighted = sb("weighted", [P, GROUP, ER])
        rot_a = sb("rot_a", [P, GT])
        rot_b = sb("rot_b", [P, GT])
        ident = sb("ident", [P, P])
        prod = [[w_stage[:, 2 * n + m // 2, (m % 2) * 512:(m % 2 + 1) * 512] for m in range(4)] for n in range(2)]
        rot_f = [x_all[:, 8 + 2 * n:10 + 2 * n, :] for n in range(2)]
        rot_hl = [x_all[:, 4 * n:4 * n + 4, :].bitcast(F32R).rearrange("p (w e) n -> p w e n", w=2) for n in range(2)]
        stats = sb("stats", [P, GROUP, 6])
        moments = sb("moments", [P, GROUP, 2])
        deviation = sb("deviation", [P, GROUP])
        rstd = sb("rstd", [P, GROUP])
        eps = sb("eps", [P, 1])
        warm = sb("warm", [P, 1])
        order = sb("order", [P, EXPERTS])
        r1 = sb("r1", [P, GROUP])
        rt = [sb(f"rt{n}", [P, GROUP, EXPERTS]) for n in range(5)]
        rw = sb("rw", [P, GROUP, EXPERTS])

        base_ps = ps("base_ps", [P, GROUP, DIM])
        turn_ps = ps("turn_ps", [P, 2, 512])
        work_ps = ps("work_ps", [P, 2, 512])

        x_first = [sem(f"x_first{a}") for a in range(GROUP)]
        x_next, x_late = sem("x_next"), sem("x_late")
        w_in = [sem(f"w_in{c}") for c in range(KC)]
        uqk_in, rest_in, qr_in = sem("uqk_in"), sem("rest_in"), sem("qr_in")
        constants = sem("constants")
        cleared = sem("cleared")
        absorbed = sem("absorbed")
        absorb_high = sem("absorb_high")
        absorb_split = sem("absorb_split")
        w_high, w_low = sem("w_high"), sem("w_low")
        rest_high, rest_low = sem("rest_high"), sem("rest_low")
        stats_done, var_done = sem("stats_done"), sem("var_done")
        dev_done, rstd_done = sem("dev_done"), sem("rstd_done")
        norm_done = sem("norm_done")
        lora_turned = sem("lora_turned")
        lora_high = sem("lora_high")
        lora_low = sem("lora_low")
        turned = sem("turned")
        turn_high = sem("turn_high")
        turn_used = sem("turn_used")
        worked = sem("worked")
        work_high = sem("work_high")
        work_used = sem("work_used")
        based = sem("based")
        router_x = sem("router_x")
        router_e = sem("router_e")
        router_s = sem("router_s")
        shares_done = sem("shares_done")
        weighted_done = sem("weighted_done")
        linear_done = sem("linear_done")
        y_done = sem("y_done")
        rope_s = sem("rope_s")
        r_scored = sem("r_scored")
        r_read = sem("r_read")
        r_added = sem("r_added")
        r_high, r_low = sem("r_high"), sem("r_low")
        turned_stored = sem("turned_stored")
        keys_out, values_out, y_out = sem("keys_out"), sem("values_out"), sem("y_out")

        uq = x_all[:, 2 * GROUP:3 * GROUP, :].rearrange("p a n -> p (a n)")
        uk = x_all[:, 3 * GROUP:4 * GROUP, :].rearrange("p a n -> p (a n)")
        WORK = GROUP + 3
        ROUTER = 15
        ROPE = 5
        KEY_STORES = 5

        block = ctx.enter_context(nc.Block())

        @block.sync
        def _(sp):
            def load_x(g, signal):
                sp.dma_start(x_all[:, g * GROUP:(g + 1) * GROUP, :],
                             x[g * GT:(g + 1) * GT, :].rearrange("(a p) n -> p a n", p=P)).then_inc(signal, 16)

            for a in range(GROUP):
                sp.dma_start(x_all[:, a, :], x[a * P:(a + 1) * P, :]).then_inc(x_first[a], 16)
            for c in range(KC):
                sp.dma_start(w_stage[:, c, :], w_all[c * P:(c + 1) * P, :]).then_inc(w_in[c], 16)
            sp.dma_start(uq, w_uq).then_inc(uqk_in, 16)
            sp.dma_start(uk, w_uk).then_inc(uqk_in, 16)
            load_x(1, x_next)
            sp.dma_start(b_stage[:, :], lora_b).then_inc(rest_in, 16)
            sp.dma_start(keep.cos[:, :], cos).then_inc(rest_in, 16)
            sp.dma_start(keep.sin[:, :], sin).then_inc(rest_in, 16)
            sp.dma_start(qr_stage[:, :], w_qr).then_inc(qr_in, 16)
            sp.wait_ge(absorbed, 2)
            load_x(2, x_late)
            sp.wait_ge(x_late, 16)
            load_x(3, x_late)

            def store_rows(g):
                sp.wait_ge(work_used, WORK * g + GROUP)
                sp.dma_start(values[bass.ds(g * GROUP, GROUP), :, :].rearrange("a p n -> p a n"),
                             raw(value_out[:, :, :])).then_inc(values_out, 16)
                sp.wait_ge(rope_s, ROPE * (g + 1))
                out = keys[bass.ds(g * GROUP, GROUP), :, :]
                sp.dma_start(out[:, :, 0:2 * P].rearrange("a p n -> p a n"),
                             raw(key_out[:, :, 0:2 * P])).then_inc(keys_out, 16)
                for n in range(4):
                    rows = out[:, (n // 2) * ROT:(n // 2 + 1) * ROT, 2 * P:SK].rearrange("a (f e) n -> e f a n", e=2)
                    sp.dma_start(rows[n % 2], raw(key_out[n * HALF:(n + 1) * HALF, :, 2 * P:SK])).then_inc(keys_out, 16)

            with sp.Fori(0, GROUPS - 1) as g:
                store_rows(g)
                sp.wait_ge(y_done, GROUP * (g + 1))
                sp.dma_start(linear[bass.ds(g * GROUP, GROUP), :, :].rearrange("a p n -> p a n"),
                             y[:, :, :]).then_inc(y_out, 16)
            store_rows(GROUPS - 1)
            for n in range(2):
                sp.wait_ge(r_low, n + 1)
                sp.dma_start(turned_out[n].rearrange("w p n -> p w n"),
                             raw(rot_hl[n]).rearrange("p w e n -> p w (e n)")).then_inc(turned_stored, 16)
            for a in range(GROUP):
                t = (GROUPS - 1) * GROUP + a
                sp.wait_ge(y_done, t + 1)
                sp.dma_start(linear[t], y[:, a, :]).then_inc(y_out, 16)
            sp.wait_ge(turned_stored, 32)
            sp.wait_ge(keys_out, 16 * KEY_STORES * GROUPS)
            sp.wait_ge(values_out, 16 * GROUPS)
            sp.wait_ge(y_out, 16 * (GROUPS - 1 + GROUP))

        @block.gpsimd
        def _(pool):
            nc.gpsimd.memset(ident[:, :], 0.0).then_inc(cleared, 1)
            nc.gpsimd.memset(keep.causal[:, :], 1.0).then_inc(cleared, 1)
            nc.gpsimd.memset(eps[:, :], EPS).then_inc(constants, 1)
            for e in range(EXPERTS):
                nc.gpsimd.memset(order[:, e:e + 1], float(EXPERTS - e)).then_inc(constants, 1)
            pool.wait_ge(cleared, 2)
            nc.gpsimd.affine_select(out=ident[:, :], in_=ident[:, :], compare_op=ALU.not_equal, fill=1.0,
                                    base=0, pattern=[[-1, P]], channel_multiplier=1).then_inc(constants, 1)
            nc.gpsimd.affine_select(out=keep.causal[:, :], in_=keep.causal[:, :], compare_op=ALU.is_ge, fill=0.0,
                                    base=0, pattern=[[1, P]], channel_multiplier=-1).then_inc(constants, 1)
            nc.gpsimd.memset(keep.ones[:, :], 1.0).then_inc(constants, 1)

        CONSTANTS = 1 + EXPERTS + 3

        @block.tensor
        def _(pe):
            def absorb():
                pe.wait_ge(uqk_in, 32)
                for h in range(HEADS):
                    mm = pe.matmul(base_ps[:, h // 4, (h % 4) * P:(h % 4 + 1) * P], uq[:, h * P:(h + 1) * P],
                                   uk[:, h * P:(h + 1) * P], start=True, stop=True)
                    if h % 8 == 7:
                        mm.then_inc(absorbed, 1)

            pe.wait_ge(constants, CONSTANTS)

            def turn_x(a, n):
                pe.wait_ge(norm_done, n + a + 1)
                since(pe, turn_used, n + a - 1)
                for c in range(KC):
                    mm = pe.transpose(turn_ps[:, a % 2, c * P:(c + 1) * P], xn[:, a, c * P:(c + 1) * P], ident[:, :])
                mm.then_inc(turned, 1)

            for a in range(GROUP):
                turn_x(a, 0)

            def rotary(n, banks):
                for m in range(4):
                    w, out = slice((4 * n + m) * P, (4 * n + m + 1) * P), banks[:, m // 2, (m % 2) * CT:(m % 2 + 1) * CT]
                    pe.matmul(out, keep.qr_h[:, w], keep.cq_h[:, 0:CT], start=True, stop=False)
                    pe.matmul(out, keep.qr_h[:, w], keep.cq_l[:, 0:CT], start=False, stop=False)
                    mm = pe.matmul(out, keep.qr_l[:, w], keep.cq_h[:, 0:CT], start=False, stop=True)
                mm.then_inc(r_scored, 1)

            def group(g, first=False, last=False):
                for a in range(GROUP):
                    pe.wait_ge(turn_used, GROUP * g + a + 1)
                    since(pe, work_used, WORK * g + (a - 1 if a else 0))
                    n = 0
                    for c in range(KC):
                        if first and a == 0:
                            pe.wait_ge(w_low, c + 1)
                        for xs, ws in ((xt_h, w_h), (xt_l, w_h), (xt_h, w_l)):
                            mm = pe.matmul(work_ps[:, a % 2, 0:SMALL], xs[:, c, a * P:(a + 1) * P],
                                           ws[:, c, C_A:C_Q], start=(n == 0), stop=(n == 3 * KC - 1))
                            n += 1
                    mm.then_inc(worked, 1)
                for k, col in enumerate((C_KV, C_Q, C_KR)):
                    pe.wait_ge(work_used, WORK * g + GROUP + k - 1)
                    n = 0
                    for c in range(KC):
                        for ws, xs in ((w_h, xt_h), (w_l, xt_h), (w_h, xt_l)):
                            mm = pe.matmul(work_ps[:, (GROUP + k) % 2, :], ws[:, c, col:col + P], xs[:, c, :],
                                           start=(n == 0), stop=(n == 3 * KC - 1))
                            n += 1
                    mm.then_inc(worked, 1)
                    if first and k == 0:
                        absorb()
                if first:
                    pe.wait_ge(absorb_split, 2)
                since(pe, y_done, GROUP * g)
                if last:
                    pe.wait_ge(rest_low, 2)
                    rotary(0, turn_ps)
                    rotary(1, base_ps[:, 2:4, :])
                for a in range(GROUP):
                    if last and a == 2:
                        pe.wait_ge(r_read, 8)
                    if a == GROUP - 1:
                        pe.wait_ge(weighted_done, g + 1)
                        pe.wait_ge(work_used, WORK * g + GROUP + 2)
                        for b in range(GROUP):
                            mm = pe.transpose(work_ps[:, 1, b * P:(b + 1) * P], weighted[:, b, :], ident[:, :])
                        mm.then_inc(lora_turned, 1)
                    n = 0
                    for c in range(KC):
                        for xs, ws in ((xt_h, w_h), (xt_l, w_h), (xt_h, w_l)):
                            mm = pe.matmul(base_ps[:, a, :], xs[:, c, a * P:(a + 1) * P], ws[:, c, 0:DIM],
                                           start=(n == 0), stop=False)
                            n += 1
                mm.then_inc(based, 1)
                if not last:
                    for a in range(2):
                        turn_x(a, GROUP * (g + 1))
                pe.wait_ge(lora_low, g + 1)
                if first:
                    pe.wait_ge(rest_low, 1)
                for a in range(GROUP):
                    pe.matmul(base_ps[:, a, :], turn_h[:, a, :], b_h[:, :], start=False, stop=False)
                    pe.matmul(base_ps[:, a, :], turn_l[:, a, :], b_h[:, :], start=False, stop=False)
                    pe.matmul(base_ps[:, a, :], turn_h[:, a, :], b_l[:, :], start=False,
                              stop=True).then_inc(linear_done, 1)
                if not last:
                    for a in range(2, GROUP):
                        turn_x(a, GROUP * (g + 1))

            group(0, first=True)
            with pe.Fori(1, GROUPS - 1) as g:
                group(g)
            group(GROUPS - 1, last=True)

        @block.scalar
        def _(act):
            def deviations(g):
                act.wait_ge(var_done, g + 1)
                since(act, rstd_done, g)
                nc.scalar.activation(deviation[:, :], moments[:, :, 1], ACT.Sqrt,
                                     bias=eps[:, 0:1]).then_inc(dev_done, 1)

            def w_high_part(c):
                act.wait_ge(w_in[c], 16)
                nc.scalar.copy(w_h[:, c, :], w_stage[:, c, :]).then_inc(w_high, 1)

            act.wait_ge(constants, CONSTANTS)
            nc.scalar.activation(warm[:, :], eps[:, :], ACT.Sqrt)
            deviations(0)
            w_high_part(0)

            def turn_x(a, n):
                act.wait_ge(turned, n + a + 1)
                nc.scalar.copy(xt_h[:, :, a * P:(a + 1) * P],
                               turn_ps[:, a % 2, :].rearrange("p (c t) -> p c t", c=KC)).then_inc(turn_high, 1)

            for a in range(GROUP):
                if a < KC - 1:
                    w_high_part(a + 1)
                turn_x(a, 0)

            def group(g, first=False, last=False):
                since(act, values_out, 16 * g)
                for a in range(GROUP):
                    act.wait_ge(worked, WORK * g + a + 1)
                    nc.scalar.copy(value_out[:, a, 0:P], work_ps[:, a % 2, C_KV - C_A:SMALL]).then_inc(work_high, 1)
                since(act, keys_out, 16 * KEY_STORES * g)
                act.wait_ge(worked, WORK * g + GROUP + 1)
                nc.scalar.copy(key_out[:, :, 0:P],
                               work_ps[:, 0, :].rearrange("p (a t) -> p a t", a=GROUP)).then_inc(work_high, 1)
                act.wait_ge(router_x, g + 1)
                nc.scalar.activation(rt[1][:, :, :], rt[0][:, :, :], ACT.Exp).then_inc(router_e, 1)
                if first:
                    for half in range(2):
                        act.wait_ge(absorbed, half + 1)
                        nc.scalar.copy(keep.absorb_h[:, half * HW:(half + 1) * HW],
                                       base_ps[:, 2 * half:2 * half + 2, :]).then_inc(absorb_high, 1)
                act.wait_ge(worked, WORK * g + GROUP + 2)
                nc.scalar.copy(keep.cq_h[:, bass.ds(g * GT, GT)], work_ps[:, 1, :]).then_inc(work_high, 1)
                if first:
                    act.wait_ge(rest_in, 48)
                    nc.scalar.copy(b_h[:, :], b_stage[:, :]).then_inc(rest_high, 1)
                    act.wait_ge(qr_in, 16)
                    nc.scalar.copy(keep.qr_h[:, :], qr_stage[:, :]).then_inc(rest_high, 1)
                if not last:
                    deviations(g + 1)
                if last:
                    for n in range(2):
                        act.wait_ge(r_added, 2 * n + 2)
                        nc.scalar.copy(rot_hl[n][:, 0, :, :], rot_f[n]).then_inc(r_high, 1)
                act.wait_ge(lora_turned, g + 1)
                nc.scalar.copy(turn_h[:, :, :], work_ps[:, 1, :]).then_inc(lora_high, 1)
                if not last:
                    act.wait_ge(based, g + 1)
                    for a in range(GROUP):
                        turn_x(a, GROUP * (g + 1))
                since(act, y_out, 16 * g)
                for a in range(GROUP):
                    act.wait_ge(linear_done, GROUP * g + a + 1)
                    nc.scalar.copy(y[:, a, :], base_ps[:, a, :]).then_inc(y_done, 1)

            group(0, first=True)
            with act.Fori(1, GROUPS - 1) as g:
                group(g)
            group(GROUPS - 1, last=True)

        @block.vector
        def _(dve):
            tiles_seen = dve.alloc_register("tiles_seen")
            dve.reg_mov(tiles_seen, GROUP)

            def statistics(g, first=False):
                for a in range(GROUP):
                    if first:
                        dve.wait_ge(x_first[a], 16)
                    t = bass.ds(g * GROUP + a, 1)
                    nc.vector.bn_stats(stats[:, a, :], x_all[:, t, :].rearrange("p a n -> p (a n)")).then_inc(stats_done, 1)
                dve.wait_ge(stats_done, tiles_seen)
                dve.reg_add(tiles_seen, tiles_seen, GROUP)
                for a in range(GROUP):
                    ins = nc.vector.bn_aggr(moments[:, a, :], stats[:, a, :])
                ins.then_inc(var_done, 1)

            def inverses(g):
                dve.wait_ge(dev_done, g + 1)
                nc.vector.reciprocal(rstd[:, :], deviation[:, :]).then_inc(rstd_done, 1)
                dve.wait_ge(rstd_done, g + 1)

            def normalise(g, a):
                t = g * GROUP + a
                nc.vector.tensor_scalar(xn[:, a, :], x_all[:, bass.ds(t, 1), :].rearrange("p a n -> p (a n)"),
                                        moments[:, a, 0:1], rstd[:, a:a + 1],
                                        ALU.subtract, ALU.mult).then_inc(norm_done, 1)

            def turn_x(a, n):
                dve.wait_ge(turn_high, n + a + 1)
                cols = slice(a * P, (a + 1) * P)
                nc.vector.tensor_tensor(xt_l[:, :, cols], turn_ps[:, a % 2, :].rearrange("p (c t) -> p c t", c=KC),
                                        xt_h[:, :, cols], ALU.subtract).then_inc(turn_used, 1)

            def w_low_part(c):
                dve.wait_ge(w_high, c + 1)
                nc.vector.tensor_tensor(w_l[:, c, :], w_stage[:, c, :], w_h[:, c, :], ALU.subtract).then_inc(w_low, 1)

            statistics(0, first=True)
            inverses(0)
            for a in range(GROUP):
                normalise(0, a)
            w_low_part(0)
            for a in range(GROUP):
                if a < KC - 1:
                    w_low_part(a + 1)
                turn_x(a, 0)
            dve.wait_ge(constants, CONSTANTS)

            def group(g, first=False, last=False):
                for a in range(GROUP):
                    dve.wait_ge(work_high, (WORK - 1) * g + a + 1)
                    nc.vector.tensor_copy(small[:, a, :], work_ps[:, a % 2, 0:ER + EXPERTS])
                    nc.vector.tensor_tensor(value_out[:, a, P:SV], work_ps[:, a % 2, C_KV - C_A:SMALL],
                                            value_out[:, a, 0:P], ALU.subtract).then_inc(work_used, 1)
                dve.wait_ge(work_high, (WORK - 1) * g + GROUP + 1)
                nc.vector.tensor_tensor(key_out[:, :, P:2 * P], work_ps[:, 0, :].rearrange("p (a t) -> p a t", a=GROUP),
                                        key_out[:, :, 0:P], ALU.subtract).then_inc(work_used, 1)
                shape = [P, GROUP, EXPERTS]
                logits = small[:, :, ER:ER + EXPERTS]
                ranks = order[:, :].unsqueeze(1).to_broadcast(shape)
                most = r1[:, :].unsqueeze(2).to_broadcast(shape)
                expo, best, second, rest = rt[1:]
                step = [0]

                def then(ins):
                    step[0] += 1
                    ins.then_inc(router_s, 1)
                    dve.wait_ge(router_s, ROUTER * g + step[0])

                dve.wait_ge(work_used, WORK * g + GROUP)
                then(nc.vector.tensor_reduce(r1[:, :], logits, AX.X, ALU.max))
                nc.vector.tensor_tensor(rt[0][:, :, :], logits, most, ALU.subtract).then_inc(router_x, 1)
                then(nc.vector.tensor_tensor(best[:, :, :], logits, most, ALU.is_equal))
                then(nc.vector.tensor_tensor(second[:, :, :], best[:, :, :], ranks, ALU.mult))
                then(nc.vector.tensor_reduce(r1[:, :], second[:, :, :], AX.X, ALU.max))
                then(nc.vector.tensor_tensor(best[:, :, :], second[:, :, :], most, ALU.is_equal))
                then(nc.vector.scalar_tensor_tensor(out=rest[:, :, :], in0=best[:, :, :], scalar=-3.0e38, in1=logits,
                                                    op0=ALU.mult, op1=ALU.add))
                then(nc.vector.tensor_reduce(r1[:, :], rest[:, :, :], AX.X, ALU.max))
                then(nc.vector.tensor_tensor(second[:, :, :], rest[:, :, :], most, ALU.is_equal))
                then(nc.vector.tensor_tensor(rest[:, :, :], second[:, :, :], ranks, ALU.mult))
                then(nc.vector.tensor_reduce(r1[:, :], rest[:, :, :], AX.X, ALU.max))
                then(nc.vector.tensor_tensor(second[:, :, :], rest[:, :, :], most, ALU.is_equal))
                then(nc.vector.tensor_tensor(rest[:, :, :], best[:, :, :], second[:, :, :], ALU.add))
                dve.wait_ge(router_e, g + 1)
                then(nc.vector.tensor_tensor(rest[:, :, :], rest[:, :, :], expo[:, :, :], ALU.mult))
                then(nc.vector.tensor_reduce(r1[:, :], rest[:, :, :], AX.X, ALU.add))
                then(nc.vector.reciprocal(r1[:, :], r1[:, :]))
                nc.vector.scalar_tensor_tensor(out=rw[:, :, :], in0=rest[:, :, :], scalar=LORA_SCALE, in1=most,
                                               op0=ALU.mult, op1=ALU.mult).then_inc(shares_done, 1)
                dve.wait_ge(shares_done, g + 1)
                nc.vector.tensor_tensor(
                    weighted[:, :, :].rearrange("p a (e r) -> p (a e) r", r=RANK),
                    small[:, :, 0:ER].rearrange("p a (e r) -> p a e r", r=RANK),
                    rw[:, :, :].rearrange("p a e -> p (a e)").unsqueeze(2).to_broadcast([P, GROUP * EXPERTS, RANK]),
                    ALU.mult).then_inc(weighted_done, 1)
                assert step[0] == ROUTER

                if first:
                    for half in range(2):
                        dve.wait_ge(absorb_high, half + 1)
                        cols = slice(half * HW, (half + 1) * HW)
                        nc.vector.tensor_tensor(keep.absorb_l[:, cols], base_ps[:, 2 * half:2 * half + 2, :].rearrange("p b n -> p (b n)"),
                                                keep.absorb_h[:, cols], ALU.subtract).then_inc(absorb_split, 1)
                dve.wait_ge(work_high, (WORK - 1) * g + GROUP + 2)
                nc.vector.tensor_tensor(keep.cq_l[:, bass.ds(g * GT, GT)], work_ps[:, 1, :],
                                        keep.cq_h[:, bass.ds(g * GT, GT)], ALU.subtract).then_inc(work_used, 1)
                if first:
                    dve.wait_ge(rest_in, 48)
                dve.wait_ge(worked, WORK * g + WORK)
                nc.vector.tensor_tensor(rot_a[0:ROT, :], work_ps[0:ROT, 0, :], keep.cos[0:ROT, bass.ds(g * GT, GT)],
                                        ALU.mult).then_inc(rope_s, 1)
                nc.vector.tensor_tensor(rot_b[0:ROT, :], work_ps[ROT:P, 0, :], keep.sin[ROT:P, bass.ds(g * GT, GT)],
                                        ALU.mult).then_inc(work_used, 1)
                dve.wait_ge(work_used, WORK * (g + 1))
                nc.vector.tensor_tensor(rot_a[0:HALF, :], rot_a[0:HALF, :], rot_b[0:HALF, :],
                                        ALU.subtract).then_inc(rope_s, 1)
                nc.vector.tensor_tensor(rot_a[HALF:ROT, :], rot_a[HALF:ROT, :], rot_b[HALF:ROT, :],
                                        ALU.add).then_inc(rope_s, 1)
                dve.wait_ge(rope_s, ROPE * g + 3)
                turned_keys = rot_a[0:ROT, :].rearrange("p (a t) -> p a t", a=GROUP)
                nc.vector.tensor_copy(key_out[0:ROT, :, 2 * P:SK], turned_keys).then_inc(rope_s, 1)
                dve.wait_ge(rope_s, ROPE * g + 4)
                nc.vector.tensor_tensor(key_out[ROT:P, :, 2 * P:SK], turned_keys, key_out[0:ROT, :, 2 * P:SK],
                                        ALU.subtract).then_inc(rope_s, 1)

                if first:
                    dve.wait_ge(rest_high, 1)
                    nc.vector.tensor_tensor(b_l[:, :], b_stage[:, :], b_h[:, :], ALU.subtract).then_inc(rest_low, 1)
                    dve.wait_ge(rest_high, 2)
                    nc.vector.tensor_tensor(keep.qr_l[:, :], qr_stage[:, :], keep.qr_h[:, :], ALU.subtract).then_inc(rest_low, 1)
                    dve.wait_ge(x_next, 16)
                if not last:
                    if not first:
                        dve.wait_ge(x_late, 16 * g)
                    statistics(g + 1)
                    inverses(g + 1)
                    for a in range(GROUP):
                        normalise(g + 1, a)
                if last:
                    turn_queries(0, turn_ps)
                    turn_queries(1, base_ps[:, 2:4, :])
                    for n in range(2):
                        add_queries(n)
                    low_queries(0)
                dve.wait_ge(lora_high, g + 1)
                nc.vector.tensor_tensor(turn_l[:, :, :], work_ps[:, 1, :].rearrange("p (a t) -> p a t", a=GROUP),
                                        turn_h[:, :, :], ALU.subtract).then_inc(lora_low, 1)
                if last:
                    low_queries(1)
                if not last:
                    for a in range(GROUP):
                        turn_x(a, GROUP * (g + 1))

            def turn_queries(n, banks):
                dve.wait_ge(r_scored, n + 1)
                cos, sin = (w[:, 0:CT].unsqueeze(1).to_broadcast([P, 2, CT]) for w in (keep.cos, keep.sin))
                even, odd = (banks[:, eo, :].rearrange("p (g t) -> p g t", g=2) for eo in range(2))
                for out, rows, angle in zip(prod[n], (even, odd, even, odd), (cos, sin, sin, cos)):
                    nc.vector.tensor_tensor(out.rearrange("p (g t) -> p g t", g=2), rows, angle, ALU.mult).then_inc(r_read, 1)

            def add_queries(n):
                dve.wait_ge(r_read, 4 * n + 4)
                nc.vector.tensor_tensor(rot_f[n][:, 0, :], prod[n][0], prod[n][1], ALU.subtract).then_inc(r_added, 1)
                nc.vector.tensor_tensor(rot_f[n][:, 1, :], prod[n][2], prod[n][3], ALU.add).then_inc(r_added, 1)

            def low_queries(n):
                dve.wait_ge(r_high, n + 1)
                nc.vector.tensor_tensor(rot_hl[n][:, 1, :, :], rot_f[n], rot_hl[n][:, 0, :, :],
                                        ALU.subtract).then_inc(r_low, 1)

            group(0, first=True)
            with dve.Fori(1, GROUPS - 1) as g:
                group(g)
            group(GROUPS - 1, last=True)


FULL, CORNER, LATE = range(3)


class Unit:

    def __init__(self, couple, par, added):
        self.couple, self.par = couple, par
        self.added = added
        self.n = 2 * couple + par
        last = isinstance(couple, int) and couple == COUPLES - 1
        self.has_next = not (last and par == 1)
        self.has_second = not last
        self.next_couple = couple + par


def sweep(eng, pair):

    def two(t, unit, k, prev):
        pair(t, unit, k, 0, FULL, prev)
        pair(t + 1, unit, k + 1, 1, FULL, FULL)

    def units(m, before, added, prev):
        for par in range(2):
            unit = Unit(m, par, added + par * (4 * m + 2))
            t = before + par * (2 * m + 2)
            pair(t, unit, 2 * m, 0, CORNER, prev)
            pair(t + 1, unit, 2 * m + 1, 1, LATE, CORNER)
            prev = LATE
            if not (isinstance(m, int) and m == 0):
                two(t + 2, unit, 0, LATE)
                prev = FULL
                if not (isinstance(m, int) and m == 1):
                    with eng.Fori(1, m) as n:
                        two(t + 2 + 2 * n, unit, 2 * n, FULL)

    units(0, 0, 0, None)
    units(1, 4, 4, LATE)
    done, adds = eng.alloc_register("pairs_done"), eng.alloc_register("adds_done")
    eng.reg_mov(done, 12)
    eng.reg_mov(adds, 16)
    with eng.Fori(2, COUPLES - 1) as m:
        units(m, eng.snap(done, min_val=12, max_val=PAIRS), eng.snap(adds, min_val=16, max_val=2 * PAIRS), FULL)
        eng.reg_add(done, done, 4 * m + 4)
        eng.reg_add(adds, adds, 8 * m + 4)
    before = PAIRS - 4 * COUPLES
    units(COUPLES - 1, before, 2 * before - 2 * (UNITS - 2), FULL)


PAIRS = 2 * COUPLES * (COUPLES + 1)
EARLY = UNITS - 2
SPREADS = 3


def attend(nc, keep, top, keys, values, turned, w_uv, w_o, heads_out, sums_out, inverses):
    ctx = ExitStack()
    with ctx:
        def sb(name, shape, dt=F32):
            return ctx.enter_context(nc.sbuf_tensor(name, shape, dt))

        def sem(name):
            return ctx.enter_context(nc.semaphore(name))

        key_slot = [sb(f"key_slot{n}", [P, SK], F32R) for n in range(2)]
        value_slot = [sb(f"value_slot{n}", [P, SV], F32R) for n in range(2)]
        q_h = [top.q_h, sb("q_h1", [P, HQ], F32R)]
        q_l = [top.q_l, sb("q_l1", [P, HQ], F32R)]
        rot_hh = [top.rot_hh, sb("rot_hh1", [P, HQ], F32R)]
        rot_l0 = [top.rot_l0, sb("rot_l01", [P, HQ], F32R)]
        prob = [sb(f"prob{n}", [P, HW]) for n in range(2)]
        prob_h = [sb(f"prob_h{n}", [P, HW], F32R) for n in range(2)]
        prob_l = [sb(f"prob_l{n}", [P, HW], F32R) for n in range(2)]
        total = [top.total, sb("total1", [P, HQ])]
        head_rows, sums = top.head_rows, top.sums
        prod = [sb(f"prod{n}", [P, 512]) for n in range(4)]
        rot_f = sb("rot_f", [P, 2, 512])
        rot_hl = sb("rot_hl", [P, 2, 2, 512], F32R)
        early_sums = sb("early_sums", [EARLY * UHEADS, CT])

        score_ps = ctx.enter_context(nc.psum_tensor("score_ps", [P, 2, HW], F32))
        out_ps = ctx.enter_context(nc.psum_tensor("out_ps", [P, 4, 512], F32))

        zeroed = sem("zeroed")
        keys_in, values_in = sem("keys_in"), sem("values_in")
        scored = sem("scored")
        exp_done = sem("exp_done")
        bounded = sem("bounded")
        clipped = sem("clipped")
        high_done = sem("high_done")
        begun = sem("begun")
        summed = sem("summed")
        split = sem("split")
        weighed = sem("weighed")
        out_read = sem("out_read")
        q_scored = sem("q_scored")
        q_high = sem("q_high")
        q_split = sem("q_split")
        r_scored = sem("r_scored")
        r_read = sem("r_read")
        r_step = sem("r_step")
        passed = sem("passed")
        scattered = sem("scattered")
        first_scattered = sem("first_scattered")
        summed_up = sem("summed_up")
        sums_read = sem("sums_read")
        weights_in = sem("weights_in")
        early_in, inverted, inverses_out = sem("early_in"), sem("inverted"), sem("inverses_out")
        heads_stored, sums_stored = sem("heads_stored"), sem("sums_stored")

        block = ctx.enter_context(nc.Block())

        def one_of(ap, n):
            return ap[bass.ds(n, 1), :, :].rearrange("a p n -> (a p) n")

        def gather(eng, n, par, signal):
            mine = turned[bass.ds(n, 1), :, :, :]
            for to, rows, part in ((rot_hh, 0, 0), (rot_hh, ROT, 0), (rot_l0, 0, 1)):
                eng.dma_start(raw(to[par][rows:rows + ROT, :]).rearrange("r (q n) -> r q n", q=4),
                               mine[:, part, :, :].rearrange("a (q f) (e n) -> (f e) (a q) n", q=4, e=2)).then_inc(signal, 16)

        @block.sync
        def _(sp):
            loads_before = sp.alloc_register("loads_before")

            def pair(t, unit, k, slot, kind, prev):
                loaded = 16 * t
                if not isinstance(t, int):
                    sp.reg_mov(loads_before, loaded)
                    loaded = sp.snap(loads_before, min_val=0, max_val=16 * PAIRS)
                since(sp, scored, 2 * (t - 1))
                since(sp, keys_in, loaded)
                sp.dma_start(raw(key_slot[slot][:, :]), one_of(keys, k)).then_inc(keys_in, 16)
                since(sp, weighed, 2 * (t - 1))
                since(sp, values_in, loaded)
                sp.dma_start(raw(value_slot[slot][:, :]), one_of(values, k)).then_inc(values_in, 16)

            sweep(sp, pair)
            sp.wait_ge(heads_stored, 16 * (UNITS - 1))
            sp.wait_ge(sums_stored, 16 * (UNITS - 1))
            sp.wait_ge(weights_in, 32)
            sp.wait_ge(inverses_out, 16)

        @block.gpsimd
        def _(pool):
            for n in range(2):
                nc.gpsimd.memset(raw(rot_l0[n][ROT:P, :]), 0.0).then_inc(zeroed, 1)

            def store(n):
                pool.wait_ge(out_read, 2 * n + 2)
                pool.dma_start(one_of(heads_out, n), head_rows[:, :]).then_inc(heads_stored, 16)
                pool.wait_ge(sums_read, n + 1)
                pool.dma_start(one_of(sums_out, n).rearrange("(q g) t -> q (g t)", g=2),
                               sums[0:P:32, :]).then_inc(sums_stored, 16)

            queries = pool.alloc_register("queries")
            pool.reg_mov(queries, 3)

            def during(n, par, first=False, has_next=True, has_second=True):
                if has_next:
                    since(pool, passed, 16 * n)
                    pool.wait_ge(q_scored, queries)
                    pool.reg_add(queries, queries, 2)
                    gather(pool, n + 1, 1 - par, scattered)
                if not first:
                    store(n - 1)
                if has_second:
                    pool.wait_ge(r_step, 4 * n + 4)
                    pool.dma_start(turned[bass.ds(n + 2, 1), :, :, :].rearrange("a w p n -> p (a w) n"),
                                   raw(rot_hl[:, :, :, :]).rearrange("p w e n -> p w (e n)")).then_inc(passed, 16)

            during(0, 0, first=True)
            during(1, 1)
            with pool.Fori(1, COUPLES - 1) as m:
                for par in range(2):
                    during(2 * m + par, par)
            during(UNITS - 2, 0, has_second=False)
            pool.wait_ge(sums_stored, 16 * EARLY)
            pool.dma_start(early_sums[:, :], sums_out[0:EARLY].rearrange("u h t -> (u h) t")).then_inc(early_in, 16)
            pool.wait_ge(scored, 2 * (PAIRS - 2 * COUPLES) + 1)
            pool.dma_start(top.wo[:, :, :], w_o).then_inc(weights_in, 16)
            during(UNITS - 1, 1, has_next=False, has_second=False)
            pool.wait_ge(summed_up, UNITS - 1)
            pool.dma_start(top.uv[:, :, :], w_uv.rearrange("p (h l) -> p h l", h=HEADS)).then_inc(weights_in, 16)
            pool.wait_ge(inverted, 1)
            pool.dma_start(inverses[0:EARLY].rearrange("u h t -> (u h) t"), early_sums[:, :]).then_inc(inverses_out, 16)

        @block.tensor
        def _(pe):
            def latent(couple, heads, half):
                tokens = bass.ds(couple * CT, CT)
                for h in range(HH):
                    head = heads * UHEADS + half * HH + h
                    w, out = slice(head * P, (head + 1) * P), score_ps[:, half, h * CT:(h + 1) * CT]
                    pe.matmul(out, keep.absorb_h[:, w], keep.cq_h[:, tokens], start=True, stop=False)
                    pe.matmul(out, keep.absorb_h[:, w], keep.cq_l[:, tokens], start=False, stop=False)
                    mm = pe.matmul(out, keep.absorb_l[:, w], keep.cq_h[:, tokens], start=False, stop=True)
                mm.then_inc(q_scored, 1)

            def rotary(couple, heads):
                tokens = bass.ds(couple * CT, CT)
                for n in range(4):
                    w = slice((4 * heads + n) * P, (4 * heads + n + 1) * P)
                    out = out_ps[:, 2 + n // 2, (n % 2) * CT:(n % 2 + 1) * CT]
                    pe.matmul(out, keep.qr_h[:, w], keep.cq_h[:, tokens], start=True, stop=False)
                    pe.matmul(out, keep.qr_h[:, w], keep.cq_l[:, tokens], start=False, stop=False)
                    mm = pe.matmul(out, keep.qr_l[:, w], keep.cq_h[:, tokens], start=False, stop=True)
                mm.then_inc(r_scored, 1)

            def sum_up(par, bank):
                for q in range(4):
                    mm = pe.matmul(bank[q * 32:(q + 1) * 32, :], keep.ones[:, :],
                                   total[par][:, q * 512:(q + 1) * 512], start=True, stop=True)
                mm.then_inc(summed_up, 1)

            def scores(half, par, slot, kind):
                key_high, key_low, key_rot = (key_slot[slot][:, n * P:(n + 1) * P] for n in range(3))

                def columns(buffer, c):
                    if kind == LATE:
                        heads = buffer[:, :].rearrange("p (h t) -> p h t", t=CT)
                        return heads[:, half * HH:(half + 1) * HH, P:CT]
                    return buffer[:, half * HW + c * 512:half * HW + (c + 1) * 512]

                for c in range(1 if kind == LATE else 2):
                    out = score_ps[:, half, c * 512:(c + 1) * 512]
                    pe.matmul(out, key_high, columns(q_h[par], c), start=True, stop=False)
                    pe.matmul(out, key_high, columns(q_l[par], c), start=False, stop=False)
                    pe.matmul(out, key_low, columns(q_h[par], c), start=False, stop=False)
                    pe.matmul(out, key_rot, columns(rot_hh[par], c), start=False, stop=False)
                    mm = pe.matmul(out, key_rot, columns(rot_l0[par], c), start=False, stop=True)
                mm.then_inc(scored, 1)

            def weigh(t, half, slot, kind, last, turned_before=None):
                pe.wait_ge(split, 2 * t + half + 1)
                high, low = value_slot[slot][:, 0:P], value_slot[slot][:, P:SV]
                first = kind == CORNER
                for c in range(2):
                    if turned_before is not None:
                        pe.wait_ge(r_read, 4 * turned_before + 2 * c + 2)
                    out = out_ps[:, 2 * half + c, :]
                    cols = slice(c * 512, (c + 1) * 512)
                    p_h, p_l = prob_h[half][:, cols], prob_l[half][:, cols]
                    if kind == LATE:
                        out = out.rearrange("p (h t) -> p h t", t=CT)[:, :, P:CT]
                        cols = slice(c * 256, (c + 1) * 256)
                        p_h, p_l = (p[half][:, cols].rearrange("p (h t) -> p h t", t=P) for p in (prob_h, prob_l))
                    pe.matmul(out, high, p_h, start=first, stop=False)
                    pe.matmul(out, high, p_l, start=False, stop=False)
                    mm = pe.matmul(out, low, p_h, start=False, stop=last)
                mm.then_inc(weighed, 1)

            def pair(t, unit, k, slot, kind, prev):
                n, par = unit.n, unit.par
                pe.wait_ge(keys_in, 16 * (t + 1))
                if kind == CORNER:
                    pe.wait_ge(q_split, 2 * n + 2)
                    pe.wait_ge(first_scattered, 16 * SPREADS)
                    since(pe, scattered, 16 * SPREADS * n)
                if kind == LATE and unit.has_next:
                    pe.wait_ge(q_split, 2 * n + 3)
                since(pe, exp_done, 2 * t - 1)
                scores(0, par, slot, kind)
                if prev in (LATE, FULL):
                    pe.wait_ge(values_in, 16 * t)
                    weigh(t - 1, 0, 1 - slot, prev, kind == CORNER)
                if kind == LATE and unit.has_next:
                    pe.wait_ge(q_split, 2 * n + 4)
                since(pe, exp_done, 2 * t)
                scores(1, par, slot, kind)
                if prev is not None:
                    if prev == CORNER:
                        since(pe, out_read, 2 * n)
                    weigh(t - 1, 1, 1 - slot, prev, kind == CORNER, n if prev == CORNER and unit.has_second else None)
                if kind == CORNER:
                    if prev is not None:
                        pe.wait_ge(summed, unit.added)
                        pe.wait_ge(out_read, 2 * n - 1)
                        sum_up(1 - par, out_ps[:, 0, :])
                    if unit.has_next:
                        for half in range(2):
                            pe.wait_ge(exp_done, 2 * t + 1 + half)
                            latent(unit.next_couple, 1 - par, half)
                    pe.wait_ge(values_in, 16 * (t + 1))
                    since(pe, sums_read, n)
                    weigh(t, 0, slot, CORNER, False)
                    if unit.has_second:
                        since(pe, out_read, 2 * n)
                        rotary(unit.couple + 1, par)

            latent(0, 0, 0)
            latent(0, 0, 1)
            pe.wait_ge(zeroed, 2)
            sweep(pe, pair)
            pe.wait_ge(values_in, 16 * PAIRS)
            for half in range(2):
                weigh(PAIRS - 1, half, 1, FULL, True)
            pe.wait_ge(exp_done, 2 * PAIRS)
            pe.wait_ge(summed, 2 * (PAIRS - UNITS))
            sum_up(1, score_ps[:, 0, 0:512])

        @block.scalar
        def _(act):
            def latent_high(unit, par, half):
                act.wait_ge(q_scored, 2 * unit + half + 1)
                nc.scalar.copy(q_h[par][:, half * HW:(half + 1) * HW], score_ps[:, half, :]).then_inc(q_high, 1)

            def read_out(unit, half):
                if half == 0:
                    since(act, heads_stored, 16 * unit)
                nc.scalar.copy(head_rows[:, half * HW:(half + 1) * HW],
                               out_ps[:, 2 * half:2 * half + 2, :]).then_inc(out_read, 1)

            def read_sums(n, bank):
                act.wait_ge(summed_up, n + 1)
                since(act, sums_stored, 16 * n)
                nc.scalar.copy(sums[:, :], bank[:, 0:512]).then_inc(sums_read, 1)

            def pair(t, unit, k, slot, kind, prev):
                n, par = unit.n, unit.par
                width = HW // 2 if kind == LATE else HW

                def exponential(half):
                    act.wait_ge(scored, 2 * t + half + 1)
                    since(act, split, 2 * t + half - 1)
                    if kind == LATE:
                        act.wait_ge(begun, 2 * n + half + 1)
                    if kind == FULL:
                        act.wait_ge(summed, unit.added + 2 * k + half + 1)
                    if kind == CORNER and prev is not None:
                        act.wait_ge(summed, unit.added + half - 1)
                    nc.scalar.activation(prob[half][:, 0:width], score_ps[:, half, 0:width], ACT.Exp,
                                         scale=QK_SCALE).then_inc(exp_done, 1)

                def high(half):
                    act.wait_ge(clipped, 2 * t + half + 1)
                    since(act, weighed, 2 * t + half - 1)
                    nc.scalar.copy(prob_h[half][:, 0:width], prob[half][:, 0:width]).then_inc(high_done, 1)

                def begin(half):
                    since(act, summed_up, n - 1)
                    act.wait_ge(clipped, 2 * t + half + 1)
                    nc.scalar.copy(total[par][:, half * HW:(half + 1) * HW], prob[half][:, :]).then_inc(begun, 1)

                if kind != CORNER:
                    for half in range(2):
                        exponential(half)
                        high(half)
                    return
                exponential(0)
                if prev is not None:
                    act.wait_ge(weighed, 2 * t - 1)
                    read_out(n - 1, 0)
                high(0)
                exponential(1)
                begin(0)
                high(1)
                if prev is not None:
                    read_sums(n - 1, out_ps[:, 0, :])
                    act.wait_ge(weighed, 2 * t)
                    read_out(n - 1, 1)
                if unit.has_next:
                    latent_high(n + 1, 1 - par, 0)
                    latent_high(n + 1, 1 - par, 1)
                begin(1)

            gather(act, 0, 0, first_scattered)
            for half in range(2):
                latent_high(0, 0, half)
            sweep(act, pair)
            for half in range(2):
                act.wait_ge(weighed, 2 * PAIRS - 1 + half)
                read_out(UNITS - 1, half)
            read_sums(UNITS - 1, score_ps[:, 0, :])

        @block.vector
        def _(dve):
            def latent_low(unit, par, half):
                dve.wait_ge(q_high, 2 * unit + half + 1)
                cols = slice(half * HW, (half + 1) * HW)
                nc.vector.tensor_tensor(q_l[par][:, cols], score_ps[:, half, :], q_h[par][:, cols],
                                        ALU.subtract).then_inc(q_split, 1)

            def turn(n, couple):
                dve.wait_ge(r_scored, n + 1)
                tokens = bass.ds(couple * CT, CT)
                cos, sin = (w[:, tokens].unsqueeze(1).to_broadcast([P, 2, CT]) for w in (keep.cos, keep.sin))
                even, odd = (out_ps[:, 2 + eo, :].rearrange("p (g t) -> p g t", g=2) for eo in range(2))
                for out, rows, angle in zip(prod, (even, even, odd, odd), (cos, sin, sin, cos)):
                    nc.vector.tensor_tensor(out[:, :].rearrange("p (g t) -> p g t", g=2), rows, angle,
                                            ALU.mult).then_inc(r_read, 1)

            def add_turned(n):
                dve.wait_ge(r_read, 4 * n + 4)
                nc.vector.tensor_tensor(rot_f[:, 0, :], prod[0][:, :], prod[2][:, :], ALU.subtract).then_inc(r_step, 1)
                nc.vector.tensor_tensor(rot_f[:, 1, :], prod[1][:, :], prod[3][:, :], ALU.add).then_inc(r_step, 1)

            def split_turned(n):
                since(dve, passed, 16 * n)
                dve.wait_ge(r_step, 4 * n + 2)
                nc.vector.tensor_copy(rot_hl[:, 0, :, :], rot_f[:, :, :]).then_inc(r_step, 1)
                dve.wait_ge(r_step, 4 * n + 3)
                nc.vector.tensor_tensor(rot_hl[:, 1, :, :], rot_f[:, :, :], rot_hl[:, 0, :, :],
                                        ALU.subtract).then_inc(r_step, 1)

            def by_head(half, kind):
                tokens = P if kind == LATE else CT
                return prob[half][:, 0:HH * tokens].rearrange("p (h t) -> p h t", t=tokens)

            def clip(t, n, half, kind):
                p = prob[half][:, 0:HH * (P if kind == LATE else CT)]
                dve.wait_ge(exp_done, 2 * t + half + 1)
                if kind == FULL:
                    nc.vector.tensor_scalar(p, p, P_MIN, P_MAX, ALU.max, ALU.min).then_inc(clipped, 1)
                    return
                nc.vector.tensor_scalar(p, p, P_MIN, P_MAX, ALU.max, ALU.min).then_inc(bounded, 1)
                dve.wait_ge(bounded, 4 * n + (2 if kind == LATE else 0) + half + 1)
                masked = by_head(half, kind)[:, :, 0:P]
                nc.vector.tensor_tensor(masked, masked, keep.causal[:, :].unsqueeze(1).to_broadcast([P, HH, P]),
                                        ALU.mult).then_inc(clipped, 1)

            def add(t, par, half, kind):
                sums = total[par][:, half * HW:(half + 1) * HW].rearrange("p (h t) -> p h t", t=CT)
                sums = sums[:, :, P if kind == LATE else 0:CT]
                dve.wait_ge(clipped, 2 * t + half + 1)
                nc.vector.tensor_tensor(sums, sums, by_head(half, kind), ALU.add).then_inc(summed, 1)

            def low(t, half, kind):
                p, p_h, p_l = (b[half][:, 0:HH * (P if kind == LATE else CT)] for b in (prob, prob_h, prob_l))
                dve.wait_ge(high_done, 2 * t + half + 1)
                nc.vector.tensor_tensor(p_l, p, p_h, ALU.subtract).then_inc(split, 1)

            def pair(t, unit, k, slot, kind, prev):
                n, par = unit.n, unit.par
                clip(t, n, 0, kind)
                if prev == LATE:
                    dve.wait_ge(begun, 2 * n if kind == CORNER else 2 * n + 2)
                if prev == FULL:
                    dve.wait_ge(summed, unit.added - 2 if kind == CORNER else unit.added + 2 * k)
                if prev in (LATE, FULL):
                    add(t - 1, 1 - par if kind == CORNER else par, 1, prev)
                low(t, 0, kind)
                clip(t, n, 1, kind)
                if kind == LATE:
                    dve.wait_ge(begun, 2 * n + 1)
                if kind == FULL:
                    dve.wait_ge(summed, unit.added + 2 * k + 1)
                if kind != CORNER:
                    add(t, par, 0, kind)
                low(t, 1, kind)
                if kind == CORNER:
                    if unit.has_next:
                        latent_low(n + 1, 1 - par, 0)
                        latent_low(n + 1, 1 - par, 1)
                    if unit.has_second:
                        turn(n, unit.couple + 1)
                if unit.has_second:
                    if kind == LATE and isinstance(unit.couple, int) and unit.couple == 0:
                        add_turned(n)
                        split_turned(n)
                    if kind == FULL and prev == LATE:
                        add_turned(n)
                    if kind == FULL and isinstance(k, int) and k == 1:
                        split_turned(n)
                if not unit.has_next and kind == FULL and isinstance(k, int) and k == 1:
                    dve.wait_ge(early_in, 16)
                    nc.vector.reciprocal(early_sums[:, :], early_sums[:, :]).then_inc(inverted, 1)

            latent_low(0, 0, 0)
            latent_low(0, 0, 1)
            sweep(dve, pair)
            dve.wait_ge(summed, 2 * (PAIRS - UNITS) - 2)
            add(PAIRS - 1, 1, 1, FULL)


def combine(nc, top, x, heads_in, sums_in, inverses, linear, out):
    ctx = ExitStack()
    with ctx:
        def sb(name, shape, dt=F32):
            return ctx.enter_context(nc.sbuf_tensor(name, shape, dt))

        def sem(name):
            return ctx.enter_context(nc.semaphore(name))

        SCALED, SPLIT = (4, 7), (10, 13)
        late_sums = sb("late_sums", [(UNITS - EARLY) * UHEADS, CT])
        merged_h = sb("merged_h", [P, HEADS, DIM], F32R)
        merged_l = sb("merged_l", [P, HEADS, DIM], F32R)
        rows = [sb(f"rows{n}", [P, HEADS, P]) for n in range(2)]
        scale = [sb(f"scale{n}", [P, HEADS, P]) for n in range(2)]
        rows_h = [sb(f"rows_h{n}", [P, HEADS, P], F32R) for n in range(2)]
        rows_l = [sb(f"rows_l{n}", [P, HEADS, P], F32R) for n in range(2)]
        x_in = [sb(f"x_in{n}", [P, DIM]) for n in range(2)]
        lin_in = [sb(f"lin_in{n}", [P, DIM]) for n in range(2)]
        gate = [sb(f"gate{n}", [P, DIM]) for n in range(2)]
        result = [sb(f"result{n}", [P, DIM]) for n in range(2)]
        merge_ps = ctx.enter_context(nc.psum_tensor("merge_ps", [P, 4, DIM], F32))
        sum_ps = ctx.enter_context(nc.psum_tensor("sum_ps", [P, 2, DIM], F32))

        last_stored = sem("last_stored")
        sums_loaded = sem("sums_loaded")
        inverted = sem("inverted")
        inverses_stored = sem("inverses_stored")
        merged = sem("merged")
        merge_high = sem("merge_high")
        merge_split = sem("merge_split")
        rows_in = [sem(f"rows_in{n}") for n in range(2)]
        scale_in = [sem(f"scale_in{n}") for n in range(2)]
        scale_spread = [sem(f"scale_spread{n}") for n in range(2)]
        gate_in = [sem(f"gate_in{n}") for n in range(2)]
        scaled = sem("scaled")
        rows_high = sem("rows_high")
        rows_split = sem("rows_split")
        sigmoid = sem("sigmoid")
        gated = sem("gated")
        projected = [sem(f"projected{n}") for n in range(2)]
        times = [sem(f"times{n}") for n in range(2)]
        finished = sem("finished")
        stored = [sem(f"stored{n}") for n in range(2)]

        block = ctx.enter_context(nc.Block())

        def tile_of(ap, t):
            return ap[bass.ds(t, 1), :, :].rearrange("a p n -> (a p) n")

        x_tiles = x.rearrange("(t p) n -> t p n", p=P)
        out_tiles = out.rearrange("(t p) n -> t p n", p=P)

        @block.sync
        def _(sp):

            def load_rows(t, par):
                since(sp, rows_split, 2 * (t - 1))
                tokens = slice(par * P, (par + 1) * P)
                for half in range(2):
                    unit, heads = bass.ds(t - par + half, 1), slice(half * UHEADS, (half + 1) * UHEADS)
                    sp.dma_start(rows[par][:, heads, :], heads_in[unit, :, :].rearrange(
                        "a p (h t) -> (a p) h t", t=CT)[:, :, tokens]).then_inc(rows_in[par], 16)

            def load_scale(t, par):
                sp.dma_start(scale[par][0:1, :, :], inverses[bass.ds(t - par, 2), :, par * P:(par + 1) * P].rearrange(
                    "u h t -> (u h) t").unsqueeze(0)).then_inc(scale_in[par], 16)

            def load_rest(t, par):
                since(sp, finished, t - 1)
                sp.dma_start(x_in[par][:, :], tile_of(x_tiles, t)).then_inc(gate_in[par], 16)
                sp.dma_start(lin_in[par][:, :], tile_of(linear, t)).then_inc(gate_in[par], 16)

            def store(t, par):
                sp.wait_ge(finished, t + 1)
                sp.dma_start(tile_of(out_tiles, t), result[par][:, :]).then_inc(stored[par], 16)

            for par in range(2):
                load_rows(par, par)
                load_scale(par, par)
                load_rest(par, par)
            sp.dma_start(tile_of(heads_in, UNITS - 1), top.head_rows[:, :]).then_inc(last_stored, 16)
            sp.dma_start(sums_in[UNITS - 1].rearrange("(q g) t -> q (g t)", g=2), top.sums[0:P:32, :]).then_inc(last_stored, 16)
            sp.wait_ge(last_stored, 32)
            sp.dma_start(late_sums[:, :], sums_in[EARLY:UNITS].rearrange("u h t -> (u h) t")).then_inc(sums_loaded, 16)
            sp.wait_ge(inverted, 1)
            sp.dma_start(inverses[EARLY:UNITS].rearrange("u h t -> (u h) t"), late_sums[:, :]).then_inc(inverses_stored, 16)
            sp.wait_ge(inverses_stored, 16)
            with sp.Fori(0, COUPLES - 1) as n:
                for par in range(2):
                    load_rows(2 * n + par + 2, par)
                    load_scale(2 * n + par + 2, par)
                    load_rest(2 * n + par + 2, par)
                    store(2 * n + par, par)
            for par in range(2):
                store(TILES - 2 + par, par)
            for par in range(2):
                sp.wait_ge(stored[par], 16 * COUPLES)

        @block.gpsimd
        def _(pool):
            loaded = [pool.alloc_register(f"loaded{n}") for n in range(2)]
            for register in loaded:
                pool.reg_mov(register, 16)
            with pool.Fori(0, COUPLES):
                for par in range(2):
                    pool.wait_ge(scale_in[par], loaded[par])
                    pool.reg_add(loaded[par], loaded[par], 16)
                    nc.gpsimd.partition_broadcast(scale[par][:, :, :], scale[par][0:1, :, :], channels=P).then_inc(scale_spread[par], 1)

        @block.tensor
        def _(pe):
            for h in range(HEADS):
                since(pe, merge_split, h - 3)
                pe.matmul(merge_ps[:, h % 4, :], top.uv[:, h, :], top.wo[:, h, :], start=True, stop=True).then_inc(merged, 1)

            def couple(n, first=False):
                for par in range(2):
                    t = 2 * n + par
                    since(pe, times[par], n)
                    for half in range(2):
                        pe.wait_ge(rows_split, 2 * t + half + 1)
                        for h in range(half * UHEADS, (half + 1) * UHEADS):
                            if first and par == 0:
                                pe.wait_ge(merge_split, h + 1)
                            pe.matmul(sum_ps[:, par, :], rows_h[par][:, h, :], merged_h[:, h, :], start=(h == 0), stop=False)
                            pe.matmul(sum_ps[:, par, :], rows_h[par][:, h, :], merged_l[:, h, :], start=False, stop=False)
                            mm = pe.matmul(sum_ps[:, par, :], rows_l[par][:, h, :], merged_h[:, h, :],
                                           start=False, stop=(h == HEADS - 1))
                    mm.then_inc(projected[par], 1)

            couple(0, first=True)
            with pe.Fori(1, COUPLES) as n:
                couple(n)

        @block.scalar
        def _(act):
            def high_half(t, par, half):
                heads = slice(half * UHEADS, (half + 1) * UHEADS)
                act.wait_ge(scaled, 2 * t + half + 1)
                nc.scalar.copy(rows_h[par][:, heads, :], rows[par][:, heads, :]).then_inc(rows_high, 1)

            def high_rows(t, par, n):
                since(act, projected[par], n)
                for half in range(2):
                    high_half(t, par, half)

            def gates(par, n):
                act.wait_ge(gate_in[par], 32 * (n + 1))
                since(act, times[par], n)
                nc.scalar.activation(gate[par][:, :], lin_in[par][:, :], ACT.Sigmoid).then_inc(sigmoid, 1)

            for h in range(HEADS):
                if h - 2 in SCALED:
                    high_half(0, 0, SCALED.index(h - 2))
                act.wait_ge(merged, h + 1)
                nc.scalar.copy(merged_h[:, h, :], merge_ps[:, h % 4, :]).then_inc(merge_high, 1)
            gates(0, 0)
            high_rows(1, 1, 0)
            gates(1, 0)
            with act.Fori(1, COUPLES) as n:
                for par in range(2):
                    high_rows(2 * n + par, par, n)
                    gates(par, n)

        @block.vector
        def _(dve):
            def scale_half(par, n, half):
                heads = slice(half * UHEADS, (half + 1) * UHEADS)
                dve.wait_ge(rows_in[par], 32 * (n + 1))
                dve.wait_ge(scale_spread[par], n + 1)
                nc.vector.tensor_tensor(rows[par][:, heads, :], rows[par][:, heads, :], scale[par][:, heads, :],
                                        ALU.mult).then_inc(scaled, 1)

            def split_half(t, par, half):
                heads = slice(half * UHEADS, (half + 1) * UHEADS)
                dve.wait_ge(rows_high, 2 * t + half + 1)
                nc.vector.tensor_tensor(rows_l[par][:, heads, :], rows[par][:, heads, :], rows_h[par][:, heads, :],
                                        ALU.subtract).then_inc(rows_split, 1)

            def scale_rows(t, par, n):
                for half in range(2):
                    scale_half(par, n, half)
                for half in range(2):
                    split_half(t, par, half)

            def gates(t, par):
                dve.wait_ge(sigmoid, t + 1)
                nc.vector.tensor_tensor(gate[par][:, :], gate[par][:, :], lin_in[par][:, :], ALU.mult).then_inc(gated, 1)

            def finish(t, par, n):
                dve.wait_ge(projected[par], n + 1)
                dve.wait_ge(gated, t + 1)
                since(dve, stored[par], 16 * n)
                nc.vector.tensor_tensor(result[par][:, :], sum_ps[:, par, :], gate[par][:, :], ALU.mult).then_inc(times[par], 1)
                dve.wait_ge(times[par], n + 1)
                nc.vector.tensor_tensor(result[par][:, :], result[par][:, :], x_in[par][:, :], ALU.add).then_inc(finished, 1)

            def couple(n):
                scale_rows(2 * n + 1, 1, n)
                gates(2 * n + 1, 1)
                finish(2 * n, 0, n)
                scale_rows(2 * n + 2, 0, n + 1)
                gates(2 * n + 2, 0)
                finish(2 * n + 1, 1, n)

            for h in range(HEADS):
                if h in SCALED:
                    scale_half(0, 0, SCALED.index(h))
                if h in SPLIT:
                    split_half(0, 0, SPLIT.index(h))
                dve.wait_ge(merge_high, h + 1)
                nc.vector.tensor_tensor(merged_l[:, h, :], merge_ps[:, h % 4, :], merged_h[:, h, :],
                                        ALU.subtract).then_inc(merge_split, 1)
            gates(0, 0)
            dve.wait_ge(sums_loaded, 16)
            nc.vector.reciprocal(late_sums[:, :], late_sums[:, :]).then_inc(inverted, 1)
            couple(0)
            with dve.Fori(1, COUPLES - 1) as n:
                couple(n)
            scale_rows(TILES - 1, 1, COUPLES - 1)
            gates(TILES - 1, 1)
            finish(TILES - 2, 0, COUPLES - 1)
            finish(TILES - 1, 1, COUPLES - 1)


def program(nc, x, w_all, w_uq, w_uk, w_qr, lora_b, w_uv, w_o, cos, sin, out):
    keys = nc.dram_tensor("keys", [TILES, P, SK], F32, kind="Internal").ap()
    values = nc.dram_tensor("values", [TILES, P, SV], F32, kind="Internal").ap()
    linear = nc.dram_tensor("linear", [TILES, P, DIM], F32, kind="Internal").ap()
    heads_rows = nc.dram_tensor("heads_rows", [UNITS, P, HQ], F32, kind="Internal").ap()
    sums = nc.dram_tensor("sums_rows", [UNITS, UHEADS, CT], F32, kind="Internal").ap()
    inverses = nc.dram_tensor("inverses", [UNITS, UHEADS, CT], F32, kind="Internal").ap()
    turned = nc.dram_tensor("turned", [UNITS, 2, P, 1024], F32, kind="Internal").ap()
    with ExitStack() as ctx:
        with ExitStack() as first_phases:
            keep = Persistent(nc, first_phases)
            prepare(nc, keep, x, w_all, w_uq, w_uk, w_qr, lora_b, cos, sin, keys, values, linear, turned)
            top = Top(nc, ctx)
            attend(nc, keep, top, keys, values, turned, w_uv, w_o, heads_rows, sums, inverses)
        combine(nc, top, x, heads_rows, sums, inverses, linear, out)


def layout(L0_attn_x, L0_attn_W_DQ, L0_attn_W_UQ, L0_attn_W_QR, L0_attn_W_DKV, L0_attn_W_UK, L0_attn_W_UV,
           L0_attn_W_KR, L0_attn_W_O, L0_ffn_weight, L0_ffn_lora_A, L0_ffn_lora_B, L0_ffn_router_w):
    import numpy as np
    x = L0_attn_x.reshape(SEQ, DIM)
    kr_even, kr_odd = L0_attn_W_KR[0::2], L0_attn_W_KR[1::2]
    w_all = np.concatenate([L0_ffn_weight, L0_ffn_lora_A.reshape(ER, DIM), L0_ffn_router_w, L0_attn_W_DKV,
                            L0_attn_W_DQ, kr_even, kr_odd, kr_odd, kr_even], axis=0).T

    def by_head(w):
        return w.reshape(HEADS, P, LAT).transpose(1, 0, 2).reshape(P, HEADS * LAT)

    w_qr = L0_attn_W_QR.reshape(2, 4, 2, HALF, 2, LAT).transpose(5, 0, 4, 2, 1, 3).reshape(LAT, 2 * GT)
    inv_freq = np.float32(10000.0) ** (-np.arange(0, ROT, 2, dtype=np.float32) / np.float32(ROT))
    angle = np.tile(inv_freq[:, None] * np.arange(SEQ, dtype=np.float32)[None, :], (P // HALF, 1))
    arrays = {
        "x": x, "w_all": w_all, "w_uq": by_head(L0_attn_W_UQ), "w_uk": by_head(L0_attn_W_UK), "w_qr": w_qr,
        "lora_b": L0_ffn_lora_B.transpose(0, 2, 1).reshape(ER, DIM),
        "w_uv": by_head(L0_attn_W_UV), "w_o": L0_attn_W_O.T.reshape(HEADS, P, DIM).transpose(1, 0, 2),
        "cos": np.cos(angle), "sin": np.sin(angle),
    }
    return {name: np.ascontiguousarray(a) for name, a in arrays.items()}


def kernel(**inputs):
    import numpy as np
    import concourse.bacc as bacc
    from concourse.bass_utils import run_bass_kernel_spmd

    nc = bacc.Bacc("TRN2", target_bir_lowering=False, num_devices=1)
    arrays = {f"in_{n}": a for n, a in layout(**{n: np.asarray(a) for n, a in inputs.items()}).items()}
    args = [nc.dram_tensor(n, a.shape, mybir.dt.from_np(a.dtype), kind="ExternalInput").ap() for n, a in arrays.items()]
    args.append(nc.dram_tensor("out", (SEQ, DIM), F32, kind="ExternalOutput").ap())
    program(nc, *args)
    result = run_bass_kernel_spmd(nc, [arrays], core_ids=[0])
    return result.results[0]["out"].reshape(1, SEQ, DIM)
```
